# Optimizing a Trainium2 kernel written in Bass

```python
import numpy as np
import jax
import jax.numpy as jnp

def _softmax(x, axis=-1):
    return jax.nn.softmax(x, axis=axis)

def _gelu(x):
    return jax.nn.gelu(x, approximate=True)

def _silu(x):
    return jax.nn.silu(x)

def _sigmoid(x):
    return jax.nn.sigmoid(x)

def _layernorm(x, axis=-1, eps=1e-05):
    m = jnp.mean(x, axis=axis, keepdims=True)
    v = jnp.var(x, axis=axis, keepdims=True)
    return (x - m) / jnp.sqrt(v + eps)

def _scatter_add(tgt, idx, src, axis=0):
    return tgt.at[idx].add(src)

def _segment_sum(src, seg, n):
    return jax.ops.segment_sum(src, seg, n)
kernel_name = 'mk_lm_tower_d1_tok_ids768_r4_c9e8ac'

def setup_inputs(seed: int=0):
    np.random.seed(seed)
    _w = jnp.asarray

    def _rec_inputs():
        import jax
        import jax.numpy as jnp
        _rk = jax.random.key(seed)
        x = jax.random.randint(jax.random.fold_in(_rk, 1), (8, 1024), 0, 12564, jnp.int32)
        return x
    x = _rec_inputs()

    def _L0_tok_setup():
        import jax, jax.numpy as jnp
        import numpy as np
        VOCAB = 50257
        D_MODEL = 192
        BATCH = 4
        SEQ = 1024
        key = jax.random.key(seed)
        k_ids, k_tab = jax.random.split(key)
        token_ids = jax.random.randint(k_ids, (BATCH, SEQ), 0, VOCAB, dtype=jnp.int64)
        embedding_lookup = jax.random.truncated_normal(k_tab, -3.0, 3.0, (VOCAB, D_MODEL), dtype=jnp.float32)
        return {'token_ids': token_ids, 'embedding_lookup': embedding_lookup}
    _L0_tok_all = _L0_tok_setup()
    _L0_tok_in = {k: v for k, v in _L0_tok_all.items() if k in ('embedding_lookup',)}
    del _L0_tok_all

    def _L0_attn_setup():
        import jax, jax.numpy as jnp
        import numpy as np
        NUM_HEADS = 12
        WINDOW = 64
        LN_EPS = 1e-05

        def _ln(x, g, b):
            m = x.mean(-1, keepdims=True)
            v = x.var(-1, keepdims=True)
            return (x - m) / jnp.sqrt(v + LN_EPS) * g + b
        key = jax.random.key(seed)
        ks = jax.random.split(key, 10)
        B, L, D = (1, 512, 192)
        s = 0.02

        def w(k, shape):
            return jax.random.normal(k, shape, jnp.float32) * s
        return {'x': jax.random.normal(ks[0], (B, L, D), jnp.float32), 'ln1_g': jnp.ones((D,), jnp.float32), 'ln1_b': jnp.zeros((D,), jnp.float32), 'attn_qkv_w': w(ks[1], (D, 3 * D)), 'attn_qkv_b': jnp.zeros((3 * D,), jnp.float32), 'attn_proj_w': w(ks[2], (D, D)), 'attn_proj_b': jnp.zeros((D,), jnp.float32), 'ssm_qkv_w': w(ks[3], (D, 3 * D)), 'ssm_qkv_b': jnp.zeros((3 * D,), jnp.float32), 'ssm_out_w': w(ks[4], (D, D)), 'ssm_out_b': jnp.zeros((D,), jnp.float32), 'ssm_ln_g': jnp.ones((D,), jnp.float32), 'ssm_ln_b': jnp.zeros((D,), jnp.float32), 'out_w': w(ks[5], (D, D)), 'out_b': jnp.zeros((D,), jnp.float32), 'mlp_w1': w(ks[6], (D, 4 * D)), 'mlp_b1': jnp.zeros((4 * D,), jnp.float32), 'mlp_w2': w(ks[7], (4 * D, D)), 'mlp_b2': jnp.zeros((D,), jnp.float32), 'lnm_g': jnp.ones((D,), jnp.float32), 'lnm_b': jnp.zeros((D,), jnp.float32)}
    _L0_attn_all = _L0_attn_setup()
    _L0_attn_in = {k: v for k, v in _L0_attn_all.items() if k in ('ln1_g', 'ln1_b', 'attn_qkv_w', 'attn_qkv_b', 'attn_proj_w', 'attn_proj_b', 'ssm_qkv_w', 'ssm_qkv_b', 'ssm_out_w', 'ssm_out_b', 'ssm_ln_g', 'ssm_ln_b', 'out_w', 'out_b', 'mlp_w1', 'mlp_b1', 'mlp_w2', 'mlp_b2', 'lnm_g', 'lnm_b')}
    del _L0_attn_all

    def _L0_ffn_setup():
        import jax, jax.numpy as jnp
        import numpy as np
        import math
        B, S, D = (4, 1024, 192)
        E = 8
        TOP_K = 2
        H = 512
        CAP_F = 1.25
        EPS = 1e-06
        ALPHA = 1.0
        key = jax.random.key(seed)
        k0, k1, k2, k3 = jax.random.split(key, 4)
        x = jax.random.normal(k0, (B, S, D), jnp.float32)
        gate_w = jax.random.normal(k1, (E, D), jnp.float32) * 0.02
        w13 = jax.random.normal(k2, (E, 2 * H, D), jnp.float32) * 0.02
        w2 = jax.random.normal(k3, (E, D, H), jnp.float32) * 0.02
        norm_w = jnp.ones((E, D), jnp.float32)
        return {'x': x, 'gate_w': gate_w, 'w13': w13, 'w2': w2, 'norm_w': norm_w}
    _L0_ffn_all = _L0_ffn_setup()
    _L0_ffn_in = {k: v for k, v in _L0_ffn_all.items() if k in ('gate_w', 'w13', 'w2', 'norm_w')}
    del _L0_ffn_all
    return {'x': x, 'L0_tok_embedding_lookup': _L0_tok_in['embedding_lookup'], 'L0_attn_ln1_g': _L0_attn_in['ln1_g'], 'L0_attn_ln1_b': _L0_attn_in['ln1_b'], 'L0_attn_attn_qkv_w': _L0_attn_in['attn_qkv_w'], 'L0_attn_attn_qkv_b': _L0_attn_in['attn_qkv_b'], 'L0_attn_attn_proj_w': _L0_attn_in['attn_proj_w'], 'L0_attn_attn_proj_b': _L0_attn_in['attn_proj_b'], 'L0_attn_ssm_qkv_w': _L0_attn_in['ssm_qkv_w'], 'L0_attn_ssm_qkv_b': _L0_attn_in['ssm_qkv_b'], 'L0_attn_ssm_out_w': _L0_attn_in['ssm_out_w'], 'L0_attn_ssm_out_b': _L0_attn_in['ssm_out_b'], 'L0_attn_ssm_ln_g': _L0_attn_in['ssm_ln_g'], 'L0_attn_ssm_ln_b': _L0_attn_in['ssm_ln_b'], 'L0_attn_out_w': _L0_attn_in['out_w'], 'L0_attn_out_b': _L0_attn_in['out_b'], 'L0_attn_mlp_w1': _L0_attn_in['mlp_w1'], 'L0_attn_mlp_b1': _L0_attn_in['mlp_b1'], 'L0_attn_mlp_w2': _L0_attn_in['mlp_w2'], 'L0_attn_mlp_b2': _L0_attn_in['mlp_b2'], 'L0_attn_lnm_g': _L0_attn_in['lnm_g'], 'L0_attn_lnm_b': _L0_attn_in['lnm_b'], 'L0_ffn_gate_w': _L0_ffn_in['gate_w'], 'L0_ffn_w13': _L0_ffn_in['w13'], 'L0_ffn_w2': _L0_ffn_in['w2'], 'L0_ffn_norm_w': _L0_ffn_in['norm_w']}

def reference(x, L0_tok_embedding_lookup, L0_attn_ln1_g, L0_attn_ln1_b, L0_attn_attn_qkv_w, L0_attn_attn_qkv_b, L0_attn_attn_proj_w, L0_attn_attn_proj_b, L0_attn_ssm_qkv_w, L0_attn_ssm_qkv_b, L0_attn_ssm_out_w, L0_attn_ssm_out_b, L0_attn_ssm_ln_g, L0_attn_ssm_ln_b, L0_attn_out_w, L0_attn_out_b, L0_attn_mlp_w1, L0_attn_mlp_b1, L0_attn_mlp_w2, L0_attn_mlp_b2, L0_attn_lnm_g, L0_attn_lnm_b, L0_ffn_gate_w, L0_ffn_w13, L0_ffn_w2, L0_ffn_norm_w):
    import jax
    import jax.numpy as jnp

    def _L0_tok_ref(token_ids, embedding_lookup):
        import jax, jax.numpy as jnp
        import numpy as np
        VOCAB = 50257
        D_MODEL = 192
        BATCH = 4
        SEQ = 1024
        return jnp.take(embedding_lookup, token_ids, axis=0)

    def _L0_attn_ref(x, ln1_g, ln1_b, attn_qkv_w, attn_qkv_b, attn_proj_w, attn_proj_b, ssm_qkv_w, ssm_qkv_b, ssm_out_w, ssm_out_b, ssm_ln_g, ssm_ln_b, out_w, out_b, mlp_w1, mlp_b1, mlp_w2, mlp_b2, lnm_g, lnm_b):
        import jax, jax.numpy as jnp
        import numpy as np
        NUM_HEADS = 12
        WINDOW = 64
        LN_EPS = 1e-05

        def _ln(x, g, b):
            m = x.mean(-1, keepdims=True)
            v = x.var(-1, keepdims=True)
            return (x - m) / jnp.sqrt(v + LN_EPS) * g + b
        B, L, D = x.shape
        H = NUM_HEADS
        E = D // H
        xn = _ln(x, ln1_g, ln1_b)
        qkv = (xn @ attn_qkv_w + attn_qkv_b).reshape(B, L, 3, H, E)
        q = jnp.transpose(qkv[:, :, 0], (0, 2, 1, 3))
        k = jnp.transpose(qkv[:, :, 1], (0, 2, 1, 3))
        v = jnp.transpose(qkv[:, :, 2], (0, 2, 1, 3))
        scale = 1.0 / jnp.sqrt(jnp.float32(E))
        scores = jnp.einsum('bhqe,bhke->bhqk', q, k) * scale
        i = jnp.arange(L)[:, None]
        j = jnp.arange(L)[None, :]
        mask = (j > i) | (j <= i - WINDOW)
        scores = jnp.where(mask, jnp.float32(-10000.0), scores)
        attn = jax.nn.softmax(scores, axis=-1)
        ao = jnp.einsum('bhqk,bhke->bhqe', attn, v)
        ao = jnp.transpose(ao, (0, 2, 1, 3)).reshape(B, L, D)
        ao = ao @ attn_proj_w + attn_proj_b
        qkv2 = xn @ ssm_qkv_w + ssm_qkv_b
        q2, k2, v2 = jnp.split(qkv2, 3, axis=-1)
        q2 = q2.reshape(B, L, H, E)
        k2 = k2.reshape(B, L, H, E)
        v2 = v2.reshape(B, L, H, E)
        q2 = jax.nn.elu(q2) + (1.0 + 0.0001)
        k2 = jax.nn.elu(k2) + (1.0 + 0.0001)
        q2 = q2 * scale
        kv = jnp.einsum('blhe,blhf->blhef', k2, v2)
        kv_cumsum = jnp.cumsum(kv, axis=1)
        k_cumsum = jnp.cumsum(k2, axis=1)
        num = jnp.einsum('blhe,blhef->blhf', q2, kv_cumsum)
        den = jnp.einsum('blhe,blhe->blh', q2, k_cumsum)[..., None] + 0.0001
        so = (num / den).reshape(B, L, D)
        so = so @ ssm_out_w + ssm_out_b
        so = _ln(so, ssm_ln_g, ssm_ln_b)
        x2 = x + (ao + so) @ out_w + out_b
        h = _ln(x2, lnm_g, lnm_b)
        h = jax.nn.gelu(h @ mlp_w1 + mlp_b1, approximate=False)
        return x2 + (h @ mlp_w2 + mlp_b2)

    def _L0_ffn_ref(x, gate_w, w13, w2, norm_w):
        import jax, jax.numpy as jnp
        import numpy as np
        import math
        B, S, D = (4, 1024, 192)
        E = 8
        TOP_K = 2
        H = 512
        CAP_F = 1.25
        EPS = 1e-06
        ALPHA = 1.0
        Bx, Sx, Dx = x.shape
        N = Bx * Sx
        cap = int(math.ceil(CAP_F * TOP_K * N / E))
        xf = x.reshape(N, Dx)
        logits = xf.astype(jnp.float32) @ gate_w.T
        probs = jax.nn.softmax(logits, axis=-1)
        top_p, top_i = jax.lax.top_k(probs, TOP_K)
        w = top_p / jnp.sum(top_p, axis=-1, keepdims=True)
        flat_e = top_i.reshape(-1)
        onehot = jax.nn.one_hot(flat_e, E, dtype=jnp.int32)
        pos = jnp.take_along_axis(jnp.cumsum(onehot, axis=0) - 1, flat_e[:, None], axis=1)[:, 0]
        keep = pos < cap
        didx = flat_e * cap + jnp.minimum(pos, cap - 1)
        safe = jnp.where(keep, didx, E * cap)
        x_rep = jnp.repeat(xf, TOP_K, axis=0)
        buf = jnp.zeros((E * cap + 1, Dx), x.dtype).at[safe].set(x_rep)
        buf = buf[:-1].reshape(E, cap, Dx)
        z = 2.0 * buf
        z = z * jax.lax.rsqrt(jnp.mean(z * z, axis=-1, keepdims=True) + EPS)
        z = z * norm_w[:, None, :]
        gu = jnp.einsum('ecd,ehd->ech', z, w13)
        g, u = jnp.split(gu, 2, axis=-1)
        y = buf + ALPHA * jnp.einsum('ech,edh->ecd', jax.nn.silu(g) * u, w2)
        y_tok = y.reshape(E * cap, Dx)[didx]
        cw = (w.reshape(-1) * keep.astype(w.dtype)).astype(x.dtype)
        out = (cw[:, None] * y_tok).reshape(N, TOP_K, Dx).sum(axis=1)
        return out.reshape(Bx, Sx, Dx)
    h = _L0_tok_ref(x, L0_tok_embedding_lookup)
    h = h + _L0_attn_ref(_layernorm(h, axis=-1), L0_attn_ln1_g, L0_attn_ln1_b, L0_attn_attn_qkv_w, L0_attn_attn_qkv_b, L0_attn_attn_proj_w, L0_attn_attn_proj_b, L0_attn_ssm_qkv_w, L0_attn_ssm_qkv_b, L0_attn_ssm_out_w, L0_attn_ssm_out_b, L0_attn_ssm_ln_g, L0_attn_ssm_ln_b, L0_attn_out_w, L0_attn_out_b, L0_attn_mlp_w1, L0_attn_mlp_b1, L0_attn_mlp_w2, L0_attn_mlp_b2, L0_attn_lnm_g, L0_attn_lnm_b)
    h = h + _L0_ffn_ref(_layernorm(h, axis=-1), L0_ffn_gate_w, L0_ffn_w13, L0_ffn_w2, L0_ffn_norm_w)
    return h

_drawn_inputs = setup_inputs


def setup_inputs(seed=0):
    import zlib

    import numpy as np

    out = dict(_drawn_inputs(seed))
    spreads = {'L0_attn_ln1_g': (1.0, 0.6),
     'L0_attn_ln1_b': (0.0, 0.746),
     'L0_attn_attn_qkv_b': (0.0, 0.8),
     'L0_attn_attn_proj_b': (0.0, 0.521),
     'L0_attn_ssm_qkv_b': (0.0, 0.1),
     'L0_attn_ssm_out_b': (0.0, 0.1),
     'L0_attn_ssm_ln_g': (1.0, 0.54),
     'L0_attn_ssm_ln_b': (0.0, 0.569),
     'L0_attn_out_b': (0.0, 0.1),
     'L0_attn_mlp_b1': (0.0, 0.566),
     'L0_attn_mlp_b2': (0.0, 0.1),
     'L0_attn_lnm_g': (1.0, 0.6),
     'L0_attn_lnm_b': (0.0, 0.8),
     'L0_ffn_norm_w': (1.0, 0.6)}
    factors = {'L0_attn_attn_qkv_w': 8.0,
     'L0_attn_attn_proj_w': 8.0,
     'L0_attn_ssm_qkv_w': 3.857,
     'L0_ffn_gate_w': 2.942,
     'L0_ffn_w13': 8.0,
     'L0_ffn_w2': 8.0}
    for name, (base, spread) in spreads.items():
        noise = np.random.default_rng([zlib.crc32(name.encode()), seed]).standard_normal(out[name].shape)
        drawn = base * np.exp(spread * noise) if base else spread * noise
        out[name] = jnp.asarray(drawn.astype(out[name].dtype))
    for name, factor in factors.items():
        out[name] = (out[name] * factor).astype(out[name].dtype)
    return out
```

```python
from contextlib import ExitStack

import numpy as np

import concourse.bass as bass
from concourse import mybir

F32 = mybir.dt.float32
BF16 = mybir.dt.bfloat16
I32 = mybir.dt.int32
ALU = mybir.AluOpType
ACT = mybir.ActivationFunctionType
AX = mybir.AxisListType

P = 128
D = 192
C = 96
NH, HD = 12, 16
HC = C // HD
V1 = HD + 1
WIN = 64
SEQ, NB = 1024, 8
T = SEQ // P
HT = T // 2
HALF = SEQ // 2
FF = 768
NE, EH = 8, 512
CAP = 2560
SLOTS = NE * CAP
NTOK = NB * SEQ
SPILL = 2 * NTOK
BLK = 512
NBLK = CAP // BLK
BT = BLK // P
VOCAB = 50257
MASKED = -30000.0

C_ID, C_WM0, C_WM1, C_CAUS, C_UP, C_ONE, C_HM, C_SM, C_TIE, C_ECAP, C_SP = np.cumsum(
    [0, P, P, P, P, P, P, HC, HC * V1, NE, NE]).tolist()
C_N = C_SP + 16


def constants():
    c = np.zeros((P, C_N), np.float32)
    p = np.arange(P)[:, None]
    f = np.arange(P)[None, :]
    c[:, C_ID:C_ID + P] = p == f
    i = p % WIN
    seen = (f > i) & (f <= i + WIN)
    c[:, C_WM1:C_WM1 + P] = np.where(seen, 0.0, MASKED)
    c[:, C_WM0:C_WM0 + P] = np.where(seen & ((f >= WIN) | (p >= WIN)), 0.0, MASKED)
    c[:, C_CAUS:C_CAUS + P] = p <= f
    c[:, C_UP:C_UP + P] = p < f
    c[:, C_ONE:C_ONE + P] = 1.0
    c[:, C_HM:C_HM + HC] = p // HD == np.arange(HC)[None, :]
    c[:, C_SM:C_SM + HC * V1] = p // HD == np.arange(HC * V1)[None, :] // V1
    c[:, C_TIE:C_TIE + NE] = NE - np.arange(NE)[None, :]
    c[:, C_ECAP:C_ECAP + NE] = CAP * np.arange(NE)[None, :]
    t, k = np.arange(16)[None, :] // 2, np.arange(16)[None, :] % 2
    c[:, C_SP:C_SP + 16] = SLOTS + (t * P + p) * 2 + k
    return c


ORDER = [(s, h) for h in range(2) for s in ("Fa", "Fb", "Fc", "P")]
for _t in range(T + 1):
    for _s in ("V", "Oc", "Sa", "Od", "La", "Oe", "Sb", "Of", "Lb", "Oa", "Ob"):
        _late = _s in ("Oc", "Od", "Oe", "Of")
        if (_t > 0) if _late else (_t < T):
            ORDER.append((_s, _t - _late))
        if (_s, _t - 1) == ("Of", HT - 1):
            ORDER += [("M", 0), ("Ra", 0), ("Rb", 0), ("Rc", 0)]
ORDER += [("M", 1), ("Ra", 1), ("Rb", 1), ("Rc", 1), ("T", 0)]

TR_FILLS = {"Fc": 2, "Sb": 3, "La": 1, "Oa": 1, "Od": 1, "Of": 1, "Rc": HT, "T": 1}
BG_FILLS = {"P": 8, "V": 2, "Sa": 3, "La": 4, "Lb": 1, "M": 6, "T": 1}
OP_FILLS = {"Ob": 1, "Oe": 1, "M": HT}


def fills(table, banks):
    out, k = {}, 0
    for stage, i in ORDER:
        last = i == T - 1 and (stage == "Lb" or (stage == "La" and banks == 2))
        for j in range(0 if last else table.get(stage, 0)):
            out[stage, i, j] = (k % banks, k // banks)
            k += 1
    assert k % banks == 0, (k, banks)
    return out, k // banks


TR, TR_PER = fills(TR_FILLS, 2)
BG, BG_PER = fills(BG_FILLS, 3)
OP, OP_PER = fills(OP_FILLS, 1)

N_LOADS = 18
N_PRESET = 17
DVE_PER = 126
POOL_PER = 41


def phase_a(nc, ids, table, consts, cols, rows3, wqk, wv, wp, ws, wo, w1, w2, gate,
            hbase, zbuf, gidx, cw, NBATCH, dbg):
    with ExitStack() as ca:
        def sa(name, shape, dt=F32):
            return ca.enter_context(nc.sbuf_tensor(name, shape, dt))

        def sem(name):
            return ca.enter_context(nc.semaphore(name))

        cst = sa("cst", [P, C_N])
        ident = cst[:, C_ID:C_ID + P]
        identb = sa("identb", [P, P], BF16)
        wmask = sa("wmask", [P, 2, 4, P], BF16)
        colt = sa("colt", [C, 8])
        rowt = sa("rowt", [P, 3, D])
        wqk_s = sa("wqk_s", [C + 1, 2, 4 * D])
        wv_s = sa("wv_s", [C + 1, 2, 2 * D])
        wp_s = sa("wp_s", [C + 1, 2, D])
        ws_s = sa("ws_s", [C + 1, 2, D])
        wo_s = sa("wo_s", [C + 1, 2, D])
        w1_s = sa("w1_s", [C + 1, 2, FF])
        w2_s = sa("w2_s", [P, FF // P, D])
        gate_s = sa("gate_s", [C, 2, NE])
        ids_s = sa("ids_s", [P, (NB + 1) * T], I32)
        idx_s = sa("idx_s", [P, T], I32)
        half_c = sa("half_c", [P, HT])
        eps_ln = sa("eps_ln", [P, HT])
        eps_rms = sa("eps_rms", [P, HT])
        emb = sa("emb", [P, T, D])
        xb = sa("xb", [P, T, D])
        ebt = sa("ebt", [P, T, D])
        xh = sa("xh", [P, HT, D])
        st = sa("st", [P, HT, 6])
        mv = sa("mv", [P, HT, 2])
        mv2 = sa("mv2", [P, HT, 2])
        rs = sa("rs", [P, HT])
        rs2 = sa("rs2", [P, HT])
        xnT = sa("xnT", [C + 1, 2, WIN + SEQ])
        qT = sa("qT", [C, 2, 2, HALF])
        kT = sa("kT", [C, 2, WIN + SEQ])
        q2T = sa("q2T", [C, 2, 2, HALF])
        k2T = sa("k2T", [C, 2, 2, HALF])
        ex = sa("ex", [C, 2, HALF])
        rl = sa("rl", [C, 2, HALF])
        qm = sa("qm", [C, 2, HC, P])
        q2m = sa("q2m", [C, 2, HC, P])
        va = sa("va", [P, NH, V1])
        vb = sa("vb", [P, 2 * NH, V1])
        nmax = sa("nmax", [P, 3, 4])
        pr = sa("pr", [P, 3, 4, P])
        prT = sa("prT", [P, 2, 4, P])
        at = sa("at", [P, 4, 3, P])
        k2m = sa("k2m", [P, 2, C])
        state = sa("state", [C, 2, HC * V1])
        stated = sa("stated", [C, 2, HC * V1])
        aoso = sa("aoso", [P, 2, D])
        rec = sa("rec", [P, 2, NH])
        aosoT = sa("aosoT", [C + 1, 4, P])
        sh = sa("sh", [P, D])
        ssum = sa("ssum", [P, D])
        sT = sa("sT", [C + 1, 2, P])
        x2 = sa("x2", [P, D])
        hh = sa("hh", [P, D])
        sto = sa("sto", [P, 2, 6])
        mo = sa("mo", [P, 2, 2])
        rso = sa("rso", [P, 2])
        hT = sa("hT", [C + 1, 2, HALF])
        gT = sa("gT", [P, FF // P, HALF])
        h1 = sa("h1", [P, HT, 2, D])
        zn = sa("zn", [P, T, D])
        mr = sa("mr", [P, HT, 2])
        msq = sa("msq", [P, HT])
        rr = sa("rr", [P, 2, HT])
        hlT = sa("hlT", [C, 2, SEQ])
        lg, pb, oh1, oh2, tmp8, pos = (sa(n, [P, T, NE]) for n in ("lg", "pb", "oh1", "oh2", "tmp8", "pos"))
        r1 = sa("r1", [P, 4, T])
        pk = sa("pk", [P, T, 2])
        ek = sa("ek", [P, T, 2])
        keep = sa("keep", [P, T, 2])
        slot = sa("slot", [P, T, 2])
        wk = sa("wk", [P, T, 2])
        carry = sa("carry", [P, NE])
        spill = sa("spill", [P, T, 2])
        sidx = sa("sidx", [P, T, 2], I32)
        zero = sa("zero", [P, 4, D])

        tr = [ca.enter_context(nc.psum_tensor(f"tr{i}", [P, 512], F32)) for i in range(2)]
        bg = [ca.enter_context(nc.psum_tensor(f"bg{i}", [P, 512], F32)) for i in range(3)]
        ao_ps = ca.enter_context(nc.psum_tensor("ao_ps", [P, 512], F32))
        nu_ps = ca.enter_context(nc.psum_tensor("nu_ps", [P, 512], F32))
        op_ps = ca.enter_context(nc.psum_tensor("op_ps", [P, 512], F32))

        loaded, preset, zeroed = sem("loaded"), sem("preset"), sem("zeroed")
        emb_in = [sem(f"emb_in{t}") for t in range(T)]
        e_var, e_rstd, x_var, x_rstd, xh_ready = (
            sem("e_var"), sem("e_rstd"), sem("x_var"), sem("x_rstd"), sem("xh_ready"))
        exp_ready = sem("exp_ready")
        qm_ready, q2m_ready, max_ready = sem("qm_ready"), sem("q2m_ready"), sem("max_ready")
        ao_full, ao_ready, nu_full, so_ready, state_ready = (
            sem("ao_full"), sem("ao_ready"), sem("nu_full"), sem("so_ready"), sem("state_ready"))
        so_var, so_rstd, sh_ready, shg_ready, s_ready = (
            sem("so_var"), sem("so_rstd"), sem("sh_ready"), sem("shg_ready"), sem("s_ready"))
        x2_var, x2_rstd, r_ready, hh_ready = sem("x2_var"), sem("x2_rstd"), sem("r_ready"), sem("hh_ready")
        h_var, h_rstd, hl_ready, z_sq, z_rstd, hb_stored = (
            sem("h_var"), sem("h_rstd"), sem("hl_ready"), sem("z_sq"), sem("z_rstd"), sem("hb_stored"))
        lmax_ready, lexp_ready, cnt_ready, sidx_ready, scattered = (
            sem("lmax_ready"), sem("lexp_ready"), sem("cnt_ready"), sem("sidx_ready"), sem("scattered"))
        tr_full = [sem(f"tr_full{i}") for i in range(2)]
        tr_drained = [sem(f"tr_drained{i}") for i in range(2)]
        bg_full = [sem(f"bg_full{i}") for i in range(3)]
        bg_drained = [sem(f"bg_drained{i}") for i in range(3)]
        op_full, op_drained = sem("op_full"), sem("op_drained")
        dve_step, pool_step = sem("dve_step"), sem("pool_step")
        passed = sem("passed")

        def tr_bank(*key):
            return tr[TR[key][0]]

        def bg_bank(*key):
            return bg[BG[key][0]]

        def wait_tr_full(eng, it, *key):
            eng.wait_ge(tr_full[TR[key][0]], it * TR_PER + (TR[key][1] + 1))

        def wait_tr_drained(eng, it, *key):
            eng.wait_ge(tr_drained[TR[key][0]], it * TR_PER + (TR[key][1] + 2))

        def wait_tr_free(eng, it, *key):
            eng.wait_ge(tr_drained[TR[key][0]], it * TR_PER + (TR[key][1] + 1))

        def wait_bg_full(eng, it, *key):
            eng.wait_ge(bg_full[BG[key][0]], it * BG_PER + (BG[key][1] + 1))

        def wait_bg_drained(eng, it, *key):
            eng.wait_ge(bg_drained[BG[key][0]], it * BG_PER + (BG[key][1] + 2))

        def wait_bg_free(eng, it, *key):
            eng.wait_ge(bg_drained[BG[key][0]], it * BG_PER + (BG[key][1] + 1))

        def wait_op_full(eng, it, *key):
            eng.wait_ge(op_full, it * OP_PER + (OP[key][1] + 1))

        def wait_op_free(eng, it, *key):
            eng.wait_ge(op_drained, it * OP_PER + (OP[key][1] + 1))

        def wait_op_drained(eng, it, *key):
            eng.wait_ge(op_drained, it * OP_PER + (OP[key][1] + 2))

        block = ca.enter_context(nc.Block())

        @block.sync
        def _(sp):
            for dst, src in ((cst[:], consts), (colt[:], cols), (rowt[:], rows3),
                             (ids_s[:, 0:NB * T], ids), (gate_s[:], gate)):
                sp.dma_start(dst, src).then_inc(loaded, 16)
            for dst, src in ((wqk_s, wqk), (wv_s, wv), (wp_s, wp), (ws_s, ws), (wo_s, wo), (w1_s, w1)):
                sp.dma_start(dst[0:C, 0, :], src[0:C, :]).then_inc(loaded, 16)
                sp.dma_start(dst[:, 1, :], src[C:2 * C + 1, :]).then_inc(loaded, 16)
            sp.wait_ge(preset, N_PRESET)
            sp.dma_start(w2_s[:], w2).then_inc(loaded, 16)
            zr = zbuf[0:SLOTS, :].rearrange("(p n r) c -> n p r c", p=P, r=4)
            for n in range(SLOTS // P // 4):
                sp.dma_start(zr[n], zero[:]).then_inc(zeroed, 16)
            with sp.Fori(0, NBATCH) as it:
                for stage, i in ORDER:
                    if stage == "Rc":
                        sp.wait_ge(hl_ready, it * T + HT * (i + 1))
                        dst = hbase[bass.ds(it * SEQ + i * HALF, HALF), :, :].rearrange(
                            "(t p) k c -> p t k c", p=P)
                        sp.dma_start(dst, h1[:]).then_inc(hb_stored, 16)
            sp.wait_ge(hb_stored, 32 * NBATCH + 16)
            sp.wait_ge(zeroed, 16 * (SLOTS // P // 4))

        @block.gpsimd
        def _(pool):
            nc.gpsimd.memset(half_c[:], -0.5).then_inc(preset, 1)
            nc.gpsimd.memset(eps_ln[:], 1e-5).then_inc(preset, 1)
            nc.gpsimd.memset(eps_rms[:], 1e-6).then_inc(preset, 1)
            nc.gpsimd.memset(zero[:], 0.0).then_inc(preset, 1)
            nc.gpsimd.memset(va[:], 1.0).then_inc(preset, 1)
            nc.gpsimd.memset(vb[:], 1.0).then_inc(preset, 1)
            nc.gpsimd.memset(ids_s[:, NB * T:], 0).then_inc(preset, 1)
            pool.wait_ge(loaded, 16 * N_LOADS)
            pool.wait_ge(preset, N_PRESET)

            def gather():
                pool.sem_inc(passed, 1)
                for t in range(T):
                    nc.gpsimd.indirect_dma_start(
                        out=emb[:, t, :], out_offset=None, in_=table,
                        in_offset=bass.IndirectOffsetOnAxis(ap=idx_s[:, t:t + 1], axis=0),
                    ).then_inc(emb_in[t], 16)

            pool.dma_start(spill[:], consts[:, C_SP:C_SP + 2 * T].rearrange("p (t k) -> p t k", k=2),
                           ).then_inc(scattered, 16)
            nc.gpsimd.tensor_copy(idx_s[:], ids_s[:, 0:T]).then_inc(pool_step, 1)
            pool.wait_ge(pool_step, 1)
            gather()
            with pool.Fori(0, NBATCH) as it:
                step = [0]

                def link(ins):
                    step[0] += 1
                    ins.then_inc(pool_step, 1)
                    pool.wait_ge(pool_step, it * POOL_PER + (step[0] + 1))

                def rsqrt(dst, src, n, eps):
                    link(nc.gpsimd.tensor_tensor(out=src, in0=src, in1=eps[:, 0:n], op=ALU.add))
                    return nc.gpsimd.tensor_tensor(out=dst, in0=src, in1=half_c[:, 0:n], op=ALU.pow)

                nhm = cst[0:C, C_HM:C_HM + HC].unsqueeze(2).to_broadcast([C, HC, P])
                for stage, i in ORDER:
                    h, j = i // HT, (i % HT) * P
                    if stage == "Fa":
                        pool.wait_ge(e_var, it * 2 + (i + 1))
                        rsqrt(rs[:], mv[:, :, 1], HT, eps_ln).then_inc(e_rstd, 1)
                    elif stage == "Fb":
                        for t in range(HT * i, HT * i + HT):
                            pool.wait_ge(emb_in[t], it * 16 + 16)
                            link(nc.gpsimd.tensor_tensor(out=ebt[:, t, :], in0=emb[:, t, :], in1=rowt[:, 2, :],
                                                         op=ALU.add))
                        pool.wait_ge(x_var, it * 2 + (i + 1))
                        rsqrt(rs2[:], mv2[:, :, 1], HT, eps_ln).then_inc(x_rstd, 1)
                        if i == 1:
                            link(nc.gpsimd.tensor_copy(idx_s[:], ids_s[:, bass.ds(it * T + T, T)]))
                            gather()
                    elif stage == "Sa":
                        wait_bg_drained(pool, it, "P", h, 1)
                        if i:
                            wait_bg_full(pool, it, "Sa", i - 1, 2)
                        for c in range(2):
                            src = qT[:, h, c, j:j + P].unsqueeze(1).to_broadcast([C, HC, P])
                            nc.gpsimd.tensor_tensor(out=qm[:, c], in0=src, in1=nhm,
                                                    op=ALU.mult).then_inc(qm_ready, 1)
                    elif stage == "La":
                        wait_bg_drained(pool, it, "P", h, 5)
                        if i:
                            wait_bg_full(pool, it, "La", i - 1, 3)
                        for c in range(2):
                            src = q2T[:, h, c, j:j + P].unsqueeze(1).to_broadcast([C, HC, P])
                            nc.gpsimd.tensor_tensor(out=q2m[:, c], in0=src, in1=nhm,
                                                    op=ALU.mult).then_inc(q2m_ready, 1)
                    elif stage == "Ob":
                        pool.wait_ge(so_var, it * T + (i + 1))
                        rsqrt(rso[:, 0:1], mo[:, 0, 1:2], 1, eps_ln).then_inc(so_rstd, 1)
                    elif stage == "Oc":
                        pool.wait_ge(sh_ready, it * T + (i + 1))
                        link(nc.gpsimd.tensor_tensor(out=sh[:], in0=sh[:], in1=rowt[:, 0, :], op=ALU.mult))
                        nc.gpsimd.tensor_tensor(out=sh[:], in0=sh[:], in1=rowt[:, 1, :],
                                                op=ALU.add).then_inc(shg_ready, 1)
                    elif stage == "Oe":
                        pool.wait_ge(x2_var, it * T + (i + 1))
                        rsqrt(rso[:, 1:2], mo[:, 1, 1:2], 1, eps_ln).then_inc(x2_rstd, 1)
                        nc.gpsimd.tensor_tensor(out=ebt[:, i, :], in0=ebt[:, i, :], in1=x2[:],
                                                op=ALU.add).then_inc(r_ready, 1)
                    elif stage == "Ra":
                        pool.wait_ge(h_var, it * 2 + (i + 1))
                        rsqrt(rr[:, 0, :], mr[:, :, 1], HT, eps_ln).then_inc(h_rstd, 1)
                    elif stage == "Rb":
                        pool.wait_ge(z_sq, it * 2 + (i + 1))
                        rsqrt(rr[:, 1, :], msq[:], HT, eps_rms).then_inc(z_rstd, 1)
                    elif stage == "T":
                        pool.wait_ge(sidx_ready, it + 1)
                        pool.wait_ge(zeroed, 16 * (SLOTS // P // 4))
                        pool.sem_inc(passed, 1)
                        for t in range(T):
                            for k in range(2):
                                nc.gpsimd.indirect_dma_start(
                                    out=zbuf, in_=zn[:, t, :], in_offset=None,
                                    out_offset=bass.IndirectOffsetOnAxis(ap=sidx[:, t, k:k + 1], axis=0),
                                ).then_inc(scattered, 16)
                assert step[0] == POOL_PER, step
            for t in range(T):
                pool.wait_ge(emb_in[t], 16 * (NBATCH + 1))
            pool.wait_ge(scattered, NBATCH * T * 2 * 16 + 16)

        @block.scalar
        def _(act):
            act.wait_ge(loaded, 16 * (N_LOADS - 1))
            nc.scalar.copy(identb[:], ident).then_inc(preset, 1)
            for v in range(2):
                src = cst[:, C_WM0 + v * P:C_WM0 + (v + 1) * P].unsqueeze(1).to_broadcast([P, 4, P])
                nc.scalar.copy(wmask[:, v], src).then_inc(preset, 1)
            act.wait_ge(preset, N_PRESET)
            with act.Fori(0, NBATCH) as it:
                for stage, i in ORDER:
                    if stage == "Fc":
                        for c in range(2):
                            wait_tr_full(act, it, "Fc", i, c)
                            nc.scalar.activation(xnT[0:C, c, WIN + i * HALF:WIN + (i + 1) * HALF],
                                                 tr_bank("Fc", i, c)[0:C, :], ACT.Identity,
                                                 bias=colt[:, 2 + c:3 + c], scale=colt[:, c:c + 1],
                                                 ).then_inc(tr_drained[TR["Fc", i, c][0]], 1)
                    elif stage == "P":
                        for c in range(2):
                            wait_bg_full(act, it, "P", i, c)
                            nc.scalar.mul(qT[:, i, c, :], bg_bank("P", i, c)[0:C, :], float(HD) ** -0.5,
                                          ).then_inc(bg_drained[BG["P", i, c][0]], 1)
                        for n in range(4, 8):
                            wait_bg_full(act, it, "P", i, n)
                            if n >= 6:
                                wait_bg_drained(act, it, "P", i, n - 2)
                            nc.scalar.activation(ex[:, n % 2, :], bg_bank("P", i, n)[0:C, :],
                                                 ACT.Exp).then_inc(exp_ready, 1)
                    elif stage == "V":
                        for n, dst in enumerate((va, vb)):
                            wait_bg_full(act, it, "V", i, n)
                            nc.scalar.copy(dst[:, :, 0:HD], bg_bank("V", i, n)[:, 0:D * (n + 1)].rearrange(
                                "p (h e) -> p h e", e=HD)).then_inc(bg_drained[BG["V", i, n][0]], 1)
                    elif stage == "Sa":
                        for g in range(3):
                            act.wait_ge(max_ready, it * 3 * T + (3 * i + g + 1))
                            b = bg_bank("Sa", i, g)
                            for j in range(4):
                                ins = nc.scalar.activation(pr[:, g, j, :], b[:, j * P:(j + 1) * P], ACT.Exp,
                                                           bias=nmax[:, g, j:j + 1])
                            ins.then_inc(bg_drained[BG["Sa", i, g][0]], 1)
                    elif stage == "Sb":
                        for g in range(3):
                            wait_tr_full(act, it, "Sb", i, g)
                            nc.scalar.copy(prT[:, g % 2], tr_bank("Sb", i, g)[:, :].rearrange(
                                "p (j q) -> p j q", j=4)).then_inc(tr_drained[TR["Sb", i, g][0]], 1)
                    elif stage == "La" and i < T - 1:
                        wait_tr_full(act, it, "La", i, 0)
                        nc.scalar.copy(k2m[:], tr_bank("La", i, 0)[:, 0:D].rearrange("p (c f) -> p c f", c=2),
                                       ).then_inc(tr_drained[TR["La", i, 0][0]], 1)
                    elif stage == "Oa":
                        wait_tr_full(act, it, "Oa", i, 0)
                        nc.scalar.copy(aosoT[0:C], tr_bank("Oa", i, 0)[0:C, :].rearrange("p (j q) -> p j q", j=4),
                                       ).then_inc(tr_drained[TR["Oa", i, 0][0]], 1)
                    elif stage == "Od":
                        wait_tr_full(act, it, "Od", i, 0)
                        nc.scalar.copy(sT[0:C], tr_bank("Od", i, 0)[0:C, 0:2 * P].rearrange(
                            "p (c q) -> p c q", c=2)).then_inc(tr_drained[TR["Od", i, 0][0]], 1)
                    elif stage == "Of":
                        wait_tr_full(act, it, "Of", i, 0)
                        j = (i % HT) * P
                        for c in range(2):
                            ins = nc.scalar.activation(hT[0:C, c, j:j + P], tr_bank("Of", i, 0)[0:C, c * P:(c + 1) * P],
                                                       ACT.Identity, bias=colt[:, 6 + c:7 + c],
                                                       scale=colt[:, 4 + c:5 + c])
                        ins.then_inc(tr_drained[TR["Of", i, 0][0]], 1)
                    elif stage == "M":
                        for m in range(FF // P):
                            wait_bg_full(act, it, "M", i, m)
                            nc.scalar.activation(gT[:, m, :], bg_bank("M", i, m)[:, :], ACT.Gelu,
                                                 ).then_inc(bg_drained[BG["M", i, m][0]], 1)
                    elif stage == "Rc":
                        for t in range(HT):
                            wait_tr_full(act, it, "Rc", i, t)
                            j = (i * HT + t) * P
                            nc.scalar.copy(hlT[:, :, j:j + P], tr_bank("Rc", i, t)[0:C, 0:2 * P].rearrange(
                                "p (c q) -> p c q", c=2)).then_inc(tr_drained[TR["Rc", i, t][0]], 1)
                    elif stage == "T":
                        act.wait_ge(lmax_ready, it + 1)
                        nc.scalar.activation(pb[:], lg[:], ACT.Exp).then_inc(lexp_ready, 1)

        @block.vector
        def _(dve):
            for b in (xnT, kT):
                nc.vector.memset(b[0:C, :, 0:WIN], 0.0).then_inc(preset, 1)
            for b in (xnT, aosoT, sT, hT):
                nc.vector.memset(b[C:C + 1], 1.0).then_inc(preset, 1)
            nc.vector.memset(carry[:], 0.0).then_inc(preset, 1)
            dve.wait_ge(loaded, 16 * (N_LOADS - 1))
            dve.wait_ge(preset, N_PRESET)
            caus3 = cst[:, C_CAUS:C_CAUS + P].unsqueeze(1).to_broadcast([P, 3, P])
            smask = cst[0:C, C_SM:C_SM + HC * V1].unsqueeze(1).to_broadcast([C, 2, HC * V1])
            tie8 = cst[:, C_TIE:C_TIE + NE].unsqueeze(1).to_broadcast([P, T, NE])
            ecap8 = cst[:, C_ECAP:C_ECAP + NE].unsqueeze(1).to_broadcast([P, T, NE])

            def each8(ap):
                return ap.unsqueeze(2).to_broadcast([P, T, NE])

            dve.sem_inc(r_ready, 1)
            dve.sem_inc(hb_stored, 16)
            with dve.Fori(0, NBATCH) as it:
                step = [0]

                def mark(ins):
                    step[0] += 1
                    ins.then_inc(dve_step, 1)

                def settle():
                    dve.wait_ge(dve_step, it * DVE_PER + step[0])

                def link(ins):
                    mark(ins)
                    settle()

                def moments(dst, srcs):
                    for t, src in enumerate(srcs):
                        mark(nc.vector.bn_stats(st[:, t, :], src))
                    settle()
                    dve.sem_inc(passed, 1)
                    for t in range(len(srcs)):
                        ins = nc.vector.bn_aggr(dst[:, t, :], st[:, t, :])
                    return ins

                def normalise(dst, src, mean, rstd):
                    return nc.vector.tensor_scalar(dst, src, mean, rstd, ALU.subtract, ALU.mult)

                for stage, i in ORDER:
                    h = i // HT
                    if stage == "Fa":
                        for t in range(HT):
                            dve.wait_ge(emb_in[HT * i + t], it * 16 + 16)
                        moments(mv, [emb[:, HT * i + t, :] for t in range(HT)]).then_inc(e_var, 1)
                    elif stage == "Fb":
                        dve.wait_ge(e_rstd, it * 2 + (i + 1))
                        for t in range(HT):
                            k = HT * i + t
                            mark(normalise(xb[:, k, :], emb[:, k, :], mv[:, t, 0:1], rs[:, t:t + 1]))
                        settle()
                        moments(mv2, [xb[:, HT * i + t, :] for t in range(HT)]).then_inc(x_var, 1)
                    elif stage == "Fc":
                        dve.wait_ge(x_rstd, it * 2 + (i + 1))
                        if i:
                            wait_tr_full(dve, it, "Fc", 0, 1)
                        for t in range(HT):
                            normalise(xh[:, t, :], xb[:, HT * i + t, :], mv2[:, t, 0:1], rs2[:, t:t + 1],
                                      ).then_inc(xh_ready, 1)
                    elif stage == "P":
                        for c in range(2):
                            wait_bg_full(dve, it, "P", i, 2 + c)
                            nc.vector.tensor_copy(kT[:, c, WIN + i * HALF:WIN + (i + 1) * HALF],
                                                  bg_bank("P", i, 2 + c)[0:C, :],
                                                  ).then_inc(bg_drained[BG["P", i, 2 + c][0]], 1)
                        for n in range(4, 8):
                            dve.wait_ge(exp_ready, it * 8 + (4 * i + n - 3))
                            link(nc.vector.tensor_scalar(rl[:, n % 2], bg_bank("P", i, n)[0:C, :], 1e-4, 1e-4,
                                                         ALU.add, ALU.max))
                            dst = (q2T if n < 6 else k2T)[:, i, n % 2, :]
                            nc.vector.scalar_tensor_tensor(dst, ex[:, n % 2, :], 1.0, rl[:, n % 2], ALU.min, ALU.add,
                                                           ).then_inc(bg_drained[BG["P", i, n][0]], 1)
                    elif stage == "Sa":
                        for g in range(3):
                            wait_bg_full(dve, it, "Sa", i, g)
                            nc.vector.tensor_reduce(nmax[:, g, :], bg_bank("Sa", i, g)[:, :].rearrange(
                                "p (j k) -> p j k", j=4), AX.X, ALU.max, negate=True).then_inc(max_ready, 1)
                    elif stage == "La":
                        for g in range(4):
                            wait_bg_full(dve, it, "La", i, g)
                            nc.vector.tensor_tensor(out=at[:, g], in0=bg_bank("La", i, g)[:, 0:3 * P].rearrange(
                                "p (j q) -> p j q", j=3), in1=caus3, op=ALU.mult,
                            ).then_inc(bg_drained[BG["La", i, g][0]], 1)
                    elif stage == "Sb":
                        dve.wait_ge(ao_full, it * T + (i + 1))
                        acc = ao_ps[:, 0:NH * V1].rearrange("p (h e) -> p h e", e=V1)
                        link(nc.vector.reciprocal(rec[:, 0, :], acc[:, :, HD]))
                        nc.vector.tensor_tensor(out=aoso[:, 0, :].rearrange("p (h e) -> p h e", e=HD),
                                                in0=acc[:, :, 0:HD],
                                                in1=rec[:, 0, :].unsqueeze(2).to_broadcast([P, NH, HD]),
                                                op=ALU.mult).then_inc(ao_ready, 1)
                    elif stage == "Lb":
                        if i < T - 1:
                            wait_bg_full(dve, it, "Lb", i, 0)
                            new = bg_bank("Lb", i, 0)[0:C, 0:2 * HC * V1].rearrange("p (c n) -> p c n", c=2)
                            if i == 0:
                                ins = nc.vector.tensor_copy(state[:], new)
                            else:
                                ins = nc.vector.tensor_tensor(out=state[:], in0=new, in1=state[:], op=ALU.add)
                            ins.then_inc(bg_drained[BG["Lb", i, 0][0]], 1)
                            wait_bg_drained(dve, it, "Lb", i, 0)
                            nc.vector.tensor_tensor(out=stated[:], in0=state[:], in1=smask,
                                                    op=ALU.mult).then_inc(state_ready, 1)
                        dve.wait_ge(nu_full, it * T + (i + 1))
                        acc = nu_ps[:, 0:NH * V1].rearrange("p (h e) -> p h e", e=V1)
                        link(nc.vector.tensor_scalar_add(rec[:, 1, :], acc[:, :, HD], 1e-4 * HD ** 0.5))
                        link(nc.vector.reciprocal(rec[:, 1, :], rec[:, 1, :]))
                        nc.vector.tensor_tensor(out=aoso[:, 1, :].rearrange("p (h e) -> p h e", e=HD),
                                                in0=acc[:, :, 0:HD],
                                                in1=rec[:, 1, :].unsqueeze(2).to_broadcast([P, NH, HD]),
                                                op=ALU.mult).then_inc(so_ready, 1)
                    elif stage == "Ob":
                        wait_op_full(dve, it, "Ob", i, 0)
                        link(nc.vector.bn_stats(sto[:, 0, :], op_ps[:, D:2 * D]))
                        dve.sem_inc(passed, 1)
                        nc.vector.bn_aggr(mo[:, 0, :], sto[:, 0, :]).then_inc(so_var, 1)
                    elif stage == "Oc":
                        dve.wait_ge(so_rstd, it * T + (i + 1))
                        normalise(sh[:], op_ps[:, D:2 * D], mo[:, 0, 0:1], rso[:, 0:1]).then_inc(sh_ready, 1)
                    elif stage == "Od":
                        dve.wait_ge(shg_ready, it * T + (i + 1))
                        nc.vector.tensor_tensor(out=ssum[:], in0=op_ps[:, 0:D], in1=sh[:], op=ALU.add,
                                                ).then_inc(op_drained, 1)
                    elif stage == "Oe":
                        wait_op_full(dve, it, "Oe", i, 0)
                        dve.wait_ge(r_ready, it * T + (i + 1))
                        nc.vector.tensor_tensor(out=x2[:], in0=op_ps[:, 0:D], in1=xb[:, i, :], op=ALU.add,
                                                ).then_inc(op_drained, 1)
                        wait_op_drained(dve, it, "Oe", i, 0)
                        link(nc.vector.bn_stats(sto[:, 1, :], x2[:]))
                        dve.sem_inc(passed, 1)
                        nc.vector.bn_aggr(mo[:, 1, :], sto[:, 1, :]).then_inc(x2_var, 1)
                    elif stage == "Of":
                        dve.wait_ge(x2_rstd, it * T + (i + 1))
                        normalise(hh[:], x2[:], mo[:, 1, 0:1], rso[:, 1:2]).then_inc(hh_ready, 1)
                    elif stage == "M":
                        dve.wait_ge(hb_stored, it * 32 + 16 * (i + 1))
                        for t in range(HT):
                            wait_op_full(dve, it, "M", i, t)
                            dve.wait_ge(r_ready, it * T + (HT * i + t + 2))
                            nc.vector.tensor_tensor(out=h1[:, t, 0, :], in0=op_ps[:, 0:D], in1=ebt[:, HT * i + t, :],
                                                    op=ALU.add).then_inc(op_drained, 1)
                        wait_op_drained(dve, it, "M", i, HT - 1)
                    elif stage == "Ra":
                        moments(mr, [h1[:, t, 0, :] for t in range(HT)]).then_inc(h_var, 1)
                    elif stage == "Rb":
                        dve.wait_ge(h_rstd, it * 2 + (i + 1))
                        for t in range(HT):
                            normalise(h1[:, t, 1, :], h1[:, t, 0, :], mr[:, t, 0:1], rr[:, 0, t:t + 1],
                                      ).then_inc(hl_ready, 1)
                        dve.wait_ge(hl_ready, it * T + HT * (i + 1))
                        if i == 0:
                            dve.wait_ge(scattered, it * 16 * 2 * T + 16)
                        for t in range(HT):
                            ins = nc.vector.scalar_tensor_tensor(
                                zn[:, HT * i + t, :], h1[:, t, 1, :], 4.0 / D, h1[:, t, 1, :], ALU.mult, ALU.mult,
                                accum_out=msq[:, t:t + 1])
                        ins.then_inc(z_sq, 1)
                    elif stage == "Rc":
                        dve.wait_ge(z_rstd, it * 2 + (i + 1))
                        for t in range(HT):
                            mark(nc.vector.tensor_scalar(zn[:, HT * i + t, :], h1[:, t, 1, :], rr[:, 1, t:t + 1], 2.0,
                                                         ALU.mult, ALU.mult))
                    elif stage == "T":
                        tt, ts, red = nc.vector.tensor_tensor, nc.vector.tensor_scalar, nc.vector.tensor_reduce
                        wait_tr_full(dve, it, "T", 0, 0)
                        lps = tr_bank("T", 0, 0)[:, 0:T * NE].rearrange("p (t e) -> p t e", e=NE)
                        link(red(r1[:, 0, :], lps, AX.X, ALU.max))
                        tt(out=lg[:], in0=lps, in1=each8(r1[:, 0, :]), op=ALU.subtract).then_inc(lmax_ready, 1)
                        dve.wait_ge(lexp_ready, it + 1)
                        nc.vector.tensor_copy(tmp8[:], lps).then_inc(tr_drained[TR["T", 0, 0][0]], 1)
                        wait_tr_drained(dve, it, "T", 0, 0)
                        link(red(r1[:, 0, :], pb[:], AX.X, ALU.add))
                        link(nc.vector.reciprocal(r1[:, 0, :], r1[:, 0, :]))
                        link(tt(out=pb[:], in0=pb[:], in1=each8(r1[:, 0, :]), op=ALU.mult))
                        for oh, m in ((oh1, 1), (oh2, 2)):
                            link(red(r1[:, m, :], pb[:], AX.X, ALU.max))
                            link(tt(out=tmp8[:], in0=pb[:], in1=each8(r1[:, m, :]), op=ALU.is_equal))
                            link(tt(out=tmp8[:], in0=tmp8[:], in1=tie8, op=ALU.mult))
                            link(red(r1[:, 3, :], tmp8[:], AX.X, ALU.max))
                            link(tt(out=oh[:], in0=tmp8[:], in1=each8(r1[:, 3, :]), op=ALU.is_equal))
                            if m == 1:
                                link(nc.vector.scalar_tensor_tensor(pb[:], oh1[:], -2.0, pb[:], ALU.mult, ALU.add))
                        tt(out=tmp8[:], in0=oh1[:], in1=oh2[:], op=ALU.add).then_inc(cnt_ready, 1)
                        link(tt(out=r1[:, 0, :], in0=r1[:, 1, :], in1=r1[:, 2, :], op=ALU.add))
                        link(nc.vector.reciprocal(r1[:, 0, :], r1[:, 0, :]))
                        for k in range(2):
                            mark(tt(out=wk[:, :, k], in0=r1[:, 1 + k, :], in1=r1[:, 0, :], op=ALU.mult))
                        wait_bg_full(dve, it, "T", 0, 0)
                        cps = bg_bank("T", 0, 0)
                        link(tt(out=pos[:], in0=cps[:, 0:T * NE].rearrange("p (t e) -> p t e", e=NE),
                                in1=carry[:].unsqueeze(1).to_broadcast([P, T, NE]), op=ALU.add))
                        tt(out=carry[:], in0=cps[:, T * NE:(T + 1) * NE], in1=carry[:], op=ALU.add,
                           ).then_inc(bg_drained[BG["T", 0, 0][0]], 1)
                        wait_bg_drained(dve, it, "T", 0, 0)
                        for k, oh in enumerate((oh1, oh2)):
                            link(tt(out=tmp8[:], in0=pos[:], in1=oh[:], op=ALU.mult))
                            link(red(pk[:, :, k], tmp8[:], AX.X, ALU.add))
                            link(tt(out=tmp8[:], in0=oh[:], in1=ecap8, op=ALU.mult))
                            link(red(ek[:, :, k], tmp8[:], AX.X, ALU.add))
                        link(ts(keep[:], pk[:], float(CAP), None, ALU.is_lt))
                        link(tt(out=slot[:], in0=ek[:], in1=pk[:], op=ALU.add))
                        link(tt(out=slot[:], in0=slot[:], in1=spill[:], op=ALU.subtract))
                        link(tt(out=slot[:], in0=slot[:], in1=keep[:], op=ALU.mult))
                        link(tt(out=slot[:], in0=slot[:], in1=spill[:], op=ALU.add))
                        nc.vector.tensor_copy(sidx[:], slot[:]).then_inc(sidx_ready, 1)
                        link(ts(pk[:], pk[:], float(CAP - 1), None, ALU.min))
                        link(tt(out=pk[:], in0=pk[:], in1=ek[:], op=ALU.add))
                        mark(nc.vector.tensor_copy(gidx[:, bass.ds(it * T, T), :], pk[:]))
                        mark(tt(out=cw[:, bass.ds(it * T, T), :], in0=wk[:], in1=keep[:], op=ALU.mult))
                        link(nc.vector.tensor_scalar_add(spill[:], spill[:], float(2 * SEQ)))
                assert step[0] == DVE_PER, step

        @block.tensor
        def _(pe):
            mm, tp = nc.tensor.matmul, nc.tensor.transpose
            pe.wait_ge(loaded, 16 * N_LOADS)
            pe.wait_ge(preset, N_PRESET)
            ident_c = cst[0:C, C_ID:C_ID + C]
            for s in (*tr_drained, *bg_drained, op_drained, ao_ready, so_ready):
                pe.sem_inc(s, 1)
            with pe.Fori(0, NBATCH) as it:
                for stage, i in ORDER:
                    h, j = i // HT, (i % HT) * P
                    if stage == "Fc":
                        pe.wait_ge(xh_ready, it * T + HT * (i + 1))
                        for c in range(2):
                            wait_tr_free(pe, it, "Fc", i, c)
                            for t in range(HT):
                                ins = tp(tr_bank("Fc", i, c)[0:C, t * P:(t + 1) * P], xh[:, t, c * C:(c + 1) * C], ident)
                            ins.then_inc(tr_full[TR["Fc", i, c][0]], 1)
                    elif stage == "P":
                        wait_tr_drained(pe, it, "Fc", i, 1)
                        for n in range(8):
                            wait_bg_free(pe, it, "P", i, n)
                            for c in range(2):
                                ins = mm(bg_bank("P", i, n)[0:C, :], wqk_s[0:C + c, c, n * C:(n + 1) * C],
                                         xnT[0:C + c, c, WIN + i * HALF:WIN + (i + 1) * HALF],
                                         start=(c == 0), stop=(c == 1))
                            ins.then_inc(bg_full[BG["P", i, n][0]], 1)
                    elif stage == "V":
                        for n in range(2):
                            wait_bg_free(pe, it, "V", i, n)
                            s0 = i * P + n * WIN
                            for c in range(2):
                                ins = mm(bg_bank("V", i, n)[:, 0:D * (n + 1)], xnT[0:C + c, c, s0:s0 + P],
                                         wv_s[0:C + c, c, 0:D * (n + 1)], start=(c == 0), stop=(c == 1))
                            ins.then_inc(bg_full[BG["V", i, n][0]], 1)
                    elif stage == "Sa":
                        for g in range(3):
                            wait_bg_free(pe, it, "Sa", i, g)
                            b = bg_bank("Sa", i, g)
                            mm(b[:, :], identb[:], wmask[:, min(i, 1)].rearrange("p j k -> p (j k)"),
                               start=True, stop=False, skip_group_check=True)
                            if g == 0:
                                pe.wait_ge(qm_ready, it * 2 * T + 2 * (i + 1))
                                if i % HT == 0:
                                    wait_bg_drained(pe, it, "P", h, 3)
                            for n in range(4):
                                c, hd = divmod(4 * g + n, HC)
                                for a in range(2):
                                    r = a * WIN
                                    ins = mm(b[r:r + WIN, n * P:(n + 1) * P], qm[:, c, hd, r:r + WIN],
                                             kT[:, c, i * P + r:i * P + r + P],
                                             start=False, stop=(n == 3), skip_group_check=True)
                            ins.then_inc(bg_full[BG["Sa", i, g][0]], 1)
                    elif stage == "La":
                        pe.wait_ge(q2m_ready, it * 2 * T + 2 * (i + 1))
                        if BG["P", h, 7][0] != BG["La", i, 0][0]:
                            wait_bg_drained(pe, it, "P", h, 7)
                        for g in range(4):
                            wait_bg_free(pe, it, "La", i, g)
                            c, hd = divmod(3 * g, HC)
                            mm(bg_bank("La", i, g)[:, 0:3 * P], k2T[:, h, c, j:j + P],
                               q2m[:, c, hd:hd + 3, :].rearrange("p j q -> p (j q)"),
                               start=True, stop=True).then_inc(bg_full[BG["La", i, g][0]], 1)
                        if i < T - 1:
                            wait_tr_free(pe, it, "La", i, 0)
                            for c in range(2):
                                ins = tp(tr_bank("La", i, 0)[:, c * C:(c + 1) * C], k2T[:, h, c, j:j + P], ident_c)
                            ins.then_inc(tr_full[TR["La", i, 0][0]], 1)
                    elif stage == "Sb":
                        def products(g):
                            wait_tr_drained(pe, it, "Sb", i, g)
                            if g == 0:
                                pe.wait_ge(ao_ready, it * T + (i + 1))
                                wait_bg_drained(pe, it, "V", i, 1)
                            for n in range(4):
                                hd = 4 * g + n
                                for a, v in enumerate((va, vb)):
                                    r = a * WIN
                                    ins = mm(ao_ps[r:r + WIN, hd * V1:(hd + 1) * V1], prT[:, g % 2, n, r:r + WIN],
                                             v[:, hd, :], start=True, stop=True, skip_group_check=True)
                            return ins

                        for g in range(3):
                            wait_bg_drained(pe, it, "Sa", i, g)
                            wait_tr_free(pe, it, "Sb", i, g)
                            for n in range(4):
                                ins = tp(tr_bank("Sb", i, g)[:, n * P:(n + 1) * P], pr[:, g, n, :], ident)
                            ins.then_inc(tr_full[TR["Sb", i, g][0]], 1)
                            if g:
                                products(g - 1)
                        products(2).then_inc(ao_full, 1)
                    elif stage == "Lb":
                        pe.wait_ge(so_ready, it * T + (i + 1))
                        if i:
                            pe.wait_ge(state_ready, it * (T - 1) + i)
                            for c in range(2):
                                mm(nu_ps[:, c * HC * V1:(c + 1) * HC * V1], q2T[:, h, c, j:j + P], stated[:, c, :],
                                   start=(c == 0), stop=False, skip_group_check=True)
                        wait_bg_drained(pe, it, "La", i, 3)
                        for hd in range(NH):
                            ins = mm(nu_ps[:, hd * V1:(hd + 1) * V1], at[:, hd // 3, hd % 3, :], vb[:, NH + hd, :],
                                     start=(i == 0 and hd == 0), stop=(hd == NH - 1), skip_group_check=True)
                        ins.then_inc(nu_full, 1)
                        if i < T - 1:
                            wait_tr_drained(pe, it, "La", i, 0)
                            wait_bg_free(pe, it, "Lb", i, 0)
                            for c in range(2):
                                ins = mm(bg_bank("Lb", i, 0)[0:C, c * HC * V1:(c + 1) * HC * V1], k2m[:, c, :],
                                         vb[:, NH + c * HC:NH + (c + 1) * HC, :].rearrange("p h e -> p (h e)"),
                                         start=True, stop=True, skip_group_check=True)
                            ins.then_inc(bg_full[BG["Lb", i, 0][0]], 1)
                    elif stage == "Oa":
                        pe.wait_ge(ao_ready, it * T + (i + 2))
                        pe.wait_ge(so_ready, it * T + (i + 2))
                        wait_tr_free(pe, it, "Oa", i, 0)
                        for n in range(4):
                            ins = tp(tr_bank("Oa", i, 0)[0:C, n * P:(n + 1) * P],
                                     aoso[:, n // 2, (n % 2) * C:(n % 2 + 1) * C], ident)
                        ins.then_inc(tr_full[TR["Oa", i, 0][0]], 1)
                    elif stage == "Ob":
                        wait_tr_drained(pe, it, "Oa", i, 0)
                        wait_op_free(pe, it, "Ob", i, 0)
                        for n, w in enumerate((wp_s, ws_s)):
                            for c in range(2):
                                ins = mm(op_ps[:, n * D:(n + 1) * D], aosoT[0:C + c, 2 * n + c, :], w[0:C + c, c, :],
                                         start=(c == 0), stop=(c == 1), skip_group_check=True)
                        ins.then_inc(op_full, 1)
                    elif stage == "Od":
                        wait_op_drained(pe, it, "Ob", i, 0)
                        wait_tr_free(pe, it, "Od", i, 0)
                        for c in range(2):
                            ins = tp(tr_bank("Od", i, 0)[0:C, c * P:(c + 1) * P], ssum[:, c * C:(c + 1) * C], ident)
                        ins.then_inc(tr_full[TR["Od", i, 0][0]], 1)
                    elif stage == "Oe":
                        wait_tr_drained(pe, it, "Od", i, 0)
                        wait_op_free(pe, it, "Oe", i, 0)
                        for c in range(2):
                            ins = mm(op_ps[:, 0:D], sT[0:C + c, c, :], wo_s[0:C + c, c, :],
                                     start=(c == 0), stop=(c == 1))
                        ins.then_inc(op_full, 1)
                    elif stage == "Of":
                        pe.wait_ge(hh_ready, it * T + (i + 1))
                        wait_tr_free(pe, it, "Of", i, 0)
                        for c in range(2):
                            ins = tp(tr_bank("Of", i, 0)[0:C, c * P:(c + 1) * P], hh[:, c * C:(c + 1) * C], ident)
                        ins.then_inc(tr_full[TR["Of", i, 0][0]], 1)
                    elif stage == "M":
                        wait_tr_drained(pe, it, "Of", HT * i + HT - 1, 0)
                        for m in range(FF // P):
                            wait_bg_free(pe, it, "M", i, m)
                            for c in range(2):
                                ins = mm(bg_bank("M", i, m)[:, :], w1_s[0:C + c, c, m * P:(m + 1) * P], hT[0:C + c, c, :],
                                         start=(c == 0), stop=(c == 1))
                            ins.then_inc(bg_full[BG["M", i, m][0]], 1)
                        for t in range(HT):
                            wait_op_free(pe, it, "M", i, t)
                            for m in range(FF // P):
                                if t == 0:
                                    wait_bg_drained(pe, it, "M", i, m)
                                ins = mm(op_ps[:, 0:D], gT[:, m, t * P:(t + 1) * P], w2_s[:, m, :],
                                         start=(m == 0), stop=(m == FF // P - 1))
                            ins.then_inc(op_full, 1)
                    elif stage == "Rc":
                        pe.wait_ge(hl_ready, it * T + HT * (i + 1))
                        for t in range(HT):
                            wait_tr_free(pe, it, "Rc", i, t)
                            for c in range(2):
                                ins = tp(tr_bank("Rc", i, t)[0:C, c * P:(c + 1) * P], h1[:, t, 1, c * C:(c + 1) * C], ident)
                            ins.then_inc(tr_full[TR["Rc", i, t][0]], 1)
                    elif stage == "T":
                        wait_tr_drained(pe, it, "Rc", 1, HT - 1)
                        wait_tr_free(pe, it, "T", 0, 0)
                        for t in range(T):
                            for c in range(2):
                                ins = mm(tr_bank("T", 0, 0)[:, t * NE:(t + 1) * NE], hlT[:, c, t * P:(t + 1) * P],
                                         gate_s[:, c, :], start=(c == 0), stop=(c == 1), skip_group_check=True)
                        ins.then_inc(tr_full[TR["T", 0, 0][0]], 1)
                        pe.wait_ge(cnt_ready, it + 1)
                        wait_bg_free(pe, it, "T", 0, 0)
                        b = bg_bank("T", 0, 0)
                        up, one = cst[:, C_UP:C_UP + P], cst[:, C_ONE:C_ONE + P]
                        mm(b[:, 0:T * NE], up, tmp8[:].rearrange("p t e -> p (t e)"),
                           start=True, stop=False, skip_group_check=True)
                        for t in range(T):
                            n = T - 1 - t
                            if n:
                                mm(b[:, (t + 1) * NE:T * NE].rearrange("p (t e) -> p t e", e=NE), one,
                                   tmp8[:, t, :].unsqueeze(1).to_broadcast([P, n, NE]),
                                   start=False, stop=False, skip_group_check=True)
                            ins = mm(b[:, T * NE:(T + 1) * NE], one, tmp8[:, t, :],
                                     start=False, stop=(t == T - 1), skip_group_check=True)
                        ins.then_inc(bg_full[BG["T", 0, 0][0]], 1)


def phase_b(nc, w13, w2e, nw, consts, zbuf, ybuf, NPAIR):
    with ExitStack() as cb:
        def sa(name, shape, dt=F32):
            return cb.enter_context(nc.sbuf_tensor(name, shape, dt))

        def sem(name):
            return cb.enter_context(nc.semaphore(name))

        NBK = 2 * NBLK
        idb = sa("idb", [P, P])
        w13_s = sa("w13_s", [C, 2, 2, 2 * EH])
        w2_s = sa("w2e_s", [P, 2, EH // P, D])
        nw_s = sa("nw_s", [C, 2, 2])
        z = sa("z", [P, 2, BT, D])
        zT = sa("zT", [C, 2, 2, BLK])
        sg = sa("sg", [P, 2, BLK])
        hm = sa("hm", [P, 2, EH // P, BLK])
        y = sa("y", [P, 2, BT, D])
        tr = [cb.enter_context(nc.psum_tensor(f"btr{i}", [P, 512], F32)) for i in range(2)]
        gu = [cb.enter_context(nc.psum_tensor(f"bgu{i}", [P, 512], F32)) for i in range(4)]
        yp = [cb.enter_context(nc.psum_tensor(f"byp{i}", [P, 512], F32)) for i in range(2)]
        id_in = sem("id_in")
        w_in = [sem(f"w_in{x}") for x in range(2)]
        z_in = [sem(f"z_in{b}") for b in range(2)]
        y_out = [sem(f"y_out{b}") for b in range(2)]
        t_full, zT_ready, g_full, silu_ready, hm_ready, y_full, y_ready = (
            sem("t_full"), sem("zT_ready"), sem("g_full"), sem("silu_ready"), sem("hm_ready"),
            sem("y_full"), sem("y_ready"))
        MG = EH // P
        block = cb.enter_context(nc.Block())
        zv = zbuf[0:SLOTS, :].rearrange("(b s p) c -> b p s c", s=BT, p=P)
        yv = ybuf.rearrange("(b s p) c -> b p s c", s=BT, p=P)

        @block.sync
        def _(sp):
            sp.dma_start(idb[:], consts[:, C_ID:C_ID + P]).then_inc(id_in, 16)
            sp.sem_inc(y_full, 1)
            with sp.Fori(0, NPAIR) as it:
                for x in range(2):
                    sp.wait_ge(y_full, it * (NBK * BT) + 1)
                    sp.dma_start(w13_s[:, x], w13[bass.ds(it * 2 + x, 1)].rearrange("o p c f -> p (o c) f"),
                                 ).then_inc(w_in[x], 16)
                    sp.dma_start(w2_s[:, x], w2e[bass.ds(it * 2 + x, 1)].rearrange("o p c f -> p (o c) f"),
                                 ).then_inc(w_in[x], 16)
                    sp.dma_start(nw_s[:, x], nw[bass.ds(it * 2 + x, 1)].rearrange("o p c -> p (o c)"),
                                 ).then_inc(w_in[x], 16)
                for b in range(NBK):
                    if b >= 2:
                        sp.wait_ge(t_full, it * (2 * NBK) + 2 * (b - 1))
                    sp.dma_start(z[:, b % 2], zv[bass.ds(it * NBK + b, 1)].rearrange("o p s c -> p (o s) c"),
                                 ).then_inc(z_in[b % 2], 16)

        @block.scalar
        def _(act):
            with act.Fori(0, NPAIR) as it:
                def store(b):
                    act.wait_ge(y_ready, it * (NBK * BT) + (BT * (b + 1) + 1))
                    act.dma_start(yv[bass.ds(it * NBK + b, 1)].rearrange("o p s c -> p (o s) c"), y[:, b % 2],
                                  ).then_inc(y_out[b % 2], 16)

                for b in range(NBK):
                    x = b // NBLK
                    for c in range(2):
                        if c == 0 and b % NBLK == 0:
                            act.wait_ge(w_in[x], it * 48 + 48)
                        act.wait_ge(t_full, it * (2 * NBK) + (2 * b + c + 1))
                        nc.scalar.mul(zT[:, b % 2, c, :], tr[c][0:C, :], nw_s[:, x, c:c + 1]).then_inc(zT_ready, 1)
                    for m in range(MG):
                        k = b * MG + m
                        act.wait_ge(g_full, it * (NBK * MG) + (k + 1))
                        if k >= 2:
                            act.wait_ge(hm_ready, it * (NBK * MG) + k)
                        nc.scalar.activation(sg[:, k % 2, :], gu[2 * (k % 2)][:, :], ACT.Silu).then_inc(silu_ready, 1)
                    if b:
                        store(b - 1)
                store(NBK - 1)
            for b in range(2):
                act.wait_ge(y_out[b], 16 * NPAIR * NBLK + 16)

        @block.vector
        def _(dve):
            for b in range(2):
                dve.sem_inc(y_out[b], 16)
            with dve.Fori(0, NPAIR) as it:
                for b in range(NBK):
                    for m in range(MG):
                        k = b * MG + m
                        dve.wait_ge(silu_ready, it * (NBK * MG) + (k + 1))
                        nc.vector.tensor_tensor(out=hm[:, b % 2, m, :], in0=gu[2 * (k % 2) + 1][:, :],
                                                in1=sg[:, k % 2, :], op=ALU.mult).then_inc(hm_ready, 1)
                    for s in range(BT):
                        k = b * BT + s
                        dve.wait_ge(y_full, it * (NBK * BT) + (k + 2))
                        if s == 0:
                            dve.wait_ge(y_out[b % 2], it * (16 * NBLK) + 16 * (b // 2 + 1))
                        nc.vector.tensor_copy(y[:, b % 2, s, :], yp[k % 2][:, 0:D]).then_inc(y_ready, 1)

        @block.tensor
        def _(pe):
            pe.wait_ge(id_in, 16)
            for s in (zT_ready, y_ready, hm_ready):
                pe.sem_inc(s, 1)
            with pe.Fori(0, NPAIR) as it:
                def down(b):
                    pe.wait_ge(hm_ready, it * (NBK * MG) + ((b + 1) * MG + 1))
                    for s in range(BT):
                        k = b * BT + s
                        pe.wait_ge(y_ready, it * (NBK * BT) + max(k, 1))
                        for m in range(MG):
                            ins = nc.tensor.matmul(yp[k % 2][:, 0:D], hm[:, b % 2, m, s * P:(s + 1) * P],
                                                   w2_s[:, b // NBLK, m, :], start=(m == 0), stop=(m == MG - 1))
                        ins.then_inc(y_full, 1)

                for b in range(NBK):
                    x = b // NBLK
                    pe.wait_ge(z_in[b % 2], it * (16 * NBLK) + 16 * (b // 2 + 1))
                    for c in range(2):
                        pe.wait_ge(zT_ready, it * (2 * NBK) + max(2 * b + c, 1))
                        for s in range(BT):
                            ins = nc.tensor.transpose(tr[c][0:C, s * P:(s + 1) * P], z[:, b % 2, s, c * C:(c + 1) * C],
                                                      idb[:])
                        ins.then_inc(t_full, 1)
                    if b:
                        down(b - 1)
                    pe.wait_ge(zT_ready, it * (2 * NBK) + (2 * b + 3))
                    if b % NBLK == 0:
                        pe.wait_ge(w_in[x], it * 48 + 48)
                    for m in range(MG):
                        k = b * MG + m
                        pe.wait_ge(hm_ready, it * (NBK * MG) + max(k, 1))
                        for u in range(2):
                            for c in range(2):
                                ins = nc.tensor.matmul(
                                    gu[2 * (k % 2) + u][:, :], w13_s[:, x, c, u * EH + m * P:u * EH + (m + 1) * P],
                                    zT[:, b % 2, c, :], start=(c == 0), stop=(c == 1))
                        ins.then_inc(g_full, 1)
                down(NBK - 1)


def phase_c(nc, hbase, ybuf, out, gidx, cw, NT):
    with ExitStack() as cc:
        def sa(name, shape, dt=F32):
            return cc.enter_context(nc.sbuf_tensor(name, shape, dt))

        def sem(name):
            return cc.enter_context(nc.semaphore(name))

        U = 4
        passed = sem("passed")
        ix = sa("ix", [P, U, 2], I32)
        wt = sa("wt", [P, U, 3])
        hb = sa("hb", [P, U, 2, D])
        yg = sa("yg", [P, U, 2, D])
        o = sa("o", [P, U, 3, D])
        h_in = [sem(f"h_in{u}") for u in range(U)]
        y_in = [sem(f"y_in{u}") for u in range(U)]
        o_out = [sem(f"o_out{u}") for u in range(U)]
        ix_ready, w_ready, s_ready, o_ready, step = (
            sem("ix_ready"), sem("w_ready"), sem("s_ready"), sem("o_ready"), sem("c_step"))
        block = cc.enter_context(nc.Block())
        hv = hbase.rearrange("(t p) k c -> t p k c", p=P)
        ov = out.rearrange("(t p) c -> t p c", p=P)

        @block.sync
        def _(sp):
            with sp.Fori(0, NT // U) as it:
                for u in range(U):
                    sp.wait_ge(o_ready, it * U + 1)
                    sp.dma_start(hb[:, u], hv[bass.ds(it * U + u, 1)].rearrange("o p k c -> p (o k) c"),
                                 ).then_inc(h_in[u], 16)

        @block.gpsimd
        def _(pool):
            with pool.Fori(0, NT // U) as it:
                pool.wait_ge(o_ready, it * U + 1)
                nc.gpsimd.tensor_copy(ix[:], gidx[:, bass.ds(it * U, U), :]).then_inc(ix_ready, 1)
                pool.wait_ge(ix_ready, it + 1)
                pool.sem_inc(passed, 1)
                for u in range(U):
                    for k in range(2):
                        nc.gpsimd.indirect_dma_start(
                            out=yg[:, u, k, :], out_offset=None, in_=ybuf,
                            in_offset=bass.IndirectOffsetOnAxis(ap=ix[:, u, k:k + 1], axis=0),
                        ).then_inc(y_in[u], 16)

        @block.vector
        def _(dve):
            dve.sem_inc(o_ready, 1)
            for u in range(U):
                dve.sem_inc(o_out[u], 16)
            with dve.Fori(0, NT // U) as it:
                nc.vector.tensor_copy(wt[:, :, 0:2], cw[:, bass.ds(it * U, U), :]).then_inc(step, 1)
                dve.wait_ge(step, it * (3 * U + 2) + 1)
                nc.vector.tensor_tensor(out=wt[:, :, 2], in0=wt[:, :, 0], in1=wt[:, :, 1], op=ALU.add).then_inc(step, 1)
                dve.wait_ge(step, it * (3 * U + 2) + 2)
                for u in range(U):
                    dve.wait_ge(h_in[u], it * 16 + 16)
                    nc.vector.scalar_tensor_tensor(o[:, u, 0, :], hb[:, u, 1, :], wt[:, u, 2:3], hb[:, u, 0, :],
                                                   ALU.mult, ALU.add).then_inc(step, 1)
                dve.wait_ge(step, it * (3 * U + 2) + (U + 2))
                for k in range(2):
                    for u in range(U):
                        if k == 0:
                            dve.wait_ge(y_in[u], it * 32 + 32)
                        else:
                            dve.wait_ge(o_out[u], it * 16 + 16)
                        ins = nc.vector.scalar_tensor_tensor(o[:, u, k + 1, :], yg[:, u, k, :], wt[:, u, k:k + 1],
                                                             o[:, u, k, :], ALU.mult, ALU.add)
                        ins.then_inc(step if k == 0 else o_ready, 1)
                    if k == 0:
                        dve.wait_ge(step, it * (3 * U + 2) + (2 * U + 2))
                for u in range(U):
                    nc.vector.memset(wt[:, u, 2:3], 0.0).then_inc(step, 1)
                dve.wait_ge(step, it * (3 * U + 2) + (3 * U + 2))

        @block.scalar
        def _(act):
            with act.Fori(0, NT // U) as it:
                for u in range(U):
                    act.wait_ge(o_ready, it * U + (u + 2))
                    act.dma_start(ov[bass.ds(it * U + u, 1)].rearrange("o p c -> p (o c)"), o[:, u, 2, :],
                                  ).then_inc(o_out[u], 16)
            for u in range(U):
                act.wait_ge(o_out[u], 16 * (NT // U) + 16)


def lay_out(a):
    f = lambda n: np.asarray(a[n])
    g = lambda n: f("L0_attn_" + n)

    def with_bias(w, b):
        return np.ascontiguousarray(np.concatenate([w, b[None, :]], 0))

    qkv, qkv2 = (with_bias(g(n + "_w"), g(n + "_b")) for n in ("attn_qkv", "ssm_qkv"))
    two = lambda v: v.reshape(2, C).T
    ins = {
        "ids": np.ascontiguousarray(f("x").reshape(NB * T, P).T),
        "table": f("L0_tok_embedding_lookup"),
        "consts": constants(),
        "cols": np.concatenate([two(g(n)) for n in ("ln1_g", "ln1_b", "lnm_g", "lnm_b")], 1),
        "rows3": np.broadcast_to(np.stack([g("ssm_ln_g"), g("ssm_ln_b"), g("mlp_b2")])[None], (P, 3, D)),
        "wqk": np.concatenate([qkv[:, 0:2 * D], qkv2[:, 0:2 * D]], 1),
        "wv": np.concatenate([qkv[:, 2 * D:], qkv2[:, 2 * D:]], 1),
        "wp": with_bias(g("attn_proj_w"), g("attn_proj_b")),
        "ws": with_bias(g("ssm_out_w"), g("ssm_out_b")),
        "wo": with_bias(g("out_w"), g("out_b")),
        "w1": with_bias(g("mlp_w1"), g("mlp_b1")),
        "w2": g("mlp_w2").reshape(FF // P, P, D).transpose(1, 0, 2),
        "gate": f("L0_ffn_gate_w").T.reshape(2, C, NE).transpose(1, 0, 2),
        "w13": f("L0_ffn_w13").transpose(0, 2, 1).reshape(NE, 2, C, 2 * EH).transpose(0, 2, 1, 3),
        "w2e": f("L0_ffn_w2").transpose(0, 2, 1).reshape(NE, EH // P, P, D).transpose(0, 2, 1, 3),
        "nw": f("L0_ffn_norm_w").reshape(NE, 2, C).transpose(0, 2, 1),
    }
    return {k: np.ascontiguousarray(v) for k, v in ins.items()}


def build(nc, ins, out, NBATCH=NB, NPAIR=NE // 2, NT=NB * T, phases="abc"):
    hbase = nc.dram_tensor("hbase", [NTOK, 2, D], F32).ap()
    zbuf = nc.dram_tensor("zbuf", [SLOTS + SPILL, D], F32).ap()
    ybuf = nc.dram_tensor("ybuf", [SLOTS, D], F32).ap()
    with nc.sbuf_tensor("gidx", [P, NB * T, 2], I32) as gidx, nc.sbuf_tensor("cw", [P, NB * T, 2], F32) as cw:
        phase_a(nc, ins["ids"], ins["table"], ins["consts"], ins["cols"], ins["rows3"], ins["wqk"], ins["wv"],
                ins["wp"], ins["ws"], ins["wo"], ins["w1"], ins["w2"], ins["gate"], hbase, zbuf, gidx, cw, NBATCH, None)
        if "b" in phases:
            phase_b(nc, ins["w13"], ins["w2e"], ins["nw"], ins["consts"], zbuf, ybuf, NPAIR)
        if "c" in phases:
            phase_c(nc, hbase, ybuf, out, gidx, cw, NT)


def kernel(**inputs):
    import concourse.bacc as bacc
    from concourse.bass_utils import run_bass_kernel_spmd

    arrays = lay_out(inputs)
    nc = bacc.Bacc("TRN2", target_bir_lowering=False, num_devices=1)
    ins = {k: nc.dram_tensor(k, v.shape, mybir.dt.from_np(v.dtype), kind="ExternalInput").ap()
           for k, v in arrays.items()}
    out = nc.dram_tensor("out", (NTOK, D), F32, kind="ExternalOutput").ap()
    build(nc, ins, out)
    r = run_bass_kernel_spmd(nc, [arrays], core_ids=[0])
    return r.results[0]["out"].reshape(NB, SEQ, D)
```

```python
from contextlib import ExitStack

import numpy as np

import concourse.bass as bass
from concourse import mybir

F32 = mybir.dt.float32
BF16 = mybir.dt.bfloat16
F32R = mybir.dt.float32r
I32 = mybir.dt.int32
ALU = mybir.AluOpType
ACT = mybir.ActivationFunctionType
AX = mybir.AxisListType

P = 128
D = 192
C = 96
NH, HD = 12, 16
HC = C // HD
V1 = HD + 1
WIN = 64
SEQ, NB = 1024, 8
T = SEQ // P
HT = T // 2
HALF = SEQ // 2
FF = 768
NE, EH = 8, 512
CAP = 2560
SLOTS = NE * CAP
NTOK = NB * SEQ
SPILL = 2 * NTOK
BLK = 512
NBLK = CAP // BLK
BT = BLK // P
VOCAB = 50257
MASKED = -30000.0

C_ID, C_WM0, C_WM1, C_CAUS, C_UP, C_ONE, C_HM, C_SM, C_TIE, C_ECAP, C_SP = np.cumsum(
    [0, P, P, P, P, P, P, HC, HC * V1, NE, NE]).tolist()
C_N = C_SP + 16


def constants():
    c = np.zeros((P, C_N), np.float32)
    p = np.arange(P)[:, None]
    f = np.arange(P)[None, :]
    c[:, C_ID:C_ID + P] = p == f
    i = p % WIN
    seen = (f > i) & (f <= i + WIN)
    c[:, C_WM1:C_WM1 + P] = np.where(seen, 0.0, MASKED)
    c[:, C_WM0:C_WM0 + P] = np.where(seen & ((f >= WIN) | (p >= WIN)), 0.0, MASKED)
    c[:, C_CAUS:C_CAUS + P] = p <= f
    c[:, C_UP:C_UP + P] = p < f
    c[:, C_ONE:C_ONE + P] = 1.0
    c[:, C_HM:C_HM + HC] = p // HD == np.arange(HC)[None, :]
    c[:, C_SM:C_SM + HC * V1] = p // HD == np.arange(HC * V1)[None, :] // V1
    c[:, C_TIE:C_TIE + NE] = NE - np.arange(NE)[None, :]
    c[:, C_ECAP:C_ECAP + NE] = CAP * np.arange(NE)[None, :]
    t, k = np.arange(16)[None, :] // 2, np.arange(16)[None, :] % 2
    c[:, C_SP:C_SP + 16] = SLOTS + (t * P + p) * 2 + k
    return c


STEP = (("V", 0), ("Oe", -2), ("Sa", 0), ("On", -2), ("Oa", -1), ("La", 0), ("Of", -2), ("Sp", 0), ("Ob", -1),
        ("Oc", -1), ("Qm", 1), ("Qn", 1), ("Os", -1), ("Sq", 0), ("Sr", 0), ("Lb", 0), ("Od", -1))
AFTER = {
    (1, "Sr"): [("M", 1, 1)], (1, "Lb"): [("Ra", 1, 1)], (1, "Od"): [("Fa", 1, 0)],
    (2, "Os"): [("Rb", 1, 1)], (2, "Sr"): [("Fb", 1, 0)], (3, "V"): [("Rc", 1, 1)], (3, "Sa"): [("Fc", 1, 0)],
    (3, "Sp"): [("P", 1, 0)],
    (4, "Oa"): [("T", 0, 1)], (4, "Os"): [("Tb", 0, 1)], (4, "Od"): [("Tc", 0, 1)],
    (5, "Oe"): [("Td", 0, 1)], (5, "La"): [("Te", 0, 1)],
    (5, "Sr"): [("M", 0, 0), ("Tf", 0, 1)], (5, "Lb"): [("Ra", 0, 0)], (5, "Od"): [("Fa", 0, -1)],
    (6, "Os"): [("Rb", 0, 0)], (6, "Sr"): [("Fb", 0, -1)], (7, "V"): [("Rc", 0, 0)], (7, "Sa"): [("Fc", 0, -1)],
    (7, "Sp"): [("P", 0, -1)],
}
BODY = []
for _t in range(T):
    for _s, _d in STEP:
        BODY.append((_s, (_t + _d) % T, -((_t + _d) // T)))
        BODY += AFTER.get((_t, _s), [])
LAG = {(_s, _i): _lag for _s, _i, _lag in BODY}
BODIES = {-1: [x for x in BODY if x[2] == -1], 0: [x for x in BODY if x[2] <= 0], 1: BODY,
          2: [x for x in BODY if x[2] == 1]}

TR_FILLS = {"Fc": 2, "Sp": 2, "Sq": 1, "La": 1, "Oa": 1, "Od": 1, "Of": 1, "Rc": HT, "T": 1}
BG_FILLS = {"P": 8, "V": 2, "Sa": 3, "La": 4, "Lb": 1, "M": FF // P + HT, "Td": 1}
OP_FILLS = {"Ob": 1, "Oe": 1}


class Ring:

    def __init__(self, table, banks):
        def keys(body):
            for stage, i, _ in BODIES[body]:
                last = i == T - 1 and (stage == "Lb" or (stage == "La" and banks == 2))
                for j in range(0 if last else table.get(stage, 0)):
                    yield stage, i, j
        self.bank = {key: k % banks for k, key in enumerate(keys(1))}
        self.per = [list(self.bank.values()).count(b) for b in range(banks)]
        self.before, count = {}, [0] * banks
        for body in BODIES:
            for key in keys(body):
                self.before[body, key] = count[self.bank[key]]
                count[self.bank[key]] += 1

    def __getitem__(self, key):
        return self.bank[key]

    def fills(self, seq, key, n):
        per, body = self.per[self.bank[key]], seq.first + LAG[key[0], key[1]]
        if seq.reg is not None:
            return seq.reg * per + (self.before[1, key] + (body - 1) * per + n)
        if body < 1:
            return self.before[body, key] + n
        return self.before[2 if body == seq.total else 1, key] + (seq.total - 2) * per + n


class Seq:

    def __init__(self, reg, first, total, k=1, last=False):
        self.reg, self.first, self.total, self.k, self.last = reg, first, total, k, last

    def __mul__(self, k):
        return Seq(self.reg, self.first, self.total, self.k * k, self.last)

    def __add__(self, c):
        c += self.first * self.k
        return c if self.reg is None else self.reg * self.k + c

    def zeroth(self):
        return self.reg is None and self.first == 0

    def prev(self):
        return Seq(self.reg, self.first - 1, self.total)

    def steps(self, n, per):
        if self.reg is not None:
            return self.reg * per + n
        return n + (self.total - 2) * per if self.last else n


TR, BG, OP = Ring(TR_FILLS, 2), Ring(BG_FILLS, 3), Ring(OP_FILLS, 1)


def traverse(eng, nseq):
    for body in (-1, 0):
        for stage, i, lag in BODIES[body]:
            yield stage, i, Seq(None, body - lag, nseq)
    with eng.Fori(0, nseq - 1) as it:
        for stage, i, lag in BODIES[1]:
            yield stage, i, Seq(it, 1 - lag, nseq)
    for stage, i, lag in BODIES[2]:
        yield stage, i, Seq(None, nseq - lag, nseq, last=True)


N_LOADS = 18
N_PRESET = 17
DVE_PER = 126
POOL_PER = 42


def phase_a(nc, ids, table, consts, cols, rows3, wqk, wv, wp, ws, wo, w1, w2, gate,
            hbase, zbuf, gidx, cw, NBATCH, dbg):
    with ExitStack() as ca:
        def sa(name, shape, dt=F32):
            return ca.enter_context(nc.sbuf_tensor(name, shape, dt))

        def sem(name):
            return ca.enter_context(nc.semaphore(name))

        cst = sa("cst", [P, C_N])
        ident = cst[:, C_ID:C_ID + P]
        identb = sa("identb", [P, P], BF16)
        wmask = sa("wmask", [P, 2, 4, P], BF16)
        colt = sa("colt", [C, 8])
        rowt = sa("rowt", [P, 3, D])
        wqk_s = sa("wqk_s", [C + 1, 2, 4 * D])
        wv_s = sa("wv_s", [C + 1, 2, 2 * D])
        wp_s = sa("wp_s", [C + 1, 2, D])
        ws_s = sa("ws_s", [C + 1, 2, D])
        wo_s = sa("wo_s", [C + 1, 2, D])
        w1_s = sa("w1_s", [C + 1, 2, FF])
        w2_s = sa("w2_s", [P, FF // P, D])
        gate_s = sa("gate_s", [C, 2, NE])
        ids_s = sa("ids_s", [P, (NB + 2) * T], I32)
        idx_s = sa("idx_s", [P, T], I32)
        half_c = sa("half_c", [P, HT])
        eps_ln = sa("eps_ln", [P, HT])
        eps_rms = sa("eps_rms", [P, HT])
        emb = sa("emb", [P, T, D])
        xb = sa("xb", [P, T, D])
        ebt = sa("ebt", [P, T, D])
        xh = sa("xh", [P, HT, D])
        st = sa("st", [P, 2, HT, 6])
        mv = sa("mv", [P, HT, 2])
        mv2 = sa("mv2", [P, HT, 2])
        rs = sa("rs", [P, HT])
        rs2 = sa("rs2", [P, HT])
        xnT = sa("xnT", [C + 1, 2, WIN + SEQ])
        qT = sa("qT", [C, 2, 2, HALF])
        kT = sa("kT", [C, 2, WIN + SEQ])
        q2T = sa("q2T", [C, 2, 2, HALF])
        k2T = sa("k2T", [C, 2, 2, HALF])
        ex = sa("ex", [C, 2, HALF])
        rl = sa("rl", [C, 2, HALF])
        qm = sa("qm", [C, 2, HC, P])
        q2m = sa("q2m", [C, 2, HC, P])
        va = sa("va", [P, NH, V1])
        vb = sa("vb", [P, 2 * NH, V1])
        nmax = sa("nmax", [P, 3, 4])
        pr = sa("pr", [P, 3, 4, P])
        prT = sa("prT", [P, 2, 4, P])
        at = sa("at", [P, 4, 3, P])
        k2m = sa("k2m", [P, 2, C])
        state = sa("state", [C, 2, HC * V1])
        stated = sa("stated", [C, 2, HC * V1])
        aoso = sa("aoso", [P, 2, D])
        rec = sa("rec", [P, 2, NH])
        aosoT = sa("aosoT", [C + 1, 4, P])
        sh = sa("sh", [P, D])
        ssum = sa("ssum", [P, D])
        sT = sa("sT", [C + 1, 2, P])
        x2 = sa("x2", [P, D])
        hh = sa("hh", [P, D])
        sto = sa("sto", [P, 2, 6])
        mo = sa("mo", [P, 2, 2])
        rso = sa("rso", [P, 2])
        hT = sa("hT", [C + 1, 2, HALF])
        gT = sa("gT", [P, FF // P, HALF])
        h1 = sa("h1", [P, HT, 2, D])
        zn = sa("zn", [P, T, D])
        mr = sa("mr", [P, HT, 2])
        msq = sa("msq", [P, HT])
        rr = sa("rr", [P, 2, HT])
        hlT = sa("hlT", [C, 2, SEQ])
        lg, pb, oh1, oh2, tmp8, pos = (sa(n, [P, T, NE]) for n in ("lg", "pb", "oh1", "oh2", "tmp8", "pos"))
        r1 = sa("r1", [P, 4, T])
        pk = sa("pk", [P, T, 2])
        ek = sa("ek", [P, T, 2])
        keep = sa("keep", [P, T, 2])
        slot = sa("slot", [P, T, 2])
        wk = sa("wk", [P, T, 2])
        carry = sa("carry", [P, NE])
        spill = sa("spill", [P, T, 2])
        sidx = sa("sidx", [P, T, 2], I32)
        zero = sa("zero", [P, 4, D])

        tr = [ca.enter_context(nc.psum_tensor(f"tr{i}", [P, 512], F32)) for i in range(2)]
        bg = [ca.enter_context(nc.psum_tensor(f"bg{i}", [P, 512], F32)) for i in range(3)]
        ao_ps = ca.enter_context(nc.psum_tensor("ao_ps", [P, 512], F32))
        nu_ps = ca.enter_context(nc.psum_tensor("nu_ps", [P, 512], F32))
        op_ps = ca.enter_context(nc.psum_tensor("op_ps", [P, 512], F32))

        loaded, preset, zeroed = sem("loaded"), sem("preset"), sem("zeroed")
        emb_in = [sem(f"emb_in{t}") for t in range(T)]
        e_var, e_rstd, x_var, x_rstd, xh_ready = (
            sem("e_var"), sem("e_rstd"), sem("x_var"), sem("x_rstd"), sem("xh_ready"))
        exp_ready = sem("exp_ready")
        qm_ready, q2m_ready, max_ready = sem("qm_ready"), sem("q2m_ready"), sem("max_ready")
        ao_full, ao_ready, nu_full, so_ready, state_ready = (
            sem("ao_full"), sem("ao_ready"), sem("nu_full"), sem("so_ready"), sem("state_ready"))
        so_var, so_rstd, sh_ready, shg_ready, s_ready = (
            sem("so_var"), sem("so_rstd"), sem("sh_ready"), sem("shg_ready"), sem("s_ready"))
        x2_var, x2_rstd, r_ready, hh_ready = sem("x2_var"), sem("x2_rstd"), sem("r_ready"), sem("hh_ready")
        h_var, h_rstd, hl_ready, z_sq, z_rstd, hb_stored = (
            sem("h_var"), sem("h_rstd"), sem("hl_ready"), sem("z_sq"), sem("z_rstd"), sem("hb_stored"))
        lmax_ready, lexp_ready, cnt_ready, sidx_ready, scattered = (
            sem("lmax_ready"), sem("lexp_ready"), sem("cnt_ready"), sem("sidx_ready"), sem("scattered"))
        tr_full = [sem(f"tr_full{i}") for i in range(2)]
        tr_drained = [sem(f"tr_drained{i}") for i in range(2)]
        bg_full = [sem(f"bg_full{i}") for i in range(3)]
        bg_drained = [sem(f"bg_drained{i}") for i in range(3)]
        op_full, op_drained = sem("op_full"), sem("op_drained")
        dve_step, pool_step = sem("dve_step"), sem("pool_step")
        passed = sem("passed")

        def tr_bank(*key):
            return tr[TR[key]]

        def bg_bank(*key):
            return bg[BG[key]]

        def wait_tr_full(eng, it, *key):
            eng.wait_ge(tr_full[TR[key]], TR.fills(it, key, 1))

        def wait_tr_drained(eng, it, *key):
            eng.wait_ge(tr_drained[TR[key]], TR.fills(it, key, 2))

        def wait_tr_free(eng, it, *key):
            eng.wait_ge(tr_drained[TR[key]], TR.fills(it, key, 1))

        def wait_bg_full(eng, it, *key):
            eng.wait_ge(bg_full[BG[key]], BG.fills(it, key, 1))

        def wait_bg_drained(eng, it, *key):
            eng.wait_ge(bg_drained[BG[key]], BG.fills(it, key, 2))

        def wait_bg_free(eng, it, *key):
            eng.wait_ge(bg_drained[BG[key]], BG.fills(it, key, 1))

        def wait_op_full(eng, it, *key):
            eng.wait_ge(op_full, OP.fills(it, key, 1))

        def wait_op_free(eng, it, *key):
            eng.wait_ge(op_drained, OP.fills(it, key, 1))

        def wait_op_drained(eng, it, *key):
            eng.wait_ge(op_drained, OP.fills(it, key, 2))

        block = ca.enter_context(nc.Block())

        @block.sync
        def _(sp):
            for dst, src in ((cst[:], consts), (colt[:], cols), (rowt[:], rows3),
                             (ids_s[:, 0:NB * T], ids), (gate_s[:], gate)):
                sp.dma_start(dst, src).then_inc(loaded, 16)
            for dst, src in ((wqk_s, wqk), (wv_s, wv), (wp_s, wp), (ws_s, ws), (wo_s, wo), (w1_s, w1)):
                sp.dma_start(dst[0:C, 0, :], src[0:C, :]).then_inc(loaded, 16)
                sp.dma_start(dst[:, 1, :], src[C:2 * C + 1, :]).then_inc(loaded, 16)
            sp.wait_ge(preset, N_PRESET)
            sp.dma_start(w2_s[:], w2).then_inc(loaded, 16)
            zr = zbuf[0:SLOTS, :].rearrange("(p n r) c -> n p r c", p=P, r=4)
            for n in range(SLOTS // P // 4):
                sp.dma_start(zr[n], zero[:]).then_inc(zeroed, 16)
            for stage, i, it in traverse(sp, NBATCH):
                if stage == "Rc":
                    sp.wait_ge(hl_ready, it * T + HT * (i + 1))
                    dst = hbase[bass.ds(it * SEQ + i * HALF, HALF), :, :].rearrange(
                        "(t p) k c -> p t k c", p=P)
                    sp.dma_start(dst, h1[:]).then_inc(hb_stored, 16)
            sp.wait_ge(hb_stored, 32 * NBATCH + 16)
            sp.wait_ge(zeroed, 16 * (SLOTS // P // 4))

        @block.gpsimd
        def _(pool):
            nc.gpsimd.memset(half_c[:], -0.5).then_inc(preset, 1)
            nc.gpsimd.memset(eps_ln[:], 1e-5).then_inc(preset, 1)
            nc.gpsimd.memset(eps_rms[:], 1e-6).then_inc(preset, 1)
            nc.gpsimd.memset(zero[:], 0.0).then_inc(preset, 1)
            nc.gpsimd.memset(va[:], 1.0).then_inc(preset, 1)
            nc.gpsimd.memset(vb[:], 1.0).then_inc(preset, 1)
            nc.gpsimd.memset(ids_s[:, NB * T:], 0).then_inc(preset, 1)
            pool.wait_ge(loaded, 16 * N_LOADS)
            pool.wait_ge(preset, N_PRESET)

            def gather(h):
                pool.sem_inc(passed, 1)
                for t in range(HT * h, HT * h + HT):
                    nc.gpsimd.indirect_dma_start(
                        out=emb[:, t, :], out_offset=None, in_=table,
                        in_offset=bass.IndirectOffsetOnAxis(ap=idx_s[:, t:t + 1], axis=0),
                    ).then_inc(emb_in[t], 16)

            pool.dma_start(spill[:], consts[:, C_SP:C_SP + 2 * T].rearrange("p (t k) -> p t k", k=2),
                           ).then_inc(scattered, 16)
            nc.gpsimd.tensor_copy(idx_s[:], ids_s[:, 0:T]).then_inc(pool_step, 1)
            pool.wait_ge(pool_step, 1)
            for h in range(2):
                gather(h)
            step = [1, 0]

            def link(ins):
                step[0] += 1
                step[1] += it.reg is not None
                ins.then_inc(pool_step, 1)
                pool.wait_ge(pool_step, it.steps(step[0], POOL_PER))

            def rsqrt(dst, src, n, eps):
                link(nc.gpsimd.tensor_tensor(out=src, in0=src, in1=eps[:, 0:n], op=ALU.add))
                return nc.gpsimd.tensor_tensor(out=dst, in0=src, in1=half_c[:, 0:n], op=ALU.pow)

            nhm = cst[0:C, C_HM:C_HM + HC].unsqueeze(2).to_broadcast([C, HC, P])
            for stage, i, it in traverse(pool, NBATCH):
                h, j = i // HT, (i % HT) * P
                if stage == "Fa":
                    pool.wait_ge(e_var, it * 2 + (i + 1))
                    rsqrt(rs[:], mv[:, :, 1], HT, eps_ln).then_inc(e_rstd, 1)
                elif stage == "Fb":
                    if not it.zeroth():
                        wait_bg_drained(pool, it.prev(), "M", i, FF // P + HT - 1)
                    for t in range(HT * i, HT * i + HT):
                        pool.wait_ge(emb_in[t], it * 16 + 16)
                        link(nc.gpsimd.tensor_tensor(out=ebt[:, t, :], in0=emb[:, t, :], in1=rowt[:, 2, :],
                                                     op=ALU.add))
                    pool.wait_ge(x_var, it * 2 + (i + 1))
                    rsqrt(rs2[:], mv2[:, :, 1], HT, eps_ln).then_inc(x_rstd, 1)
                    link(nc.gpsimd.tensor_copy(idx_s[:, HT * i:HT * i + HT],
                                               ids_s[:, bass.ds(it * T + (T + HT * i), HT)]))
                    gather(i)
                elif stage == "Qm":
                    wait_bg_drained(pool, it, "P", h, 1)
                    if i or not it.zeroth():
                        wait_bg_full(pool, it if i else it.prev(), "Sa", (i - 1) % T, 2)
                    for c in range(2):
                        src = qT[:, h, c, j:j + P].unsqueeze(1).to_broadcast([C, HC, P])
                        nc.gpsimd.tensor_tensor(out=qm[:, c], in0=src, in1=nhm,
                                                op=ALU.mult).then_inc(qm_ready, 1)
                elif stage == "Qn":
                    wait_bg_drained(pool, it, "P", h, 5)
                    if i or not it.zeroth():
                        wait_bg_full(pool, it if i else it.prev(), "La", (i - 1) % T, 3)
                    for c in range(2):
                        src = q2T[:, h, c, j:j + P].unsqueeze(1).to_broadcast([C, HC, P])
                        nc.gpsimd.tensor_tensor(out=q2m[:, c], in0=src, in1=nhm,
                                                op=ALU.mult).then_inc(q2m_ready, 1)
                elif stage == "Ob":
                    pool.wait_ge(so_var, it * T + (i + 1))
                    rsqrt(rso[:, 0:1], mo[:, 0, 1:2], 1, eps_ln).then_inc(so_rstd, 1)
                elif stage == "Oc":
                    pool.wait_ge(sh_ready, it * T + (i + 1))
                    link(nc.gpsimd.tensor_tensor(out=sh[:], in0=sh[:], in1=rowt[:, 0, :], op=ALU.mult))
                    nc.gpsimd.tensor_tensor(out=sh[:], in0=sh[:], in1=rowt[:, 1, :],
                                            op=ALU.add).then_inc(shg_ready, 1)
                elif stage == "Oe":
                    pool.wait_ge(x2_var, it * T + (i + 1))
                    rsqrt(rso[:, 1:2], mo[:, 1, 1:2], 1, eps_ln).then_inc(x2_rstd, 1)
                    nc.gpsimd.tensor_tensor(out=ebt[:, i, :], in0=ebt[:, i, :], in1=x2[:],
                                            op=ALU.add).then_inc(r_ready, 1)
                elif stage == "Ra":
                    pool.wait_ge(h_var, it * 2 + (i + 1))
                    rsqrt(rr[:, 0, :], mr[:, :, 1], HT, eps_ln).then_inc(h_rstd, 1)
                elif stage == "Rb":
                    pool.wait_ge(z_sq, it * 2 + (i + 1))
                    rsqrt(rr[:, 1, :], msq[:], HT, eps_rms).then_inc(z_rstd, 1)
                elif stage == "Tf":
                    pool.wait_ge(sidx_ready, it + 1)
                    pool.wait_ge(zeroed, 16 * (SLOTS // P // 4))
                    pool.sem_inc(passed, 1)
                    for t in range(T):
                        for k in range(2):
                            nc.gpsimd.indirect_dma_start(
                                out=zbuf, in_=zn[:, t, :], in_offset=None,
                                out_offset=bass.IndirectOffsetOnAxis(ap=sidx[:, t, k:k + 1], axis=0),
                            ).then_inc(scattered, 16)
            assert step[1] == POOL_PER, step
            for t in range(T):
                pool.wait_ge(emb_in[t], 16 * (NBATCH + (2 if t < HT else 1)))
            pool.wait_ge(scattered, NBATCH * T * 2 * 16 + 16)

        @block.scalar
        def _(act):
            act.wait_ge(loaded, 16 * (N_LOADS - 1))
            nc.scalar.copy(identb[:], ident).then_inc(preset, 1)
            for v in range(2):
                src = cst[:, C_WM0 + v * P:C_WM0 + (v + 1) * P].unsqueeze(1).to_broadcast([P, 4, P])
                nc.scalar.copy(wmask[:, v], src).then_inc(preset, 1)
            act.wait_ge(preset, N_PRESET)
            for stage, i, it in traverse(act, NBATCH):
                if stage == "Fc":
                    for c in range(2):
                        wait_tr_full(act, it, "Fc", i, c)
                        nc.scalar.activation(xnT[0:C, c, WIN + i * HALF:WIN + (i + 1) * HALF],
                                             tr_bank("Fc", i, c)[0:C, :], ACT.Identity,
                                             bias=colt[:, 2 + c:3 + c], scale=colt[:, c:c + 1],
                                             ).then_inc(tr_drained[TR["Fc", i, c]], 1)
                elif stage == "P":
                    for c in range(2):
                        wait_bg_full(act, it, "P", i, c)
                        nc.scalar.mul(qT[:, i, c, :], bg_bank("P", i, c)[0:C, :], float(HD) ** -0.5,
                                      ).then_inc(bg_drained[BG["P", i, c]], 1)
                    for n in range(4, 8):
                        wait_bg_full(act, it, "P", i, n)
                        if n >= 6:
                            wait_bg_drained(act, it, "P", i, n - 2)
                        nc.scalar.activation(ex[:, n % 2, :], bg_bank("P", i, n)[0:C, :],
                                             ACT.Exp).then_inc(exp_ready, 1)
                elif stage == "V":
                    for n, dst in enumerate((va, vb)):
                        wait_bg_full(act, it, "V", i, n)
                        nc.scalar.copy(dst[:, :, 0:HD], bg_bank("V", i, n)[:, 0:D * (n + 1)].rearrange(
                            "p (h e) -> p h e", e=HD)).then_inc(bg_drained[BG["V", i, n]], 1)
                elif stage == "Sa":
                    for g in range(3):
                        act.wait_ge(max_ready, it * 3 * T + (3 * i + g + 1))
                        b = bg_bank("Sa", i, g)
                        for j in range(4):
                            ins = nc.scalar.activation(pr[:, g, j, :], b[:, j * P:(j + 1) * P], ACT.Exp,
                                                       bias=nmax[:, g, j:j + 1])
                        ins.then_inc(bg_drained[BG["Sa", i, g]], 1)
                elif stage in ("Sp", "Sq"):
                    for g in range(TR_FILLS[stage]):
                        wait_tr_full(act, it, stage, i, g)
                        nc.scalar.copy(prT[:, g], tr_bank(stage, i, g)[:, :].rearrange(
                            "p (j q) -> p j q", j=4)).then_inc(tr_drained[TR[stage, i, g]], 1)
                elif stage == "La" and i < T - 1:
                    wait_tr_full(act, it, "La", i, 0)
                    nc.scalar.copy(k2m[:], tr_bank("La", i, 0)[:, 0:D].rearrange("p (c f) -> p c f", c=2),
                                   ).then_inc(tr_drained[TR["La", i, 0]], 1)
                elif stage == "Oa":
                    wait_tr_full(act, it, "Oa", i, 0)
                    nc.scalar.copy(aosoT[0:C], tr_bank("Oa", i, 0)[0:C, :].rearrange("p (j q) -> p j q", j=4),
                                   ).then_inc(tr_drained[TR["Oa", i, 0]], 1)
                elif stage == "Od":
                    wait_tr_full(act, it, "Od", i, 0)
                    nc.scalar.copy(sT[0:C], tr_bank("Od", i, 0)[0:C, 0:2 * P].rearrange(
                        "p (c q) -> p c q", c=2)).then_inc(tr_drained[TR["Od", i, 0]], 1)
                elif stage == "Of":
                    wait_tr_full(act, it, "Of", i, 0)
                    j = (i % HT) * P
                    for c in range(2):
                        ins = nc.scalar.activation(hT[0:C, c, j:j + P], tr_bank("Of", i, 0)[0:C, c * P:(c + 1) * P],
                                                   ACT.Identity, bias=colt[:, 6 + c:7 + c],
                                                   scale=colt[:, 4 + c:5 + c])
                    ins.then_inc(tr_drained[TR["Of", i, 0]], 1)
                elif stage == "M":
                    for m in range(FF // P):
                        wait_bg_full(act, it, "M", i, m)
                        nc.scalar.activation(gT[:, m, :], bg_bank("M", i, m)[:, :], ACT.Gelu,
                                             ).then_inc(bg_drained[BG["M", i, m]], 1)
                elif stage == "Rc":
                    for t in range(HT):
                        wait_tr_full(act, it, "Rc", i, t)
                        j = (i * HT + t) * P
                        nc.scalar.copy(hlT[:, :, j:j + P], tr_bank("Rc", i, t)[0:C, 0:2 * P].rearrange(
                            "p (c q) -> p c q", c=2)).then_inc(tr_drained[TR["Rc", i, t]], 1)
                elif stage == "T":
                    act.wait_ge(lmax_ready, it + 1)
                    nc.scalar.activation(pb[:], lg[:], ACT.Exp).then_inc(lexp_ready, 1)

        @block.vector
        def _(dve):
            for b in (xnT, kT):
                nc.vector.memset(b[0:C, :, 0:WIN], 0.0).then_inc(preset, 1)
            for b in (xnT, aosoT, sT, hT):
                nc.vector.memset(b[C:C + 1], 1.0).then_inc(preset, 1)
            nc.vector.memset(carry[:], 0.0).then_inc(preset, 1)
            dve.wait_ge(loaded, 16 * (N_LOADS - 1))
            dve.wait_ge(preset, N_PRESET)
            caus3 = cst[:, C_CAUS:C_CAUS + P].unsqueeze(1).to_broadcast([P, 3, P])
            smask = cst[0:C, C_SM:C_SM + HC * V1].unsqueeze(1).to_broadcast([C, 2, HC * V1])
            tie8 = cst[:, C_TIE:C_TIE + NE].unsqueeze(1).to_broadcast([P, T, NE])
            ecap8 = cst[:, C_ECAP:C_ECAP + NE].unsqueeze(1).to_broadcast([P, T, NE])

            def each8(ap):
                return ap.unsqueeze(2).to_broadcast([P, T, NE])

            dve.sem_inc(r_ready, 1)
            dve.sem_inc(hb_stored, 16)
            step = [0, 0]

            def mark(ins):
                step[0] += 1
                step[1] += it.reg is not None
                ins.then_inc(dve_step, 1)

            def settle():
                dve.wait_ge(dve_step, it.steps(step[0], DVE_PER))

            def link(ins):
                mark(ins)
                settle()

            def moments(dst, srcs, st):
                for t, src in enumerate(srcs):
                    mark(nc.vector.bn_stats(st[:, t, :], src))
                settle()
                dve.sem_inc(passed, 1)
                for t in range(len(srcs)):
                    ins = nc.vector.bn_aggr(dst[:, t, :], st[:, t, :])
                return ins

            def normalise(dst, src, mean, rstd):
                return nc.vector.tensor_scalar(dst, src, mean, rstd, ALU.subtract, ALU.mult)

            tt, ts, red = nc.vector.tensor_tensor, nc.vector.tensor_scalar, nc.vector.tensor_reduce

            def largest(m, oh):
                link(red(r1[:, m, :], pb[:], AX.X, ALU.max))
                link(tt(out=tmp8[:], in0=pb[:], in1=each8(r1[:, m, :]), op=ALU.is_equal))
                link(tt(out=tmp8[:], in0=tmp8[:], in1=tie8, op=ALU.mult))
                link(red(r1[:, 3, :], tmp8[:], AX.X, ALU.max))
                link(tt(out=oh[:], in0=tmp8[:], in1=each8(r1[:, 3, :]), op=ALU.is_equal))

            for stage, i, it in traverse(dve, NBATCH):
                h = i // HT
                if stage == "Fa":
                    for t in range(HT):
                        dve.wait_ge(emb_in[HT * i + t], it * 16 + 16)
                    moments(mv, [emb[:, HT * i + t, :] for t in range(HT)], st[:, 0]).then_inc(e_var, 1)
                elif stage == "Fb":
                    dve.wait_ge(e_rstd, it * 2 + (i + 1))
                    for t in range(HT):
                        k = HT * i + t
                        mark(normalise(xb[:, k, :], emb[:, k, :], mv[:, t, 0:1], rs[:, t:t + 1]))
                    settle()
                    moments(mv2, [xb[:, HT * i + t, :] for t in range(HT)], st[:, 0]).then_inc(x_var, 1)
                elif stage == "Fc":
                    dve.wait_ge(x_rstd, it * 2 + (i + 1))
                    if i:
                        wait_tr_full(dve, it, "Fc", 0, 1)
                    elif not it.zeroth():
                        wait_tr_full(dve, it.prev(), "Fc", 1, 1)
                    for t in range(HT):
                        normalise(xh[:, t, :], xb[:, HT * i + t, :], mv2[:, t, 0:1], rs2[:, t:t + 1],
                                  ).then_inc(xh_ready, 1)
                elif stage == "P":
                    for c in range(2):
                        wait_bg_full(dve, it, "P", i, 2 + c)
                        nc.vector.tensor_copy(kT[:, c, WIN + i * HALF:WIN + (i + 1) * HALF],
                                              bg_bank("P", i, 2 + c)[0:C, :],
                                              ).then_inc(bg_drained[BG["P", i, 2 + c]], 1)
                    for n in range(4, 8):
                        dve.wait_ge(exp_ready, it * 8 + (4 * i + n - 3))
                        link(nc.vector.tensor_scalar(rl[:, n % 2], bg_bank("P", i, n)[0:C, :], 1e-4, 1e-4,
                                                     ALU.add, ALU.max))
                        dst = (q2T if n < 6 else k2T)[:, i, n % 2, :]
                        nc.vector.scalar_tensor_tensor(dst, ex[:, n % 2, :], 1.0, rl[:, n % 2], ALU.min, ALU.add,
                                                       ).then_inc(bg_drained[BG["P", i, n]], 1)
                elif stage == "Sa":
                    for g in range(3):
                        wait_bg_full(dve, it, "Sa", i, g)
                        nc.vector.tensor_reduce(nmax[:, g, :], bg_bank("Sa", i, g)[:, :].rearrange(
                            "p (j k) -> p j k", j=4), AX.X, ALU.max, negate=True).then_inc(max_ready, 1)
                elif stage == "La":
                    for g in range(4):
                        wait_bg_full(dve, it, "La", i, g)
                        nc.vector.tensor_tensor(out=at[:, g], in0=bg_bank("La", i, g)[:, 0:3 * P].rearrange(
                            "p (j q) -> p j q", j=3), in1=caus3, op=ALU.mult,
                        ).then_inc(bg_drained[BG["La", i, g]], 1)
                elif stage == "Sr":
                    dve.wait_ge(ao_full, it * T + (i + 1))
                    acc = ao_ps[:, 0:NH * V1].rearrange("p (h e) -> p h e", e=V1)
                    link(nc.vector.reciprocal(rec[:, 0, :], acc[:, :, HD]))
                    nc.vector.tensor_tensor(out=aoso[:, 0, :].rearrange("p (h e) -> p h e", e=HD),
                                            in0=acc[:, :, 0:HD],
                                            in1=rec[:, 0, :].unsqueeze(2).to_broadcast([P, NH, HD]),
                                            op=ALU.mult).then_inc(ao_ready, 1)
                elif stage == "Lb":
                    if i < T - 1:
                        wait_bg_full(dve, it, "Lb", i, 0)
                        new = bg_bank("Lb", i, 0)[0:C, 0:2 * HC * V1].rearrange("p (c n) -> p c n", c=2)
                        if i == 0:
                            ins = nc.vector.tensor_copy(state[:], new)
                        else:
                            ins = nc.vector.tensor_tensor(out=state[:], in0=new, in1=state[:], op=ALU.add)
                        ins.then_inc(bg_drained[BG["Lb", i, 0]], 1)
                        wait_bg_drained(dve, it, "Lb", i, 0)
                        nc.vector.tensor_tensor(out=stated[:], in0=state[:], in1=smask,
                                                op=ALU.mult).then_inc(state_ready, 1)
                    dve.wait_ge(nu_full, it * T + (i + 1))
                    acc = nu_ps[:, 0:NH * V1].rearrange("p (h e) -> p h e", e=V1)
                    link(nc.vector.tensor_scalar_add(rec[:, 1, :], acc[:, :, HD], 1e-4 * HD ** 0.5))
                    link(nc.vector.reciprocal(rec[:, 1, :], rec[:, 1, :]))
                    nc.vector.tensor_tensor(out=aoso[:, 1, :].rearrange("p (h e) -> p h e", e=HD),
                                            in0=acc[:, :, 0:HD],
                                            in1=rec[:, 1, :].unsqueeze(2).to_broadcast([P, NH, HD]),
                                            op=ALU.mult).then_inc(so_ready, 1)
                elif stage == "Ob":
                    wait_op_full(dve, it, "Ob", i, 0)
                    link(nc.vector.bn_stats(sto[:, 0, :], op_ps[:, D:2 * D]))
                    dve.sem_inc(passed, 1)
                    nc.vector.bn_aggr(mo[:, 0, :], sto[:, 0, :]).then_inc(so_var, 1)
                elif stage == "Oc":
                    dve.wait_ge(so_rstd, it * T + (i + 1))
                    normalise(sh[:], op_ps[:, D:2 * D], mo[:, 0, 0:1], rso[:, 0:1]).then_inc(sh_ready, 1)
                elif stage == "Os":
                    dve.wait_ge(shg_ready, it * T + (i + 1))
                    nc.vector.tensor_tensor(out=ssum[:], in0=op_ps[:, 0:D], in1=sh[:], op=ALU.add,
                                            ).then_inc(op_drained, 1)
                elif stage == "Oe":
                    wait_op_full(dve, it, "Oe", i, 0)
                    dve.wait_ge(r_ready, it * T + (i + 1))
                    nc.vector.tensor_tensor(out=x2[:], in0=op_ps[:, 0:D], in1=xb[:, i, :], op=ALU.add,
                                            ).then_inc(op_drained, 1)
                    wait_op_drained(dve, it, "Oe", i, 0)
                    link(nc.vector.bn_stats(sto[:, 1, :], x2[:]))
                    dve.sem_inc(passed, 1)
                    nc.vector.bn_aggr(mo[:, 1, :], sto[:, 1, :]).then_inc(x2_var, 1)
                elif stage == "On":
                    dve.wait_ge(x2_rstd, it * T + (i + 1))
                    normalise(hh[:], x2[:], mo[:, 1, 0:1], rso[:, 1:2]).then_inc(hh_ready, 1)
                elif stage == "M":
                    dve.wait_ge(hb_stored, it * 32 + 16 * (i + 1))
                    for t in range(HT):
                        wait_bg_full(dve, it, "M", i, FF // P + t)
                        dve.wait_ge(r_ready, it * T + (HT * i + t + 2))
                        nc.vector.tensor_tensor(out=h1[:, t, 0, :], in0=bg_bank("M", i, FF // P + t)[:, 0:D],
                                                in1=ebt[:, HT * i + t, :], op=ALU.add,
                                                ).then_inc(bg_drained[BG["M", i, FF // P + t]], 1)
                elif stage == "Ra":
                    for t in range(HT - 3, HT):
                        wait_bg_drained(dve, it, "M", i, FF // P + t)
                    moments(mr, [h1[:, t, 0, :] for t in range(HT)], st[:, 1]).then_inc(h_var, 1)
                elif stage == "Rb":
                    dve.wait_ge(h_rstd, it * 2 + (i + 1))
                    for t in range(HT):
                        normalise(h1[:, t, 1, :], h1[:, t, 0, :], mr[:, t, 0:1], rr[:, 0, t:t + 1],
                                  ).then_inc(hl_ready, 1)
                    dve.wait_ge(hl_ready, it * T + HT * (i + 1))
                    if i == 0:
                        dve.wait_ge(scattered, it * 16 * 2 * T + 16)
                    for t in range(HT):
                        ins = nc.vector.scalar_tensor_tensor(
                            zn[:, HT * i + t, :], h1[:, t, 1, :], 4.0 / D, h1[:, t, 1, :], ALU.mult, ALU.mult,
                            accum_out=msq[:, t:t + 1])
                    ins.then_inc(z_sq, 1)
                elif stage == "Rc":
                    dve.wait_ge(z_rstd, it * 2 + (i + 1))
                    for t in range(HT):
                        mark(nc.vector.tensor_scalar(zn[:, HT * i + t, :], h1[:, t, 1, :], rr[:, 1, t:t + 1], 2.0,
                                                     ALU.mult, ALU.mult))
                elif stage == "T":
                    wait_tr_full(dve, it, "T", 0, 0)
                    lps = tr_bank("T", 0, 0)[:, 0:T * NE].rearrange("p (t e) -> p t e", e=NE)
                    nc.vector.tensor_copy(tmp8[:], lps).then_inc(tr_drained[TR["T", 0, 0]], 1)
                    wait_tr_drained(dve, it, "T", 0, 0)
                    link(red(r1[:, 0, :], tmp8[:], AX.X, ALU.max))
                    tt(out=lg[:], in0=tmp8[:], in1=each8(r1[:, 0, :]), op=ALU.subtract).then_inc(lmax_ready, 1)
                elif stage == "Tb":
                    dve.wait_ge(lexp_ready, it + 1)
                    link(red(r1[:, 0, :], pb[:], AX.X, ALU.add))
                    link(nc.vector.reciprocal(r1[:, 0, :], r1[:, 0, :]))
                    link(tt(out=pb[:], in0=pb[:], in1=each8(r1[:, 0, :]), op=ALU.mult))
                    largest(1, oh1)
                elif stage == "Tc":
                    link(nc.vector.scalar_tensor_tensor(pb[:], oh1[:], -2.0, pb[:], ALU.mult, ALU.add))
                    largest(2, oh2)
                    tt(out=tmp8[:], in0=oh1[:], in1=oh2[:], op=ALU.add).then_inc(cnt_ready, 1)
                    link(tt(out=r1[:, 0, :], in0=r1[:, 1, :], in1=r1[:, 2, :], op=ALU.add))
                    link(nc.vector.reciprocal(r1[:, 0, :], r1[:, 0, :]))
                    for k in range(2):
                        mark(tt(out=wk[:, :, k], in0=r1[:, 1 + k, :], in1=r1[:, 0, :], op=ALU.mult))
                elif stage == "Td":
                    wait_bg_full(dve, it, "Td", 0, 0)
                    cps = bg_bank("Td", 0, 0)
                    link(tt(out=pos[:], in0=cps[:, 0:T * NE].rearrange("p (t e) -> p t e", e=NE),
                            in1=carry[:].unsqueeze(1).to_broadcast([P, T, NE]), op=ALU.add))
                    tt(out=carry[:], in0=cps[:, T * NE:(T + 1) * NE], in1=carry[:], op=ALU.add,
                       ).then_inc(bg_drained[BG["Td", 0, 0]], 1)
                    wait_bg_drained(dve, it, "Td", 0, 0)
                    for k, oh in enumerate((oh1, oh2)):
                        link(tt(out=tmp8[:], in0=pos[:], in1=oh[:], op=ALU.mult))
                        link(red(pk[:, :, k], tmp8[:], AX.X, ALU.add))
                        link(tt(out=tmp8[:], in0=oh[:], in1=ecap8, op=ALU.mult))
                        link(red(ek[:, :, k], tmp8[:], AX.X, ALU.add))
                elif stage == "Te":
                    link(ts(keep[:], pk[:], float(CAP), None, ALU.is_lt))
                    link(tt(out=slot[:], in0=ek[:], in1=pk[:], op=ALU.add))
                    link(tt(out=slot[:], in0=slot[:], in1=spill[:], op=ALU.subtract))
                    link(tt(out=slot[:], in0=slot[:], in1=keep[:], op=ALU.mult))
                    link(tt(out=slot[:], in0=slot[:], in1=spill[:], op=ALU.add))
                    nc.vector.tensor_copy(sidx[:], slot[:]).then_inc(sidx_ready, 1)
                    link(ts(pk[:], pk[:], float(CAP - 1), None, ALU.min))
                    link(tt(out=pk[:], in0=pk[:], in1=ek[:], op=ALU.add))
                    mark(nc.vector.tensor_copy(gidx[:, bass.ds(it * T + 0, T), :], pk[:]))
                    mark(tt(out=cw[:, bass.ds(it * T + 0, T), :], in0=wk[:], in1=keep[:], op=ALU.mult))
                    link(nc.vector.tensor_scalar_add(spill[:], spill[:], float(2 * SEQ)))
            assert step[1] == DVE_PER, step

        @block.tensor
        def _(pe):
            mm, tp = nc.tensor.matmul, nc.tensor.transpose
            pe.wait_ge(loaded, 16 * N_LOADS)
            pe.wait_ge(preset, N_PRESET)
            ident_c = cst[0:C, C_ID:C_ID + C]
            for s in (*tr_drained, *bg_drained, op_drained, ao_ready, so_ready):
                pe.sem_inc(s, 1)
            def exp_transposes(stage, i, n, g):
                wait_bg_drained(pe, it, "Sa", i, g)
                wait_tr_free(pe, it, stage, i, n)
                for j in range(4):
                    ins = tp(tr_bank(stage, i, n)[:, j * P:(j + 1) * P], pr[:, g, j, :], ident)
                ins.then_inc(tr_full[TR[stage, i, n]], 1)

            def window_products(stage, i, n, g):
                wait_tr_drained(pe, it, stage, i, n)
                for j in range(4):
                    hd = 4 * g + j
                    for a, v in enumerate((va, vb)):
                        r = a * WIN
                        ins = mm(ao_ps[r:r + WIN, hd * V1:(hd + 1) * V1], prT[:, n, j, r:r + WIN],
                                 v[:, hd, :], start=True, stop=True, skip_group_check=True)
                return ins

            for stage, i, it in traverse(pe, NBATCH):
                h, j = i // HT, (i % HT) * P
                if stage == "Fc":
                    pe.wait_ge(xh_ready, it * T + HT * (i + 1))
                    for c in range(2):
                        wait_tr_free(pe, it, "Fc", i, c)
                        for t in range(HT):
                            ins = tp(tr_bank("Fc", i, c)[0:C, t * P:(t + 1) * P], xh[:, t, c * C:(c + 1) * C], ident)
                        ins.then_inc(tr_full[TR["Fc", i, c]], 1)
                elif stage == "P":
                    wait_tr_drained(pe, it, "Fc", i, 1)
                    for n in range(8):
                        wait_bg_free(pe, it, "P", i, n)
                        for c in range(2):
                            ins = mm(bg_bank("P", i, n)[0:C, :], wqk_s[0:C + c, c, n * C:(n + 1) * C],
                                     xnT[0:C + c, c, WIN + i * HALF:WIN + (i + 1) * HALF],
                                     start=(c == 0), stop=(c == 1))
                        ins.then_inc(bg_full[BG["P", i, n]], 1)
                elif stage == "V":
                    for n in range(2):
                        wait_bg_free(pe, it, "V", i, n)
                        s0 = i * P + n * WIN
                        for c in range(2):
                            ins = mm(bg_bank("V", i, n)[:, 0:D * (n + 1)], xnT[0:C + c, c, s0:s0 + P],
                                     wv_s[0:C + c, c, 0:D * (n + 1)], start=(c == 0), stop=(c == 1))
                        ins.then_inc(bg_full[BG["V", i, n]], 1)
                elif stage == "Sa":
                    for g in range(3):
                        wait_bg_free(pe, it, "Sa", i, g)
                        b = bg_bank("Sa", i, g)
                        mm(b[:, :], identb[:], wmask[:, min(i, 1)].rearrange("p j k -> p (j k)"),
                           start=True, stop=False, skip_group_check=True)
                        if g == 0:
                            pe.wait_ge(qm_ready, it * 2 * T + 2 * (i + 1))
                            if i % HT == 0:
                                wait_bg_drained(pe, it, "P", h, 3)
                        for n in range(4):
                            c, hd = divmod(4 * g + n, HC)
                            for a in range(2):
                                r = a * WIN
                                ins = mm(b[r:r + WIN, n * P:(n + 1) * P], qm[:, c, hd, r:r + WIN],
                                         kT[:, c, i * P + r:i * P + r + P],
                                         start=False, stop=(n == 3), skip_group_check=True)
                        ins.then_inc(bg_full[BG["Sa", i, g]], 1)
                elif stage == "La":
                    pe.wait_ge(q2m_ready, it * 2 * T + 2 * (i + 1))
                    if i % HT == 0 and BG["P", h, 7] != BG["La", i, 0]:
                        wait_bg_drained(pe, it, "P", h, 7)
                    for g in range(4):
                        wait_bg_free(pe, it, "La", i, g)
                        c, hd = divmod(3 * g, HC)
                        mm(bg_bank("La", i, g)[:, 0:3 * P], k2T[:, h, c, j:j + P],
                           q2m[:, c, hd:hd + 3, :].rearrange("p j q -> p (j q)"),
                           start=True, stop=True).then_inc(bg_full[BG["La", i, g]], 1)
                    if i < T - 1:
                        wait_tr_free(pe, it, "La", i, 0)
                        for c in range(2):
                            ins = tp(tr_bank("La", i, 0)[:, c * C:(c + 1) * C], k2T[:, h, c, j:j + P], ident_c)
                        ins.then_inc(tr_full[TR["La", i, 0]], 1)
                elif stage == "Sp":
                    for g in range(2):
                        exp_transposes("Sp", i, g, g)
                elif stage == "Sq":
                    pe.wait_ge(ao_ready, it * T + (i + 1))
                    wait_bg_drained(pe, it, "V", i, 1)
                    window_products("Sp", i, 0, 0)
                    exp_transposes("Sq", i, 0, 2)
                    window_products("Sp", i, 1, 1)
                elif stage == "Sr":
                    window_products("Sq", i, 0, 2).then_inc(ao_full, 1)
                elif stage == "Lb":
                    pe.wait_ge(so_ready, it * T + (i + 1))
                    if i:
                        pe.wait_ge(state_ready, it * (T - 1) + i)
                        for c in range(2):
                            mm(nu_ps[:, c * HC * V1:(c + 1) * HC * V1], q2T[:, h, c, j:j + P], stated[:, c, :],
                               start=(c == 0), stop=False, skip_group_check=True)
                    wait_bg_drained(pe, it, "La", i, 3)
                    for hd in range(NH):
                        for r in (0, WIN):
                            ins = mm(nu_ps[r:r + WIN, hd * V1:(hd + 1) * V1], at[:, hd // 3, hd % 3, r:r + WIN],
                                     vb[:, NH + hd, :], start=(i == 0 and hd == 0), stop=(hd == NH - 1),
                                     skip_group_check=True)
                    ins.then_inc(nu_full, 1)
                    if i < T - 1:
                        wait_tr_drained(pe, it, "La", i, 0)
                        wait_bg_free(pe, it, "Lb", i, 0)
                        for c in range(2):
                            ins = mm(bg_bank("Lb", i, 0)[0:C, c * HC * V1:(c + 1) * HC * V1], k2m[:, c, :],
                                     vb[:, NH + c * HC:NH + (c + 1) * HC, :].rearrange("p h e -> p (h e)"),
                                     start=True, stop=True, skip_group_check=True)
                        ins.then_inc(bg_full[BG["Lb", i, 0]], 1)
                elif stage == "Oa":
                    pe.wait_ge(ao_ready, it * T + (i + 2))
                    pe.wait_ge(so_ready, it * T + (i + 2))
                    wait_tr_free(pe, it, "Oa", i, 0)
                    for n in range(4):
                        ins = tp(tr_bank("Oa", i, 0)[0:C, n * P:(n + 1) * P],
                                 aoso[:, n // 2, (n % 2) * C:(n % 2 + 1) * C], ident)
                    ins.then_inc(tr_full[TR["Oa", i, 0]], 1)
                elif stage == "Ob":
                    wait_tr_drained(pe, it, "Oa", i, 0)
                    wait_op_free(pe, it, "Ob", i, 0)
                    for n, w in enumerate((wp_s, ws_s)):
                        for c in range(2):
                            ins = mm(op_ps[:, n * D:(n + 1) * D], aosoT[0:C + c, 2 * n + c, :], w[0:C + c, c, :],
                                     start=(c == 0), stop=(c == 1), skip_group_check=True)
                    ins.then_inc(op_full, 1)
                elif stage == "Od":
                    wait_op_drained(pe, it, "Ob", i, 0)
                    wait_tr_free(pe, it, "Od", i, 0)
                    for c in range(2):
                        ins = tp(tr_bank("Od", i, 0)[0:C, c * P:(c + 1) * P], ssum[:, c * C:(c + 1) * C], ident)
                    ins.then_inc(tr_full[TR["Od", i, 0]], 1)
                elif stage == "Oe":
                    wait_tr_drained(pe, it, "Od", i, 0)
                    wait_op_free(pe, it, "Oe", i, 0)
                    for c in range(2):
                        ins = mm(op_ps[:, 0:D], sT[0:C + c, c, :], wo_s[0:C + c, c, :],
                                 start=(c == 0), stop=(c == 1))
                    ins.then_inc(op_full, 1)
                elif stage == "Of":
                    pe.wait_ge(hh_ready, it * T + (i + 1))
                    wait_tr_free(pe, it, "Of", i, 0)
                    for c in range(2):
                        ins = tp(tr_bank("Of", i, 0)[0:C, c * P:(c + 1) * P], hh[:, c * C:(c + 1) * C], ident)
                    ins.then_inc(tr_full[TR["Of", i, 0]], 1)
                elif stage == "M":
                    wait_tr_drained(pe, it, "Of", HT * i + HT - 1, 0)
                    for m in range(FF // P):
                        wait_bg_free(pe, it, "M", i, m)
                        for c in range(2):
                            ins = mm(bg_bank("M", i, m)[:, :], w1_s[0:C + c, c, m * P:(m + 1) * P], hT[0:C + c, c, :],
                                     start=(c == 0), stop=(c == 1))
                        ins.then_inc(bg_full[BG["M", i, m]], 1)
                    for t in range(HT):
                        n = FF // P + t
                        wait_bg_free(pe, it, "M", i, n)
                        for m in range(FF // P):
                            if t == 0:
                                wait_bg_drained(pe, it, "M", i, m)
                            ins = mm(bg_bank("M", i, n)[:, 0:D], gT[:, m, t * P:(t + 1) * P], w2_s[:, m, :],
                                     start=(m == 0), stop=(m == FF // P - 1))
                        ins.then_inc(bg_full[BG["M", i, n]], 1)
                elif stage == "Rc":
                    pe.wait_ge(hl_ready, it * T + HT * (i + 1))
                    for t in range(HT):
                        wait_tr_free(pe, it, "Rc", i, t)
                        for c in range(2):
                            ins = tp(tr_bank("Rc", i, t)[0:C, c * P:(c + 1) * P], h1[:, t, 1, c * C:(c + 1) * C], ident)
                        ins.then_inc(tr_full[TR["Rc", i, t]], 1)
                elif stage == "T":
                    wait_tr_drained(pe, it, "Rc", 1, HT - 1)
                    wait_tr_free(pe, it, "T", 0, 0)
                    for t in range(T):
                        for c in range(2):
                            ins = mm(tr_bank("T", 0, 0)[:, t * NE:(t + 1) * NE], hlT[:, c, t * P:(t + 1) * P],
                                     gate_s[:, c, :], start=(c == 0), stop=(c == 1), skip_group_check=True)
                    ins.then_inc(tr_full[TR["T", 0, 0]], 1)
                elif stage == "Td":
                    pe.wait_ge(cnt_ready, it + 1)
                    wait_bg_free(pe, it, "Td", 0, 0)
                    b = bg_bank("Td", 0, 0)
                    up, one = cst[:, C_UP:C_UP + P], cst[:, C_ONE:C_ONE + P]
                    mm(b[:, 0:T * NE], up, tmp8[:].rearrange("p t e -> p (t e)"),
                       start=True, stop=False, skip_group_check=True)
                    for t in range(T):
                        n = T - 1 - t
                        if n:
                            mm(b[:, (t + 1) * NE:T * NE].rearrange("p (t e) -> p t e", e=NE), one,
                               tmp8[:, t, :].unsqueeze(1).to_broadcast([P, n, NE]),
                               start=False, stop=False, skip_group_check=True)
                        ins = mm(b[:, T * NE:(T + 1) * NE], one, tmp8[:, t, :],
                                 start=False, stop=(t == T - 1), skip_group_check=True)
                    ins.then_inc(bg_full[BG["Td", 0, 0]], 1)


def phase_b(nc, w13, w2e, nw, consts, zbuf, ybuf, NPAIR):
    with ExitStack() as cb:
        def sa(name, shape, dt=F32):
            return cb.enter_context(nc.sbuf_tensor(name, shape, dt))

        def sem(name):
            return cb.enter_context(nc.semaphore(name))

        NBK = 2 * NBLK
        MG = EH // P
        CUT = float(2 ** 13)
        PARTS = 5
        idb = sa("idb", [P, P])
        w13_in = sa("w13_in", [P, 2, 2 * EH])
        w_up, w_sum = sa("w_up", [P, 2, 2 * EH]), sa("w_sum", [P, 2, 2 * EH])
        w_hi = sa("w_hi", [P, 2, 2, 2 * EH], F32R)
        w_lo = sa("w_lo", [P, 2, 2, 2 * EH], F32R)
        w2_s = sa("w2e_s", [P, 2, EH // P, D])
        nw_s = sa("nw_s", [P, 2, 2])
        z = sa("z", [P, 2, BT, 2 * P])
        zT = sa("zT", [P, 2, 2, BLK])
        z_up = sa("z_up", [P, 2, BLK])
        z_hi = sa("z_hi", [P, 2, 2, BLK], F32R)
        z_lo = sa("z_lo", [P, 2, BLK], F32R)
        z_hl = sa("z_hl", [P, 2, BLK], F32R)
        sg = sa("sg", [P, 2, BLK])
        hm = sa("hm", [P, 2, EH // P, BLK])
        y = sa("y", [P, 2, BT, D])
        tr = [cb.enter_context(nc.psum_tensor(f"btr{i}", [P, 512], F32)) for i in range(2)]
        gu = [cb.enter_context(nc.psum_tensor(f"bgu{i}", [P, 512], F32)) for i in range(4)]
        yp = [cb.enter_context(nc.psum_tensor(f"byp{i}", [P, 512], F32)) for i in range(2)]
        id_in, raw_in, passed = sem("id_in"), sem("raw_in"), sem("passed_b")
        w_in = [sem(f"w_in{x}") for x in range(2)]
        z_in = [sem(f"z_in{b}") for b in range(2)]
        y_out = [sem(f"y_out{b}") for b in range(2)]
        t_full, zT_ready, z_up_ready, z_hi_ready, z_hl_ready, z_lo_ready = (
            sem("t_full"), sem("zT_ready"), sem("z_up_ready"), sem("z_hi_ready"), sem("z_hl_ready"), sem("z_lo_ready"))
        w_up_ready, w_hi_ready, w_ready = sem("w_up_ready"), sem("w_hi_ready"), sem("w_ready")
        g_full, silu_ready, hm_ready, y_full, y_ready = (
            sem("g_full"), sem("silu_ready"), sem("hm_ready"), sem("y_full"), sem("y_ready"))
        T0, Y0 = 4, NBLK * BT + 1
        block = cb.enter_context(nc.Block())
        zv = zbuf[0:SLOTS, :].rearrange("(b s p) c -> b p s c", s=BT, p=P)
        yv = ybuf.rearrange("(b s p) c -> b p s c", s=BT, p=P)

        @block.sync
        def _(sp):
            sp.dma_start(idb[:], consts[:, C_ID:C_ID + P]).then_inc(id_in, 16)
            sp.sem_inc(y_full, Y0)
            sp.sem_inc(w_ready, 1)
            with sp.Fori(0, NPAIR) as it:
                def load_weights(x):
                    sp.wait_ge(w_ready, it * 2 + (x + 1))
                    sp.dma_start(w13_in[:], w13[bass.ds(it * 2 + x, 1)].rearrange("o p c f -> p (o c) f"),
                                 ).then_inc(raw_in, 16)
                    sp.wait_ge(y_full, it * (NBK * BT) + (1 if x == 0 else Y0))
                    sp.dma_start(w2_s[:, x], w2e[bass.ds(it * 2 + x, 1)].rearrange("o p c f -> p (o c) f"),
                                 ).then_inc(w_in[x], 16)
                    sp.dma_start(nw_s[:, x], nw[bass.ds(it * 2 + x, 1)].rearrange("o p c -> p (o c)"),
                                 ).then_inc(w_in[x], 16)

                load_weights(0)
                for b in range(NBK):
                    sp.wait_ge(t_full, it * (2 * NBK) + (2 * (b - 1) + T0))
                    rows = zv[bass.ds(it * NBK + b, 1)].rearrange("o p s c -> p (o s) c")
                    sp.dma_start(z[:, b % 2, :, 0:D], rows).then_inc(z_in[b % 2], 16)
                    sp.dma_start(z[:, b % 2, :, D:2 * P], rows[:, :, P:D]).then_inc(z_in[b % 2], 16)
                    if b == 1:
                        load_weights(1)

        @block.gpsimd
        def _(pool):
            with pool.Fori(0, NPAIR) as it:
                def cut_weights(x):
                    pool.wait_ge(z_lo_ready, it * (2 * NBK) + (4 * x + 1))
                    pool.wait_ge(raw_in, it * 32 + 16 * (x + 1))
                    pool.wait_ge(y_full, it * (NBK * BT) + (1 if x == 0 else Y0))
                    pool.sem_inc(passed, 1)
                    nc.gpsimd.tensor_scalar(w_up[:], w13_in[:], CUT, None, ALU.mult).then_inc(w_up_ready, 1)
                    pool.wait_ge(w_up_ready, it * 6 + (3 * x + 1))
                    nc.gpsimd.tensor_tensor(out=w_sum[:], in0=w13_in[:], in1=w_up[:], op=ALU.add).then_inc(w_up_ready, 1)
                    pool.wait_ge(w_up_ready, it * 6 + (3 * x + 2))
                    nc.gpsimd.tensor_tensor(out=w_hi[:, x], in0=w_sum[:], in1=w_up[:], op=ALU.subtract).then_inc(w_up_ready, 1)
                    pool.wait_ge(w_up_ready, it * 6 + (3 * x + 3))
                    nc.gpsimd.tensor_tensor(out=w_lo[:, x], in0=w13_in[:], in1=w_hi[:, x], op=ALU.subtract).then_inc(w_ready, 1)

                cut_weights(0)
                for b in range(NBK):
                    for c, r, dst in ((0, 0, z_lo), (1, P // 2, z_hl)):
                        pool.wait_ge(z_lo_ready, it * (2 * NBK) + (2 * b + c + 1))
                        pool.wait_ge(z_hi_ready, it * (2 * NBK) + (2 * b + c + 1))
                        nc.gpsimd.tensor_tensor(out=dst[r:P, b % 2, :], in0=zT[r:P, b % 2, c, :],
                                                in1=z_hi[r:P, b % 2, c, :], op=ALU.subtract).then_inc(z_lo_ready, 1)
                    if b == 1:
                        cut_weights(1)

        @block.scalar
        def _(act):
            with act.Fori(0, NPAIR) as it:
                def store(b):
                    act.wait_ge(y_ready, it * (NBK * BT) + (BT * (b + 1) + 1))
                    act.dma_start(yv[bass.ds(it * NBK + b, 1)].rearrange("o p s c -> p (o s) c"), y[:, b % 2],
                                  ).then_inc(y_out[b % 2], 16)

                def rows_out(b):
                    x = b // NBLK
                    if b % NBLK == 0:
                        act.wait_ge(w_in[x], it * 32 + 32)
                    for c in range(2):
                        act.wait_ge(t_full, it * (2 * NBK) + (2 * b + c + 1 + T0))
                        nc.scalar.mul(zT[:, b % 2, c, :], tr[c][:, :], nw_s[:, x, c:c + 1]).then_inc(zT_ready, 1)
                    act.wait_ge(z_hi_ready, it * (2 * NBK) + (2 * b + 2))
                    nc.scalar.copy(z_hl[0:P // 2, b % 2, :], z_hi[0:P // 2, b % 2, 1, :]).then_inc(z_hl_ready, 1)

                for b in range(NBK):
                    if b == 0:
                        rows_out(0)
                    for m in range(MG):
                        k = b * MG + m
                        act.wait_ge(g_full, it * (NBK * MG) + (k + 1))
                        if k >= 2:
                            act.wait_ge(hm_ready, it * (NBK * MG) + k)
                        nc.scalar.activation(sg[:, k % 2, :], gu[2 * (k % 2)][:, :], ACT.Silu).then_inc(silu_ready, 1)
                        if m == 1 and b < NBK - 1:
                            rows_out(b + 1)
                    if b:
                        store(b - 1)
                store(NBK - 1)
            for b in range(2):
                act.wait_ge(y_out[b], 16 * NPAIR * NBLK + 16)

        @block.vector
        def _(dve):
            for b in range(2):
                dve.sem_inc(y_out[b], 16)
            with dve.Fori(0, NPAIR) as it:
                def cut_rows(b):
                    for c in range(2):
                        dve.wait_ge(zT_ready, it * (2 * NBK) + (2 * b + c + 2))
                        nc.vector.scalar_tensor_tensor(z_up[:, c, :], zT[:, b % 2, c, :], CUT, zT[:, b % 2, c, :],
                                                       ALU.mult, ALU.add).then_inc(z_up_ready, 1)
                    for c in range(2):
                        dve.wait_ge(z_up_ready, it * (2 * NBK) + (2 * b + c + 1))
                        nc.vector.scalar_tensor_tensor(z_hi[:, b % 2, c, :], zT[:, b % 2, c, :], -CUT, z_up[:, c, :],
                                                       ALU.mult, ALU.add).then_inc(z_hi_ready, 1)

                for b in range(NBK):
                    if b == 0:
                        cut_rows(0)
                    for m in range(MG):
                        k = b * MG + m
                        dve.wait_ge(silu_ready, it * (NBK * MG) + (k + 1))
                        nc.vector.tensor_tensor(out=hm[:, b % 2, m, :], in0=gu[2 * (k % 2) + 1][:, :],
                                                in1=sg[:, k % 2, :], op=ALU.mult).then_inc(hm_ready, 1)
                        if m == 1 and b < NBK - 1:
                            cut_rows(b + 1)
                    for s in range(BT):
                        k = b * BT + s
                        dve.wait_ge(y_full, it * (NBK * BT) + (k + 1 + Y0))
                        if s == 0:
                            dve.wait_ge(y_out[b % 2], it * (16 * NBLK) + 16 * (b // 2 + 1))
                        nc.vector.tensor_copy(y[:, b % 2, s, :], yp[k % 2][:, 0:D]).then_inc(y_ready, 1)

        @block.tensor
        def _(pe):
            pe.wait_ge(id_in, 16)
            for s in (zT_ready, y_ready, hm_ready, z_lo_ready):
                pe.sem_inc(s, 1)
            pe.sem_inc(t_full, T0)
            with pe.Fori(0, NPAIR) as it:
                def transposes(b):
                    pe.wait_ge(z_in[b % 2], it * (32 * NBLK) + 32 * (b // 2 + 1))
                    for c in range(2):
                        pe.wait_ge(zT_ready, it * (2 * NBK) + max(2 * b + c, 1))
                        for s in range(BT):
                            ins = nc.tensor.transpose(tr[c][:, s * P:(s + 1) * P],
                                                      z[:, b % 2, s, c * P:(c + 1) * P], idb[:])
                        ins.then_inc(t_full, 1)

                def down(b):
                    pe.wait_ge(hm_ready, it * (NBK * MG) + ((b + 1) * MG + 1))
                    for s in range(BT):
                        k = b * BT + s
                        pe.wait_ge(y_ready, it * (NBK * BT) + max(k, 1))
                        for m in range(MG):
                            ins = nc.tensor.matmul(yp[k % 2][:, 0:D], hm[:, b % 2, m, s * P:(s + 1) * P],
                                                   w2_s[:, b // NBLK, m, :], start=(m == 0), stop=(m == MG - 1))
                        ins.then_inc(y_full, 1)

                for b in range(NBK):
                    x = b // NBLK
                    if b == 0:
                        transposes(0)
                    else:
                        down(b - 1)
                    if b % NBLK == 0:
                        pe.wait_ge(w_in[x], it * 32 + 32)
                        pe.wait_ge(w_ready, it * 2 + (x + 2))
                    pe.wait_ge(z_hl_ready, it * NBK + (b + 1))
                    pe.wait_ge(z_lo_ready, it * (2 * NBK) + (2 * b + 3))
                    for m in range(MG):
                        k = b * MG + m
                        pe.wait_ge(hm_ready, it * (NBK * MG) + max(k, 1))
                        for u in range(2):
                            f = slice(u * EH + m * P, u * EH + (m + 1) * P)
                            parts = ((w_lo[:, x, 0, f], z_hi[:, b % 2, 0, :]), (w_hi[:, x, 0, f], z_hi[:, b % 2, 0, :]),
                                     (w_hi[:, x, 0, f], z_lo[:, b % 2, :]), (w_hi[:, x, 1, f], z_hl[:, b % 2, :]),
                                     (w_lo[:, x, 1, f], z_hl[:, b % 2, :]))
                            for n, (w, rows) in enumerate(parts):
                                ins = nc.tensor.matmul(gu[2 * (k % 2) + u][:, :], w, rows,
                                                       start=(n == 0), stop=(n == PARTS - 1))
                        ins.then_inc(g_full, 1)
                        if m == 1 and b < NBK - 1:
                            transposes(b + 1)
                down(NBK - 1)


def phase_c(nc, hbase, ybuf, out, gidx, cw, NT):
    with ExitStack() as cc:
        def sa(name, shape, dt=F32):
            return cc.enter_context(nc.sbuf_tensor(name, shape, dt))

        def sem(name):
            return cc.enter_context(nc.semaphore(name))

        U = 4
        passed = sem("passed")
        ix = sa("ix", [P, U, 2], I32)
        wt = sa("wt", [P, U, 3])
        hb = sa("hb", [P, U, 2, D])
        yg = sa("yg", [P, U, 2, D])
        o = sa("o", [P, U, 3, D])
        h_in = [sem(f"h_in{u}") for u in range(U)]
        y_in = [sem(f"y_in{u}") for u in range(U)]
        o_out = [sem(f"o_out{u}") for u in range(U)]
        ix_ready, w_ready, s_ready, o_ready, step = (
            sem("ix_ready"), sem("w_ready"), sem("s_ready"), sem("o_ready"), sem("c_step"))
        block = cc.enter_context(nc.Block())
        hv = hbase.rearrange("(t p) k c -> t p k c", p=P)
        ov = out.rearrange("(t p) c -> t p c", p=P)

        @block.sync
        def _(sp):
            with sp.Fori(0, NT // U) as it:
                for u in range(U):
                    sp.wait_ge(o_ready, it * U + 1)
                    sp.dma_start(hb[:, u], hv[bass.ds(it * U + u, 1)].rearrange("o p k c -> p (o k) c"),
                                 ).then_inc(h_in[u], 16)

        @block.gpsimd
        def _(pool):
            with pool.Fori(0, NT // U) as it:
                pool.wait_ge(o_ready, it * U + 1)
                nc.gpsimd.tensor_copy(ix[:], gidx[:, bass.ds(it * U, U), :]).then_inc(ix_ready, 1)
                pool.wait_ge(ix_ready, it + 1)
                pool.sem_inc(passed, 1)
                for u in range(U):
                    for k in range(2):
                        nc.gpsimd.indirect_dma_start(
                            out=yg[:, u, k, :], out_offset=None, in_=ybuf,
                            in_offset=bass.IndirectOffsetOnAxis(ap=ix[:, u, k:k + 1], axis=0),
                        ).then_inc(y_in[u], 16)

        @block.vector
        def _(dve):
            dve.sem_inc(o_ready, 1)
            for u in range(U):
                dve.sem_inc(o_out[u], 16)
            with dve.Fori(0, NT // U) as it:
                nc.vector.tensor_copy(wt[:, :, 0:2], cw[:, bass.ds(it * U, U), :]).then_inc(step, 1)
                dve.wait_ge(step, it * (3 * U + 2) + 1)
                nc.vector.tensor_tensor(out=wt[:, :, 2], in0=wt[:, :, 0], in1=wt[:, :, 1], op=ALU.add).then_inc(step, 1)
                dve.wait_ge(step, it * (3 * U + 2) + 2)
                for u in range(U):
                    dve.wait_ge(h_in[u], it * 16 + 16)
                    nc.vector.scalar_tensor_tensor(o[:, u, 0, :], hb[:, u, 1, :], wt[:, u, 2:3], hb[:, u, 0, :],
                                                   ALU.mult, ALU.add).then_inc(step, 1)
                dve.wait_ge(step, it * (3 * U + 2) + (U + 2))
                for k in range(2):
                    for u in range(U):
                        if k == 0:
                            dve.wait_ge(y_in[u], it * 32 + 32)
                        else:
                            dve.wait_ge(o_out[u], it * 16 + 16)
                        ins = nc.vector.scalar_tensor_tensor(o[:, u, k + 1, :], yg[:, u, k, :], wt[:, u, k:k + 1],
                                                             o[:, u, k, :], ALU.mult, ALU.add)
                        ins.then_inc(step if k == 0 else o_ready, 1)
                    if k == 0:
                        dve.wait_ge(step, it * (3 * U + 2) + (2 * U + 2))
                for u in range(U):
                    nc.vector.memset(wt[:, u, 2:3], 0.0).then_inc(step, 1)
                dve.wait_ge(step, it * (3 * U + 2) + (3 * U + 2))

        @block.scalar
        def _(act):
            with act.Fori(0, NT // U) as it:
                for u in range(U):
                    act.wait_ge(o_ready, it * U + (u + 2))
                    act.dma_start(ov[bass.ds(it * U + u, 1)].rearrange("o p c -> p (o c)"), o[:, u, 2, :],
                                  ).then_inc(o_out[u], 16)
            for u in range(U):
                act.wait_ge(o_out[u], 16 * (NT // U) + 16)


def lay_out(a):
    f = lambda n: np.asarray(a[n])
    g = lambda n: f("L0_attn_" + n)

    def with_bias(w, b):
        return np.ascontiguousarray(np.concatenate([w, b[None, :]], 0))

    qkv, qkv2 = (with_bias(g(n + "_w"), g(n + "_b")) for n in ("attn_qkv", "ssm_qkv"))
    two = lambda v: v.reshape(2, C).T

    def a_and_b(w):
        return np.stack([w[:, 0:P], np.concatenate([w[:, P:D], w[:, P:D]], 1)], 2)
    ins = {
        "ids": np.ascontiguousarray(f("x").reshape(NB * T, P).T),
        "table": f("L0_tok_embedding_lookup"),
        "consts": constants(),
        "cols": np.concatenate([two(g(n)) for n in ("ln1_g", "ln1_b", "lnm_g", "lnm_b")], 1),
        "rows3": np.broadcast_to(np.stack([g("ssm_ln_g"), g("ssm_ln_b"), g("mlp_b2")])[None], (P, 3, D)),
        "wqk": np.concatenate([qkv[:, 0:2 * D], qkv2[:, 0:2 * D]], 1),
        "wv": np.concatenate([qkv[:, 2 * D:], qkv2[:, 2 * D:]], 1),
        "wp": with_bias(g("attn_proj_w"), g("attn_proj_b")),
        "ws": with_bias(g("ssm_out_w"), g("ssm_out_b")),
        "wo": with_bias(g("out_w"), g("out_b")),
        "w1": with_bias(g("mlp_w1"), g("mlp_b1")),
        "w2": g("mlp_w2").reshape(FF // P, P, D).transpose(1, 0, 2),
        "gate": f("L0_ffn_gate_w").T.reshape(2, C, NE).transpose(1, 0, 2),
        "w13": a_and_b(f("L0_ffn_w13").transpose(0, 2, 1)),
        "w2e": f("L0_ffn_w2").transpose(0, 2, 1).reshape(NE, EH // P, P, D).transpose(0, 2, 1, 3),
        "nw": a_and_b(f("L0_ffn_norm_w")[:, :, None])[..., 0],
    }
    return {k: np.ascontiguousarray(v) for k, v in ins.items()}


def build(nc, ins, out, NBATCH=NB, NPAIR=NE // 2, NT=NB * T, phases="abc"):
    hbase = nc.dram_tensor("hbase", [NTOK, 2, D], F32).ap()
    zbuf = nc.dram_tensor("zbuf", [SLOTS + SPILL, D], F32).ap()
    ybuf = nc.dram_tensor("ybuf", [SLOTS, D], F32).ap()
    with nc.sbuf_tensor("gidx", [P, NB * T, 2], I32) as gidx, nc.sbuf_tensor("cw", [P, NB * T, 2], F32) as cw:
        phase_a(nc, ins["ids"], ins["table"], ins["consts"], ins["cols"], ins["rows3"], ins["wqk"], ins["wv"],
                ins["wp"], ins["ws"], ins["wo"], ins["w1"], ins["w2"], ins["gate"], hbase, zbuf, gidx, cw, NBATCH, None)
        if "b" in phases:
            phase_b(nc, ins["w13"], ins["w2e"], ins["nw"], ins["consts"], zbuf, ybuf, NPAIR)
        if "c" in phases:
            phase_c(nc, hbase, ybuf, out, gidx, cw, NT)


def kernel(**inputs):
    import concourse.bacc as bacc
    from concourse.bass_utils import run_bass_kernel_spmd

    arrays = lay_out(inputs)
    nc = bacc.Bacc("TRN2", target_bir_lowering=False, num_devices=1)
    ins = {k: nc.dram_tensor(k, v.shape, mybir.dt.from_np(v.dtype), kind="ExternalInput").ap()
           for k, v in arrays.items()}
    out = nc.dram_tensor("out", (NTOK, D), F32, kind="ExternalOutput").ap()
    build(nc, ins, out)
    r = run_bass_kernel_spmd(nc, [arrays], core_ids=[0])
    return r.results[0]["out"].reshape(NB, SEQ, D)
```

```python
from contextlib import ExitStack

import numpy as np

import concourse.bass as bass
from concourse import mybir

F32 = mybir.dt.float32
BF16 = mybir.dt.bfloat16
F32R = mybir.dt.float32r
I32 = mybir.dt.int32
ALU = mybir.AluOpType
ACT = mybir.ActivationFunctionType
AX = mybir.AxisListType

P = 128
D = 192
C = 96
NH, HD = 12, 16
HC = C // HD
V1 = HD + 1
WIN = 64
SEQ, NB = 1024, 8
T = SEQ // P
HT = T // 2
HALF = SEQ // 2
FF = 768
NE, EH = 8, 512
CAP = 2560
SLOTS = NE * CAP
NTOK = NB * SEQ
SPILL = 2 * NTOK
BLK = 512
NBLK = CAP // BLK
BT = BLK // P
VOCAB = 50257
MASKED = -30000.0

C_ID, C_WM0, C_WM1, C_CAUS, C_UP, C_ONE, C_HM, C_SM, C_TIE, C_ECAP, C_SP = np.cumsum(
    [0, P, P, P, P, P, P, HC, HC * V1, NE, NE]).tolist()
C_N = C_SP + 16


def constants():
    c = np.zeros((P, C_N), np.float32)
    p = np.arange(P)[:, None]
    f = np.arange(P)[None, :]
    c[:, C_ID:C_ID + P] = p == f
    i = p % WIN
    seen = (f > i) & (f <= i + WIN)
    c[:, C_WM1:C_WM1 + P] = np.where(seen, 0.0, MASKED)
    c[:, C_WM0:C_WM0 + P] = np.where(seen & ((f >= WIN) | (p >= WIN)), 0.0, MASKED)
    c[:, C_CAUS:C_CAUS + P] = p <= f
    c[:, C_UP:C_UP + P] = p < f
    c[:, C_ONE:C_ONE + P] = 1.0
    c[:, C_HM:C_HM + HC] = p // HD == np.arange(HC)[None, :]
    c[:, C_SM:C_SM + HC * V1] = p // HD == np.arange(HC * V1)[None, :] // V1
    c[:, C_TIE:C_TIE + NE] = NE - np.arange(NE)[None, :]
    c[:, C_ECAP:C_ECAP + NE] = CAP * np.arange(NE)[None, :]
    t, k = np.arange(16)[None, :] // 2, np.arange(16)[None, :] % 2
    c[:, C_SP:C_SP + 16] = SLOTS + (t * P + p) * 2 + k
    return c


STEP = (("Sa", 0), ("Oe", -2), ("Lb", -1), ("On", -2), ("La", 0), ("Of", -2), ("Oa", -1), ("Qm", 1), ("Sp", 0),
        ("Qn", 1), ("Ob", -1), ("Oc", -1), ("Os", -1), ("Sq", 0), ("V", 1), ("Sr", 0), ("Od", -1))
AFTER = {
    (1, "Sr"): [("M", 1, 1), ("Ra", 1, 1)],
    (1, "Od"): [("Fa", 1, 0)],
    (2, "Qn"): [("Rb", 1, 1)],
    (2, "Sr"): [("Fb", 1, 0), ("Fn", 1, 0), ("Fe", 1, 0), ("Fg", 1, 0), ("Rc", 1, 1)],
    (3, "Sa"): [("Fc", 1, 0)],
    (3, "Ob"): [("P", 1, 0)],
    (4, "Oe"): [("T", 0, 1)],
    (4, "Qn"): [("Tb", 0, 1)],
    (4, "Od"): [("Tc", 0, 1)],
    (5, "Sa"): [("Td", 0, 1)],
    (5, "La"): [("Te", 0, 1)],
    (5, "Sr"): [("M", 0, 0), ("Tf", 0, 1), ("Ra", 0, 0)],
    (5, "Od"): [("Fa", 0, -1)],
    (6, "Oc"): [("Rb", 0, 0)],
    (6, "V"): [("Fb", 0, -1), ("Fe", 0, -1), ("Fg", 0, -1)],
    (7, "Sa"): [("Fn", 0, -1), ("Fc", 0, -1)],
    (7, "On"): [("Rc", 0, 0)],
    (7, "Oa"): [("P", 0, -1)],
}
BODY = []
for _t in range(T):
    for _s, _d in STEP:
        BODY.append((_s, (_t + _d) % T, -((_t + _d) // T)))
        BODY += AFTER.get((_t, _s), [])
LAG = {(_s, _i): _lag for _s, _i, _lag in BODY}
BODIES = {-1: [x for x in BODY if x[2] == -1], 0: [x for x in BODY if x[2] <= 0], 1: BODY,
          2: [x for x in BODY if x[2] == 1]}

TR_FILLS = {"Fc": 2, "Sp": 2, "Sq": 1, "La": 1, "Oa": 1, "Od": 1, "Of": 1, "Rc": HT, "T": 1}
BG_FILLS = {"P": 8, "V": 1, "Sa": 3, "La": 4, "Lb": 1, "M": FF // P + HT, "Td": 1}
OP_FILLS = {"Ob": 1, "Oe": 1}


class Ring:

    def __init__(self, table, banks):
        def keys(body):
            for stage, i, _ in BODIES[body]:
                last = i == T - 1 and (stage == "Lb" or (stage == "La" and banks == 2))
                for j in range(0 if last else table.get(stage, 0)):
                    yield stage, i, j
        self.bank = {key: k % banks for k, key in enumerate(keys(1))}
        self.per = [list(self.bank.values()).count(b) for b in range(banks)]
        self.before, count = {}, [0] * banks
        for body in BODIES:
            for key in keys(body):
                self.before[body, key] = count[self.bank[key]]
                count[self.bank[key]] += 1

    def __getitem__(self, key):
        return self.bank[key]

    def fills(self, seq, key, n):
        per, body = self.per[self.bank[key]], seq.first + LAG[key[0], key[1]]
        if seq.reg is not None:
            return seq.reg * per + (self.before[1, key] + (body - 1) * per + n)
        if body < 1:
            return self.before[body, key] + n
        return self.before[2 if body == seq.total else 1, key] + (seq.total - 2) * per + n


class Seq:

    def __init__(self, reg, first, total, k=1, last=False):
        self.reg, self.first, self.total, self.k, self.last = reg, first, total, k, last

    def __mul__(self, k):
        return Seq(self.reg, self.first, self.total, self.k * k, self.last)

    def __add__(self, c):
        c += self.first * self.k
        return c if self.reg is None else self.reg * self.k + c

    def zeroth(self):
        return self.reg is None and self.first == 0

    def prev(self):
        return Seq(self.reg, self.first - 1, self.total)

    def steps(self, n, per):
        if self.reg is not None:
            return self.reg * per + n
        return n + (self.total - 2) * per if self.last else n


TR, BG, OP = Ring(TR_FILLS, 2), Ring(BG_FILLS, 3), Ring(OP_FILLS, 1)


def traverse(eng, nseq):
    for body in (-1, 0):
        for stage, i, lag in BODIES[body]:
            yield stage, i, Seq(None, body - lag, nseq)
    with eng.Fori(0, nseq - 1) as it:
        for stage, i, lag in BODIES[1]:
            yield stage, i, Seq(it, 1 - lag, nseq)
    for stage, i, lag in BODIES[2]:
        yield stage, i, Seq(None, nseq - lag, nseq, last=True)


N_TABLES = 5
N_ZERO = (SLOTS + BLK) // P // 4
N_WEIGHTS = 13
N_PRESET = 18
DVE_PER = 129
POOL_PER = 42


def phase_a(nc, ids, table, consts, cols, rows3, wqk, wv, wp, ws, wo, w1, w2, gate,
            hbase, zbuf, gidx, cw, NBATCH):
    with ExitStack() as ca:
        def sa(name, shape, dt=F32):
            return ca.enter_context(nc.sbuf_tensor(name, shape, dt))

        def sem(name):
            return ca.enter_context(nc.semaphore(name))

        cst = sa("cst", [P, C_N])
        ident = cst[:, C_ID:C_ID + P]
        identb = sa("identb", [P, P], BF16)
        wmask = sa("wmask", [P, 2, 4, P], BF16)
        colt = sa("colt", [C, 8])
        rowt = sa("rowt", [P, 3, D])
        wqk_s = sa("wqk_s", [C + 1, 2, 4 * D])
        wv_s = sa("wv_s", [C + 1, 2, 2 * D])
        wp_s = sa("wp_s", [C + 1, 2, D])
        ws_s = sa("ws_s", [C + 1, 2, D])
        wo_s = sa("wo_s", [C + 1, 2, D])
        w1_s = sa("w1_s", [C + 1, 2, FF])
        w2_s = sa("w2_s", [P, FF // P, D])
        gate_s = sa("gate_s", [C, 2, NE])
        ids_s = sa("ids_s", [P, (NB + 2) * T], I32)
        idx_s = sa("idx_s", [P, T], I32)
        half_c = sa("half_c", [P, HT])
        eps_ln = sa("eps_ln", [P, HT])
        eps_rms = sa("eps_rms", [P, HT])
        emb = sa("emb", [P, T, D])
        xb = sa("xb", [P, T, D])
        ebt = sa("ebt", [P, T, D])
        xh = sa("xh", [P, HT, D])
        st = sa("st", [P, 2, HT, 6])
        mv = sa("mv", [P, HT, 2])
        mv2 = sa("mv2", [P, HT, 2])
        rs = sa("rs", [P, HT])
        rs2 = sa("rs2", [P, HT])
        xnT = sa("xnT", [C + 1, 2, WIN + SEQ])
        qT = sa("qT", [C, 2, 2, HALF])
        kT = sa("kT", [C, 2, WIN + SEQ])
        q2T = sa("q2T", [C, 2, 2, HALF])
        k2T = sa("k2T", [C, 2, 2, HALF])
        ex = sa("ex", [C, 2, HALF])
        rl = sa("rl", [C, 2, HALF])
        qm = sa("qm", [C, 2, HC, P])
        q2m = sa("q2m", [C, 2, HC, P])
        va = sa("va", [P, 2, NH, V1])
        vb = sa("vb", [P, 2, 2 * NH, V1])
        nmax = sa("nmax", [P, 3, 4])
        pr = sa("pr", [P, 3, 4, P])
        prT = sa("prT", [P, 2, 4, P])
        at = sa("at", [P, 4, 3, P])
        k2m = sa("k2m", [P, 2, C])
        state = sa("state", [C, 2, HC * V1])
        stated = sa("stated", [C, 2, HC * V1])
        aoso = sa("aoso", [P, 2, D])
        rec = sa("rec", [P, 2, NH])
        aosoT = sa("aosoT", [C + 1, 4, P])
        sh = sa("sh", [P, D])
        ssum = sa("ssum", [P, D])
        sT = sa("sT", [C + 1, 2, P])
        x2 = sa("x2", [P, D])
        hh = sa("hh", [P, D])
        sto = sa("sto", [P, 2, 6])
        mo = sa("mo", [P, 2, 2])
        rso = sa("rso", [P, 2])
        hT = sa("hT", [C + 1, 2, HALF])
        gT = sa("gT", [P, FF // P, HALF])
        h1 = sa("h1", [P, HT, 2, D])
        zn = sa("zn", [P, T, D])
        mr = sa("mr", [P, HT, 2])
        msq = sa("msq", [P, HT])
        rr = sa("rr", [P, 2, HT])
        hlT = sa("hlT", [C, 2, SEQ])
        lg, pb, oh1, oh2, tmp8, pos = (sa(n, [P, T, NE]) for n in ("lg", "pb", "oh1", "oh2", "tmp8", "pos"))
        r1 = sa("r1", [P, 4, T])
        run = sa("run", [P, 4, 4 + T, NE])
        pk = sa("pk", [P, T, 2])
        ek = sa("ek", [P, T, 2])
        keep = sa("keep", [P, T, 2])
        slot = sa("slot", [P, T, 2])
        wk = sa("wk", [P, T, 2])
        carry = sa("carry", [P, NE])
        spill = sa("spill", [P, T, 2])
        sidx = sa("sidx", [P, T, 2], I32)
        zero = sa("zero", [P, 4, D])

        tr = [ca.enter_context(nc.psum_tensor(f"tr{i}", [P, 512], F32)) for i in range(2)]
        bg = [ca.enter_context(nc.psum_tensor(f"bg{i}", [P, 512], F32)) for i in range(3)]
        ao_ps = ca.enter_context(nc.psum_tensor("ao_ps", [P, 512], F32))
        nu_ps = ca.enter_context(nc.psum_tensor("nu_ps", [P, 512], F32))
        op_ps = ca.enter_context(nc.psum_tensor("op_ps", [P, 512], F32))

        loaded, weights_in, preset, zeroed = sem("loaded"), sem("weights_in"), sem("preset"), sem("zeroed")
        emb_in = [sem(f"emb_in{t}") for t in range(T)]
        e_var, e_rstd, x_var, x_rstd, xh_ready = (
            sem("e_var"), sem("e_rstd"), sem("x_var"), sem("x_rstd"), sem("xh_ready"))
        exp_ready, va_shifted = sem("exp_ready"), sem("va_shifted")
        qm_ready, q2m_ready, max_ready = sem("qm_ready"), sem("q2m_ready"), sem("max_ready")
        ao_full, ao_ready, nu_full, so_ready, state_ready = (
            sem("ao_full"), sem("ao_ready"), sem("nu_full"), sem("so_ready"), sem("state_ready"))
        so_var, so_rstd, sh_ready, shg_ready, s_ready = (
            sem("so_var"), sem("so_rstd"), sem("sh_ready"), sem("shg_ready"), sem("s_ready"))
        x2_var, x2_rstd, r_ready, hh_ready = sem("x2_var"), sem("x2_rstd"), sem("r_ready"), sem("hh_ready")
        h_var, h_rstd, hl_ready, z_sq, z_rstd, hb_stored = (
            sem("h_var"), sem("h_rstd"), sem("hl_ready"), sem("z_sq"), sem("z_rstd"), sem("hb_stored"))
        lmax_ready, lexp_ready, cnt_ready, sidx_ready, scattered = (
            sem("lmax_ready"), sem("lexp_ready"), sem("cnt_ready"), sem("sidx_ready"), sem("scattered"))
        tr_full = [sem(f"tr_full{i}") for i in range(2)]
        tr_drained = [sem(f"tr_drained{i}") for i in range(2)]
        bg_full = [sem(f"bg_full{i}") for i in range(3)]
        bg_drained = [sem(f"bg_drained{i}") for i in range(3)]
        op_full, op_drained = sem("op_full"), sem("op_drained")
        dve_step, pool_step = sem("dve_step"), sem("pool_step")
        passed = sem("passed")

        def tr_bank(*key):
            return tr[TR[key]]

        def bg_bank(*key):
            return bg[BG[key]]

        def wait_tr_full(eng, it, *key):
            eng.wait_ge(tr_full[TR[key]], TR.fills(it, key, 1))

        def wait_tr_drained(eng, it, *key):
            eng.wait_ge(tr_drained[TR[key]], TR.fills(it, key, 2))

        def wait_tr_free(eng, it, *key):
            eng.wait_ge(tr_drained[TR[key]], TR.fills(it, key, 1))

        def wait_bg_full(eng, it, *key):
            eng.wait_ge(bg_full[BG[key]], BG.fills(it, key, 1))

        def wait_bg_drained(eng, it, *key):
            eng.wait_ge(bg_drained[BG[key]], BG.fills(it, key, 2))

        def wait_bg_free(eng, it, *key):
            eng.wait_ge(bg_drained[BG[key]], BG.fills(it, key, 1))

        def wait_op_full(eng, it, *key):
            eng.wait_ge(op_full, OP.fills(it, key, 1))

        def wait_op_free(eng, it, *key):
            eng.wait_ge(op_drained, OP.fills(it, key, 1))

        def wait_op_drained(eng, it, *key):
            eng.wait_ge(op_drained, OP.fills(it, key, 2))

        block = ca.enter_context(nc.Block())

        @block.sync
        def _(sp):
            for dst, src in ((cst[:], consts), (colt[:], cols), (rowt[:], rows3),
                             (ids_s[:, 0:NB * T], ids), (gate_s[:], gate)):
                sp.dma_start(dst, src).then_inc(loaded, 16)
            for dst, src in ((wqk_s, wqk), (wv_s, wv), (wp_s, wp), (ws_s, ws), (wo_s, wo), (w1_s, w1)):
                sp.dma_start(dst[0:C, 0, :], src[0:C, :]).then_inc(weights_in, 16)
                sp.dma_start(dst[:, 1, :], src[C:2 * C + 1, :]).then_inc(weights_in, 16)
            sp.wait_ge(preset, N_PRESET)
            sp.dma_start(w2_s[:], w2).then_inc(weights_in, 16)
            zr = zbuf[0:SLOTS + BLK, :].rearrange("(p n r) c -> n p r c", p=P, r=4)
            for n in range(N_ZERO):
                sp.dma_start(zr[n], zero[:]).then_inc(zeroed, 16)
            for stage, i, it in traverse(sp, NBATCH):
                if stage == "Rc":
                    sp.wait_ge(hl_ready, it * T + HT * (i + 1))
                    dst = hbase[bass.ds(it * SEQ + i * HALF, HALF), :, :].rearrange(
                        "(t p) k c -> p t k c", p=P)
                    sp.dma_start(dst, h1[:]).then_inc(hb_stored, 16)
            sp.wait_ge(hb_stored, 32 * NBATCH + 16)
            sp.wait_ge(zeroed, 16 * N_ZERO)

        @block.gpsimd
        def _(pool):
            nc.gpsimd.memset(half_c[:], -0.5).then_inc(preset, 1)
            nc.gpsimd.memset(eps_ln[:], 1e-5).then_inc(preset, 1)
            nc.gpsimd.memset(eps_rms[:], 1e-6).then_inc(preset, 1)
            nc.gpsimd.memset(zero[:], 0.0).then_inc(preset, 1)
            nc.gpsimd.memset(va[:], 1.0).then_inc(preset, 1)
            nc.gpsimd.memset(vb[:], 1.0).then_inc(preset, 1)
            nc.gpsimd.memset(ids_s[:, NB * T:], 0).then_inc(preset, 1)
            pool.wait_ge(loaded, 16 * N_TABLES)
            pool.wait_ge(preset, N_PRESET)

            def gather(h):
                pool.sem_inc(passed, 1)
                for t in range(HT * h, HT * h + HT):
                    nc.gpsimd.indirect_dma_start(
                        out=emb[:, t, :], out_offset=None, in_=table,
                        in_offset=bass.IndirectOffsetOnAxis(ap=idx_s[:, t:t + 1], axis=0),
                    ).then_inc(emb_in[t], 16)

            pool.dma_start(spill[:], consts[:, C_SP:C_SP + 2 * T].rearrange("p (t k) -> p t k", k=2),
                           ).then_inc(scattered, 16)
            nc.gpsimd.tensor_copy(idx_s[:], ids_s[:, 0:T]).then_inc(pool_step, 1)
            pool.wait_ge(pool_step, 1)
            for h in range(2):
                gather(h)
            step = [1, 0]

            def link(ins):
                step[0] += 1
                step[1] += it.reg is not None
                ins.then_inc(pool_step, 1)
                pool.wait_ge(pool_step, it.steps(step[0], POOL_PER))

            def rsqrt(dst, src, n, eps):
                link(nc.gpsimd.tensor_tensor(out=src, in0=src, in1=eps[:, 0:n], op=ALU.add))
                return nc.gpsimd.tensor_tensor(out=dst, in0=src, in1=half_c[:, 0:n], op=ALU.pow)

            nhm = cst[0:C, C_HM:C_HM + HC].unsqueeze(2).to_broadcast([C, HC, P])
            for stage, i, it in traverse(pool, NBATCH):
                h, j = i // HT, (i % HT) * P
                if stage == "Fa":
                    pool.wait_ge(e_var, it * 2 + (i + 1))
                    rsqrt(rs[:], mv[:, :, 1], HT, eps_ln).then_inc(e_rstd, 1)
                elif stage == "Fb":
                    pool.wait_ge(x_var, it * 2 + (i + 1))
                    rsqrt(rs2[:], mv2[:, :, 1], HT, eps_ln).then_inc(x_rstd, 1)
                elif stage == "Fe":
                    if not it.zeroth():
                        wait_bg_drained(pool, it.prev(), "M", i, FF // P + HT - 1)
                    for t in range(HT * i, HT * i + HT):
                        pool.wait_ge(emb_in[t], it * 16 + 16)
                        link(nc.gpsimd.tensor_tensor(out=ebt[:, t, :], in0=emb[:, t, :], in1=rowt[:, 2, :],
                                                     op=ALU.add))
                elif stage == "Fg":
                    pool.wait_ge(x_var, it * 2 + (i + 1))
                    link(nc.gpsimd.tensor_copy(idx_s[:, HT * i:HT * i + HT],
                                               ids_s[:, bass.ds(it * T + (T + HT * i), HT)]))
                    gather(i)
                elif stage == "Qm":
                    wait_bg_drained(pool, it, "P", h, 1)
                    if i or not it.zeroth():
                        wait_bg_full(pool, it if i else it.prev(), "Sa", (i - 1) % T, 2)
                    for c in range(2):
                        src = qT[:, h, c, j:j + P].unsqueeze(1).to_broadcast([C, HC, P])
                        nc.gpsimd.tensor_tensor(out=qm[:, c], in0=src, in1=nhm,
                                                op=ALU.mult).then_inc(qm_ready, 1)
                elif stage == "Qn":
                    wait_bg_drained(pool, it, "P", h, 5)
                    if i or not it.zeroth():
                        wait_bg_full(pool, it if i else it.prev(), "La", (i - 1) % T, 3)
                    for c in range(2):
                        src = q2T[:, h, c, j:j + P].unsqueeze(1).to_broadcast([C, HC, P])
                        nc.gpsimd.tensor_tensor(out=q2m[:, c], in0=src, in1=nhm,
                                                op=ALU.mult).then_inc(q2m_ready, 1)
                elif stage == "Ob":
                    pool.wait_ge(so_var, it * T + (i + 1))
                    rsqrt(rso[:, 0:1], mo[:, 0, 1:2], 1, eps_ln).then_inc(so_rstd, 1)
                elif stage == "Oc":
                    pool.wait_ge(sh_ready, it * T + (i + 1))
                    link(nc.gpsimd.tensor_tensor(out=sh[:], in0=sh[:], in1=rowt[:, 0, :], op=ALU.mult))
                    nc.gpsimd.tensor_tensor(out=sh[:], in0=sh[:], in1=rowt[:, 1, :],
                                            op=ALU.add).then_inc(shg_ready, 1)
                elif stage == "Oe":
                    pool.wait_ge(x2_var, it * T + (i + 1))
                    rsqrt(rso[:, 1:2], mo[:, 1, 1:2], 1, eps_ln).then_inc(x2_rstd, 1)
                    nc.gpsimd.tensor_tensor(out=ebt[:, i, :], in0=ebt[:, i, :], in1=x2[:],
                                            op=ALU.add).then_inc(r_ready, 1)
                elif stage == "Ra":
                    pool.wait_ge(h_var, it * 2 + (i + 1))
                    rsqrt(rr[:, 0, :], mr[:, :, 1], HT, eps_ln).then_inc(h_rstd, 1)
                elif stage == "Rb":
                    pool.wait_ge(z_sq, it * 2 + (i + 1))
                    rsqrt(rr[:, 1, :], msq[:], HT, eps_rms).then_inc(z_rstd, 1)
                elif stage == "Tf":
                    pool.wait_ge(sidx_ready, it + 1)
                    pool.wait_ge(zeroed, 16 * N_ZERO)
                    pool.sem_inc(passed, 1)
                    for t in range(T):
                        for k in range(2):
                            nc.gpsimd.indirect_dma_start(
                                out=zbuf, in_=zn[:, t, :], in_offset=None,
                                out_offset=bass.IndirectOffsetOnAxis(ap=sidx[:, t, k:k + 1], axis=0),
                            ).then_inc(scattered, 16)
            assert step[1] == POOL_PER, step
            for t in range(T):
                pool.wait_ge(emb_in[t], 16 * (NBATCH + (2 if t < HT else 1)))
            pool.wait_ge(scattered, NBATCH * T * 2 * 16 + 16)

        @block.scalar
        def _(act):
            act.wait_ge(loaded, 16 * N_TABLES)
            nc.scalar.copy(identb[:], ident).then_inc(preset, 1)
            for v in range(2):
                src = cst[:, C_WM0 + v * P:C_WM0 + (v + 1) * P].unsqueeze(1).to_broadcast([P, 4, P])
                nc.scalar.copy(wmask[:, v], src).then_inc(preset, 1)
            act.wait_ge(preset, N_PRESET)
            for stage, i, it in traverse(act, NBATCH):
                if stage == "Fc":
                    for c in range(2):
                        wait_tr_full(act, it, "Fc", i, c)
                        nc.scalar.activation(xnT[0:C, c, WIN + i * HALF:WIN + (i + 1) * HALF],
                                             tr_bank("Fc", i, c)[0:C, :], ACT.Identity,
                                             bias=colt[:, 2 + c:3 + c], scale=colt[:, c:c + 1],
                                             ).then_inc(tr_drained[TR["Fc", i, c]], 1)
                elif stage == "P":
                    for c in range(2):
                        wait_bg_full(act, it, "P", i, c)
                        nc.scalar.mul(qT[:, i, c, :], bg_bank("P", i, c)[0:C, :], float(HD) ** -0.5,
                                      ).then_inc(bg_drained[BG["P", i, c]], 1)
                    for n in range(4, 8):
                        wait_bg_full(act, it, "P", i, n)
                        if n >= 6:
                            wait_bg_drained(act, it, "P", i, n - 2)
                        nc.scalar.activation(ex[:, n % 2, :], bg_bank("P", i, n)[0:C, :],
                                             ACT.Exp).then_inc(exp_ready, 1)
                elif stage == "V":
                    wait_bg_full(act, it, "V", i, 0)
                    if i or not it.zeroth():
                        wait_bg_drained(act, it if i else it.prev(), "V", (i - 1) % T, 0)
                    nc.scalar.copy(va[0:WIN, i % 2, :, 0:HD], vb[WIN:P, 1 - i % 2, 0:NH, 0:HD]).then_inc(va_shifted, 1)
                    act.wait_ge(va_shifted, it * T + (i + 1))
                    heads = bg_bank("V", i, 0)[:, 0:2 * D].rearrange("p (h e) -> p h e", e=HD)
                    nc.scalar.copy(va[WIN:P, i % 2, :, 0:HD], heads[0:WIN, 0:NH, :])
                    nc.scalar.copy(vb[:, i % 2, :, 0:HD], heads).then_inc(bg_drained[BG["V", i, 0]], 1)
                elif stage == "Sa":
                    for g in range(3):
                        act.wait_ge(max_ready, it * 3 * T + (3 * i + g + 1))
                        b = bg_bank("Sa", i, g)
                        for j in range(4):
                            ins = nc.scalar.activation(pr[:, g, j, :], b[:, j * P:(j + 1) * P], ACT.Exp,
                                                       bias=nmax[:, g, j:j + 1])
                        ins.then_inc(bg_drained[BG["Sa", i, g]], 1)
                elif stage in ("Sp", "Sq"):
                    for g in range(TR_FILLS[stage]):
                        wait_tr_full(act, it, stage, i, g)
                        nc.scalar.copy(prT[:, g], tr_bank(stage, i, g)[:, :].rearrange(
                            "p (j q) -> p j q", j=4)).then_inc(tr_drained[TR[stage, i, g]], 1)
                elif stage == "La" and i < T - 1:
                    wait_tr_full(act, it, "La", i, 0)
                    nc.scalar.copy(k2m[:], tr_bank("La", i, 0)[:, 0:D].rearrange("p (c f) -> p c f", c=2),
                                   ).then_inc(tr_drained[TR["La", i, 0]], 1)
                elif stage == "Oa":
                    wait_tr_full(act, it, "Oa", i, 0)
                    nc.scalar.copy(aosoT[0:C], tr_bank("Oa", i, 0)[0:C, :].rearrange("p (j q) -> p j q", j=4),
                                   ).then_inc(tr_drained[TR["Oa", i, 0]], 1)
                elif stage == "Od":
                    wait_tr_full(act, it, "Od", i, 0)
                    nc.scalar.copy(sT[0:C], tr_bank("Od", i, 0)[0:C, 0:2 * P].rearrange(
                        "p (c q) -> p c q", c=2)).then_inc(tr_drained[TR["Od", i, 0]], 1)
                elif stage == "Of":
                    wait_tr_full(act, it, "Of", i, 0)
                    j = (i % HT) * P
                    for c in range(2):
                        ins = nc.scalar.activation(hT[0:C, c, j:j + P], tr_bank("Of", i, 0)[0:C, c * P:(c + 1) * P],
                                                   ACT.Identity, bias=colt[:, 6 + c:7 + c],
                                                   scale=colt[:, 4 + c:5 + c])
                    ins.then_inc(tr_drained[TR["Of", i, 0]], 1)
                elif stage == "M":
                    for m in range(FF // P):
                        wait_bg_full(act, it, "M", i, m)
                        nc.scalar.activation(gT[:, m, :], bg_bank("M", i, m)[:, :], ACT.Gelu,
                                             ).then_inc(bg_drained[BG["M", i, m]], 1)
                elif stage == "Rc":
                    for t in range(HT):
                        wait_tr_full(act, it, "Rc", i, t)
                        j = (i * HT + t) * P
                        nc.scalar.copy(hlT[:, :, j:j + P], tr_bank("Rc", i, t)[0:C, 0:2 * P].rearrange(
                            "p (c q) -> p c q", c=2)).then_inc(tr_drained[TR["Rc", i, t]], 1)
                elif stage == "T":
                    act.wait_ge(lmax_ready, it + 1)
                    nc.scalar.activation(pb[:], lg[:], ACT.Exp).then_inc(lexp_ready, 1)

        @block.vector
        def _(dve):
            for b in (xnT, kT):
                nc.vector.memset(b[0:C, :, 0:WIN], 0.0).then_inc(preset, 1)
            for b in (xnT, aosoT, sT, hT):
                nc.vector.memset(b[C:C + 1], 1.0).then_inc(preset, 1)
            nc.vector.memset(carry[:], 0.0).then_inc(preset, 1)
            nc.vector.memset(run[:], 0.0).then_inc(preset, 1)
            dve.wait_ge(loaded, 16 * N_TABLES)
            dve.wait_ge(preset, N_PRESET)
            caus3 = cst[:, C_CAUS:C_CAUS + P].unsqueeze(1).to_broadcast([P, 3, P])
            smask = cst[0:C, C_SM:C_SM + HC * V1].unsqueeze(1).to_broadcast([C, 2, HC * V1])
            tie8 = cst[:, C_TIE:C_TIE + NE].unsqueeze(1).to_broadcast([P, T, NE])
            ecap8 = cst[:, C_ECAP:C_ECAP + NE].unsqueeze(1).to_broadcast([P, T, NE])

            def each8(ap):
                return ap.unsqueeze(2).to_broadcast([P, T, NE])

            dve.sem_inc(r_ready, 1)
            dve.sem_inc(hb_stored, 16)
            step = [0, 0]

            def mark(ins):
                step[0] += 1
                step[1] += it.reg is not None
                ins.then_inc(dve_step, 1)

            def settle():
                dve.wait_ge(dve_step, it.steps(step[0], DVE_PER))

            def link(ins):
                mark(ins)
                settle()

            def moments(dst, srcs, st):
                for t, src in enumerate(srcs):
                    mark(nc.vector.bn_stats(st[:, t, :], src))
                settle()
                dve.sem_inc(passed, 1)
                for t in range(len(srcs)):
                    ins = nc.vector.bn_aggr(dst[:, t, :], st[:, t, :])
                return ins

            def normalise(dst, src, mean, rstd):
                return nc.vector.tensor_scalar(dst, src, mean, rstd, ALU.subtract, ALU.mult)

            tt, ts, red = nc.vector.tensor_tensor, nc.vector.tensor_scalar, nc.vector.tensor_reduce

            def largest(m, oh):
                link(red(r1[:, m, :], pb[:], AX.X, ALU.max))
                link(tt(out=tmp8[:], in0=pb[:], in1=each8(r1[:, m, :]), op=ALU.is_equal))
                link(tt(out=tmp8[:], in0=tmp8[:], in1=tie8, op=ALU.mult))
                link(red(r1[:, 3, :], tmp8[:], AX.X, ALU.max))
                link(tt(out=oh[:], in0=tmp8[:], in1=each8(r1[:, 3, :]), op=ALU.is_equal))

            for stage, i, it in traverse(dve, NBATCH):
                h = i // HT
                if stage == "Fa":
                    for t in range(HT):
                        dve.wait_ge(emb_in[HT * i + t], it * 16 + 16)
                    moments(mv, [emb[:, HT * i + t, :] for t in range(HT)], st[:, 0]).then_inc(e_var, 1)
                elif stage == "Fb":
                    dve.wait_ge(e_rstd, it * 2 + (i + 1))
                    for t in range(HT):
                        k = HT * i + t
                        mark(normalise(xb[:, k, :], emb[:, k, :], mv[:, t, 0:1], rs[:, t:t + 1]))
                    settle()
                    moments(mv2, [xb[:, HT * i + t, :] for t in range(HT)], st[:, 0]).then_inc(x_var, 1)
                elif stage == "Fn":
                    dve.wait_ge(x_rstd, it * 2 + (i + 1))
                    if i:
                        wait_tr_full(dve, it, "Fc", 0, 1)
                    elif not it.zeroth():
                        wait_tr_full(dve, it.prev(), "Fc", 1, 1)
                    for t in range(HT):
                        normalise(xh[:, t, :], xb[:, HT * i + t, :], mv2[:, t, 0:1], rs2[:, t:t + 1],
                                  ).then_inc(xh_ready, 1)
                elif stage == "P":
                    for c in range(2):
                        wait_bg_full(dve, it, "P", i, 2 + c)
                        nc.vector.tensor_copy(kT[:, c, WIN + i * HALF:WIN + (i + 1) * HALF],
                                              bg_bank("P", i, 2 + c)[0:C, :],
                                              ).then_inc(bg_drained[BG["P", i, 2 + c]], 1)
                    for n in range(4, 8):
                        dve.wait_ge(exp_ready, it * 8 + (4 * i + n - 3))
                        link(nc.vector.tensor_scalar(rl[:, n % 2], bg_bank("P", i, n)[0:C, :], 1e-4, 1e-4,
                                                     ALU.add, ALU.max))
                        dst = (q2T if n < 6 else k2T)[:, i, n % 2, :]
                        nc.vector.scalar_tensor_tensor(dst, ex[:, n % 2, :], 1.0, rl[:, n % 2], ALU.min, ALU.add,
                                                       ).then_inc(bg_drained[BG["P", i, n]], 1)
                elif stage == "Sa":
                    for g in range(3):
                        wait_bg_full(dve, it, "Sa", i, g)
                        nc.vector.tensor_reduce(nmax[:, g, :], bg_bank("Sa", i, g)[:, :].rearrange(
                            "p (j k) -> p j k", j=4), AX.X, ALU.max, negate=True).then_inc(max_ready, 1)
                elif stage == "La":
                    for g in range(4):
                        wait_bg_full(dve, it, "La", i, g)
                        nc.vector.tensor_tensor(out=at[:, g], in0=bg_bank("La", i, g)[:, 0:3 * P].rearrange(
                            "p (j q) -> p j q", j=3), in1=caus3, op=ALU.mult,
                        ).then_inc(bg_drained[BG["La", i, g]], 1)
                elif stage == "Sr":
                    dve.wait_ge(ao_full, it * T + (i + 1))
                    acc = ao_ps[:, 0:NH * V1].rearrange("p (h e) -> p h e", e=V1)
                    link(nc.vector.reciprocal(rec[:, 0, :], acc[:, :, HD]))
                    nc.vector.tensor_tensor(out=aoso[:, 0, :].rearrange("p (h e) -> p h e", e=HD),
                                            in0=acc[:, :, 0:HD],
                                            in1=rec[:, 0, :].unsqueeze(2).to_broadcast([P, NH, HD]),
                                            op=ALU.mult).then_inc(ao_ready, 1)
                elif stage == "Lb":
                    if i < T - 1:
                        wait_bg_full(dve, it, "Lb", i, 0)
                        new = bg_bank("Lb", i, 0)[0:C, 0:2 * HC * V1].rearrange("p (c n) -> p c n", c=2)
                        if i == 0:
                            ins = nc.vector.tensor_copy(state[:], new)
                        else:
                            ins = nc.vector.tensor_tensor(out=state[:], in0=new, in1=state[:], op=ALU.add)
                        ins.then_inc(bg_drained[BG["Lb", i, 0]], 1)
                        wait_bg_drained(dve, it, "Lb", i, 0)
                        nc.vector.tensor_tensor(out=stated[:], in0=state[:], in1=smask,
                                                op=ALU.mult).then_inc(state_ready, 1)
                    dve.wait_ge(nu_full, it * T + (i + 1))
                    acc = nu_ps[:, 0:NH * V1].rearrange("p (h e) -> p h e", e=V1)
                    link(nc.vector.tensor_scalar_add(rec[:, 1, :], acc[:, :, HD], 1e-4 * HD ** 0.5))
                    link(nc.vector.reciprocal(rec[:, 1, :], rec[:, 1, :]))
                    nc.vector.tensor_tensor(out=aoso[:, 1, :].rearrange("p (h e) -> p h e", e=HD),
                                            in0=acc[:, :, 0:HD],
                                            in1=rec[:, 1, :].unsqueeze(2).to_broadcast([P, NH, HD]),
                                            op=ALU.mult).then_inc(so_ready, 1)
                elif stage == "Ob":
                    wait_op_full(dve, it, "Ob", i, 0)
                    link(nc.vector.bn_stats(sto[:, 0, :], op_ps[:, D:2 * D]))
                    dve.sem_inc(passed, 1)
                    nc.vector.bn_aggr(mo[:, 0, :], sto[:, 0, :]).then_inc(so_var, 1)
                elif stage == "Oc":
                    dve.wait_ge(so_rstd, it * T + (i + 1))
                    normalise(sh[:], op_ps[:, D:2 * D], mo[:, 0, 0:1], rso[:, 0:1]).then_inc(sh_ready, 1)
                elif stage == "Os":
                    dve.wait_ge(shg_ready, it * T + (i + 1))
                    nc.vector.tensor_tensor(out=ssum[:], in0=op_ps[:, 0:D], in1=sh[:], op=ALU.add,
                                            ).then_inc(op_drained, 1)
                elif stage == "Oe":
                    wait_op_full(dve, it, "Oe", i, 0)
                    dve.wait_ge(r_ready, it * T + (i + 1))
                    nc.vector.tensor_tensor(out=x2[:], in0=op_ps[:, 0:D], in1=xb[:, i, :], op=ALU.add,
                                            ).then_inc(op_drained, 1)
                    wait_op_drained(dve, it, "Oe", i, 0)
                    link(nc.vector.bn_stats(sto[:, 1, :], x2[:]))
                    dve.sem_inc(passed, 1)
                    nc.vector.bn_aggr(mo[:, 1, :], sto[:, 1, :]).then_inc(x2_var, 1)
                elif stage == "On":
                    dve.wait_ge(x2_rstd, it * T + (i + 1))
                    normalise(hh[:], x2[:], mo[:, 1, 0:1], rso[:, 1:2]).then_inc(hh_ready, 1)
                elif stage == "M":
                    dve.wait_ge(hb_stored, it * 32 + 16 * (i + 1))
                    for t in range(HT):
                        wait_bg_full(dve, it, "M", i, FF // P + t)
                        dve.wait_ge(r_ready, it * T + (HT * i + t + 2))
                        nc.vector.tensor_tensor(out=h1[:, t, 0, :], in0=bg_bank("M", i, FF // P + t)[:, 0:D],
                                                in1=ebt[:, HT * i + t, :], op=ALU.add,
                                                ).then_inc(bg_drained[BG["M", i, FF // P + t]], 1)
                elif stage == "Ra":
                    for t in range(HT - 3, HT):
                        wait_bg_drained(dve, it, "M", i, FF // P + t)
                    moments(mr, [h1[:, t, 0, :] for t in range(HT)], st[:, 1]).then_inc(h_var, 1)
                elif stage == "Rb":
                    dve.wait_ge(h_rstd, it * 2 + (i + 1))
                    for t in range(HT):
                        normalise(h1[:, t, 1, :], h1[:, t, 0, :], mr[:, t, 0:1], rr[:, 0, t:t + 1],
                                  ).then_inc(hl_ready, 1)
                    dve.wait_ge(hl_ready, it * T + HT * (i + 1))
                    if i == 0:
                        dve.wait_ge(scattered, it * 16 * 2 * T + 16)
                    for t in range(HT):
                        ins = nc.vector.scalar_tensor_tensor(
                            zn[:, HT * i + t, :], h1[:, t, 1, :], 4.0 / D, h1[:, t, 1, :], ALU.mult, ALU.mult,
                            accum_out=msq[:, t:t + 1])
                    ins.then_inc(z_sq, 1)
                elif stage == "Rc":
                    dve.wait_ge(z_rstd, it * 2 + (i + 1))
                    for t in range(HT):
                        mark(nc.vector.tensor_scalar(zn[:, HT * i + t, :], h1[:, t, 1, :], rr[:, 1, t:t + 1], 2.0,
                                                     ALU.mult, ALU.mult))
                elif stage == "T":
                    wait_tr_full(dve, it, "T", 0, 0)
                    lps = tr_bank("T", 0, 0)[:, 0:T * NE].rearrange("p (t e) -> p t e", e=NE)
                    nc.vector.tensor_copy(tmp8[:], lps).then_inc(tr_drained[TR["T", 0, 0]], 1)
                    wait_tr_drained(dve, it, "T", 0, 0)
                    link(red(r1[:, 0, :], tmp8[:], AX.X, ALU.max))
                    tt(out=lg[:], in0=tmp8[:], in1=each8(r1[:, 0, :]), op=ALU.subtract).then_inc(lmax_ready, 1)
                elif stage == "Tb":
                    dve.wait_ge(lexp_ready, it + 1)
                    link(red(r1[:, 0, :], pb[:], AX.X, ALU.add))
                    link(nc.vector.reciprocal(r1[:, 0, :], r1[:, 0, :]))
                    link(tt(out=pb[:], in0=pb[:], in1=each8(r1[:, 0, :]), op=ALU.mult))
                    largest(1, oh1)
                elif stage == "Tc":
                    link(nc.vector.scalar_tensor_tensor(pb[:], oh1[:], -2.0, pb[:], ALU.mult, ALU.add))
                    largest(2, oh2)
                    link(tt(out=run[:, 0, 4:], in0=oh1[:], in1=oh2[:], op=ALU.add))
                    for n in range(3):
                        d = 1 << n
                        ins = tt(out=run[:, n + 1, 4:], in0=run[:, n, 4:], in1=run[:, n, 4 - d:4 + T - d], op=ALU.add)
                        if n < 2:
                            link(ins)
                    ins.then_inc(cnt_ready, 1)
                    link(tt(out=r1[:, 0, :], in0=r1[:, 1, :], in1=r1[:, 2, :], op=ALU.add))
                    link(nc.vector.reciprocal(r1[:, 0, :], r1[:, 0, :]))
                    for k in range(2):
                        mark(tt(out=wk[:, :, k], in0=r1[:, 1 + k, :], in1=r1[:, 0, :], op=ALU.mult))
                elif stage == "Td":
                    wait_bg_full(dve, it, "Td", 0, 0)
                    cps = bg_bank("Td", 0, 0)
                    link(tt(out=pos[:], in0=cps[:, 0:T * NE].rearrange("p (t e) -> p t e", e=NE),
                            in1=carry[:].unsqueeze(1).to_broadcast([P, T, NE]), op=ALU.add))
                    tt(out=carry[:], in0=cps[:, T * NE:(T + 1) * NE], in1=carry[:], op=ALU.add,
                       ).then_inc(bg_drained[BG["Td", 0, 0]], 1)
                    wait_bg_drained(dve, it, "Td", 0, 0)
                    for k, oh in enumerate((oh1, oh2)):
                        link(tt(out=tmp8[:], in0=pos[:], in1=oh[:], op=ALU.mult))
                        link(red(pk[:, :, k], tmp8[:], AX.X, ALU.add))
                        link(tt(out=tmp8[:], in0=oh[:], in1=ecap8, op=ALU.mult))
                        link(red(ek[:, :, k], tmp8[:], AX.X, ALU.add))
                elif stage == "Te":
                    link(ts(keep[:], pk[:], float(CAP), None, ALU.is_lt))
                    link(tt(out=slot[:], in0=ek[:], in1=pk[:], op=ALU.add))
                    link(tt(out=slot[:], in0=slot[:], in1=spill[:], op=ALU.subtract))
                    link(tt(out=slot[:], in0=slot[:], in1=keep[:], op=ALU.mult))
                    link(tt(out=slot[:], in0=slot[:], in1=spill[:], op=ALU.add))
                    nc.vector.tensor_copy(sidx[:], slot[:]).then_inc(sidx_ready, 1)
                    link(ts(pk[:], pk[:], float(CAP - 1), None, ALU.min))
                    link(tt(out=pk[:], in0=pk[:], in1=ek[:], op=ALU.add))
                    mark(nc.vector.tensor_copy(gidx[:, bass.ds(it * T + 0, T), :], pk[:]))
                    mark(tt(out=cw[:, bass.ds(it * T + 0, T), :], in0=wk[:], in1=keep[:], op=ALU.mult))
                    link(nc.vector.tensor_scalar_add(spill[:], spill[:], float(2 * SEQ)))
            assert step[1] == DVE_PER, step

        @block.tensor
        def _(pe):
            mm, tp = nc.tensor.matmul, nc.tensor.transpose
            pe.wait_ge(loaded, 16 * N_TABLES)
            pe.wait_ge(weights_in, 16 * N_WEIGHTS)
            pe.wait_ge(preset, N_PRESET)
            ident_c = cst[0:C, C_ID:C_ID + C]
            for s in (*tr_drained, *bg_drained, op_drained, ao_ready, so_ready):
                pe.sem_inc(s, 1)
            def exp_transposes(stage, i, n, g):
                wait_bg_drained(pe, it, "Sa", i, g)
                wait_tr_free(pe, it, stage, i, n)
                for j in range(4):
                    ins = tp(tr_bank(stage, i, n)[:, j * P:(j + 1) * P], pr[:, g, j, :], ident)
                ins.then_inc(tr_full[TR[stage, i, n]], 1)

            def window_products(stage, i, n, g):
                wait_tr_drained(pe, it, stage, i, n)
                for j in range(4):
                    hd = 4 * g + j
                    for a, v in enumerate((va, vb)):
                        r = a * WIN
                        ins = mm(ao_ps[r:r + WIN, hd * V1:(hd + 1) * V1], prT[:, n, j, r:r + WIN],
                                 v[:, i % 2, hd, :], start=True, stop=True, skip_group_check=True)
                return ins

            for stage, i, it in traverse(pe, NBATCH):
                h, j = i // HT, (i % HT) * P
                if stage == "Fc":
                    pe.wait_ge(xh_ready, it * T + HT * (i + 1))
                    for c in range(2):
                        wait_tr_free(pe, it, "Fc", i, c)
                        for t in range(HT):
                            ins = tp(tr_bank("Fc", i, c)[0:C, t * P:(t + 1) * P], xh[:, t, c * C:(c + 1) * C], ident)
                        ins.then_inc(tr_full[TR["Fc", i, c]], 1)
                elif stage == "P":
                    wait_tr_drained(pe, it, "Fc", i, 1)
                    for n in range(8):
                        wait_bg_free(pe, it, "P", i, n)
                        for c in range(2):
                            ins = mm(bg_bank("P", i, n)[0:C, :], wqk_s[0:C + c, c, n * C:(n + 1) * C],
                                     xnT[0:C + c, c, WIN + i * HALF:WIN + (i + 1) * HALF],
                                     start=(c == 0), stop=(c == 1))
                        ins.then_inc(bg_full[BG["P", i, n]], 1)
                elif stage == "V":
                    wait_bg_free(pe, it, "V", i, 0)
                    s0 = WIN + i * P
                    for c in range(2):
                        ins = mm(bg_bank("V", i, 0)[:, 0:2 * D], xnT[0:C + c, c, s0:s0 + P],
                                 wv_s[0:C + c, c, :], start=(c == 0), stop=(c == 1))
                    ins.then_inc(bg_full[BG["V", i, 0]], 1)
                elif stage == "Sa":
                    for g in range(3):
                        wait_bg_free(pe, it, "Sa", i, g)
                        b = bg_bank("Sa", i, g)
                        mm(b[:, :], identb[:], wmask[:, min(i, 1)].rearrange("p j k -> p (j k)"),
                           start=True, stop=False, skip_group_check=True)
                        if g == 0:
                            pe.wait_ge(qm_ready, it * 2 * T + 2 * (i + 1))
                            if i % HT == 0:
                                wait_bg_drained(pe, it, "P", h, 3)
                        for n in range(4):
                            c, hd = divmod(4 * g + n, HC)
                            for a in range(2):
                                r = a * WIN
                                ins = mm(b[r:r + WIN, n * P:(n + 1) * P], qm[:, c, hd, r:r + WIN],
                                         kT[:, c, i * P + r:i * P + r + P],
                                         start=False, stop=(n == 3), skip_group_check=True)
                        ins.then_inc(bg_full[BG["Sa", i, g]], 1)
                elif stage == "La":
                    pe.wait_ge(q2m_ready, it * 2 * T + 2 * (i + 1))
                    if i % HT == 0 and BG["P", h, 7] != BG["La", i, 0]:
                        wait_bg_drained(pe, it, "P", h, 7)
                    for g in range(4):
                        wait_bg_free(pe, it, "La", i, g)
                        c, hd = divmod(3 * g, HC)
                        mm(bg_bank("La", i, g)[:, 0:3 * P], k2T[:, h, c, j:j + P],
                           q2m[:, c, hd:hd + 3, :].rearrange("p j q -> p (j q)"),
                           start=True, stop=True).then_inc(bg_full[BG["La", i, g]], 1)
                    if i < T - 1:
                        wait_tr_free(pe, it, "La", i, 0)
                        for c in range(2):
                            ins = tp(tr_bank("La", i, 0)[:, c * C:(c + 1) * C], k2T[:, h, c, j:j + P], ident_c)
                        ins.then_inc(tr_full[TR["La", i, 0]], 1)
                elif stage == "Sp":
                    for g in range(2):
                        exp_transposes("Sp", i, g, g)
                elif stage == "Sq":
                    pe.wait_ge(ao_ready, it * T + (i + 1))
                    wait_bg_drained(pe, it, "V", i, 0)
                    window_products("Sp", i, 0, 0)
                    exp_transposes("Sq", i, 0, 2)
                    window_products("Sp", i, 1, 1)
                elif stage == "Sr":
                    window_products("Sq", i, 0, 2).then_inc(ao_full, 1)
                elif stage == "Lb":
                    pe.wait_ge(so_ready, it * T + (i + 1))
                    if i:
                        pe.wait_ge(state_ready, it * (T - 1) + i)
                        for c in range(2):
                            mm(nu_ps[:, c * HC * V1:(c + 1) * HC * V1], q2T[:, h, c, j:j + P], stated[:, c, :],
                               start=(c == 0), stop=False, skip_group_check=True)
                    wait_bg_drained(pe, it, "La", i, 3)
                    for hd in range(NH):
                        for r in (0, WIN):
                            ins = mm(nu_ps[r:r + WIN, hd * V1:(hd + 1) * V1], at[:, hd // 3, hd % 3, r:r + WIN],
                                     vb[:, i % 2, NH + hd, :], start=(i == 0 and hd == 0), stop=(hd == NH - 1),
                                     skip_group_check=True)
                    ins.then_inc(nu_full, 1)
                    if i < T - 1:
                        wait_tr_drained(pe, it, "La", i, 0)
                        wait_bg_free(pe, it, "Lb", i, 0)
                        for c in range(2):
                            ins = mm(bg_bank("Lb", i, 0)[0:C, c * HC * V1:(c + 1) * HC * V1], k2m[:, c, :],
                                     vb[:, i % 2, NH + c * HC:NH + (c + 1) * HC, :].rearrange("p h e -> p (h e)"),
                                     start=True, stop=True, skip_group_check=True)
                        ins.then_inc(bg_full[BG["Lb", i, 0]], 1)
                elif stage == "Oa":
                    pe.wait_ge(ao_ready, it * T + (i + 2))
                    pe.wait_ge(so_ready, it * T + (i + 2))
                    wait_tr_free(pe, it, "Oa", i, 0)
                    for n in range(4):
                        ins = tp(tr_bank("Oa", i, 0)[0:C, n * P:(n + 1) * P],
                                 aoso[:, n // 2, (n % 2) * C:(n % 2 + 1) * C], ident)
                    ins.then_inc(tr_full[TR["Oa", i, 0]], 1)
                elif stage == "Ob":
                    wait_tr_drained(pe, it, "Oa", i, 0)
                    wait_op_free(pe, it, "Ob", i, 0)
                    for n, w in enumerate((wp_s, ws_s)):
                        for c in range(2):
                            ins = mm(op_ps[:, n * D:(n + 1) * D], aosoT[0:C + c, 2 * n + c, :], w[0:C + c, c, :],
                                     start=(c == 0), stop=(c == 1), skip_group_check=True)
                    ins.then_inc(op_full, 1)
                elif stage == "Od":
                    wait_op_drained(pe, it, "Ob", i, 0)
                    wait_tr_free(pe, it, "Od", i, 0)
                    for c in range(2):
                        ins = tp(tr_bank("Od", i, 0)[0:C, c * P:(c + 1) * P], ssum[:, c * C:(c + 1) * C], ident)
                    ins.then_inc(tr_full[TR["Od", i, 0]], 1)
                elif stage == "Oe":
                    wait_tr_drained(pe, it, "Od", i, 0)
                    wait_op_free(pe, it, "Oe", i, 0)
                    for c in range(2):
                        ins = mm(op_ps[:, 0:D], sT[0:C + c, c, :], wo_s[0:C + c, c, :],
                                 start=(c == 0), stop=(c == 1))
                    ins.then_inc(op_full, 1)
                elif stage == "Of":
                    pe.wait_ge(hh_ready, it * T + (i + 1))
                    wait_tr_free(pe, it, "Of", i, 0)
                    for c in range(2):
                        ins = tp(tr_bank("Of", i, 0)[0:C, c * P:(c + 1) * P], hh[:, c * C:(c + 1) * C], ident)
                    ins.then_inc(tr_full[TR["Of", i, 0]], 1)
                elif stage == "M":
                    wait_tr_drained(pe, it, "Of", HT * i + HT - 1, 0)
                    for m in range(FF // P):
                        wait_bg_free(pe, it, "M", i, m)
                        for c in range(2):
                            ins = mm(bg_bank("M", i, m)[:, :], w1_s[0:C + c, c, m * P:(m + 1) * P], hT[0:C + c, c, :],
                                     start=(c == 0), stop=(c == 1))
                        ins.then_inc(bg_full[BG["M", i, m]], 1)
                    for t in range(HT):
                        n = FF // P + t
                        wait_bg_free(pe, it, "M", i, n)
                        for m in range(FF // P):
                            if t == 0:
                                wait_bg_drained(pe, it, "M", i, m)
                            ins = mm(bg_bank("M", i, n)[:, 0:D], gT[:, m, t * P:(t + 1) * P], w2_s[:, m, :],
                                     start=(m == 0), stop=(m == FF // P - 1))
                        ins.then_inc(bg_full[BG["M", i, n]], 1)
                elif stage == "Rc":
                    pe.wait_ge(hl_ready, it * T + HT * (i + 1))
                    for t in range(HT):
                        wait_tr_free(pe, it, "Rc", i, t)
                        for c in range(2):
                            ins = tp(tr_bank("Rc", i, t)[0:C, c * P:(c + 1) * P], h1[:, t, 1, c * C:(c + 1) * C], ident)
                        ins.then_inc(tr_full[TR["Rc", i, t]], 1)
                elif stage == "T":
                    wait_tr_drained(pe, it, "Rc", 1, HT - 1)
                    wait_tr_free(pe, it, "T", 0, 0)
                    for t in range(T):
                        for c in range(2):
                            ins = mm(tr_bank("T", 0, 0)[:, t * NE:(t + 1) * NE], hlT[:, c, t * P:(t + 1) * P],
                                     gate_s[:, c, :], start=(c == 0), stop=(c == 1), skip_group_check=True)
                    ins.then_inc(tr_full[TR["T", 0, 0]], 1)
                elif stage == "Td":
                    pe.wait_ge(cnt_ready, it + 1)
                    wait_bg_free(pe, it, "Td", 0, 0)
                    b = bg_bank("Td", 0, 0)
                    up, one = cst[:, C_UP:C_UP + P], cst[:, C_ONE:C_ONE + P]
                    mm(b[:, 0:T * NE], up, run[:, 0, 4:].rearrange("p t e -> p (t e)"),
                       start=True, stop=False, skip_group_check=True)
                    ins = mm(b[:, 0:(T + 1) * NE], one, run[:, 3, 3:].rearrange("p t e -> p (t e)"),
                             start=False, stop=True, skip_group_check=True)
                    ins.then_inc(bg_full[BG["Td", 0, 0]], 1)


def phase_b(nc, w13, w2e, nw, consts, zbuf, ybuf, NPAIR):
    with ExitStack() as cb:
        def sa(name, shape, dt=F32):
            return cb.enter_context(nc.sbuf_tensor(name, shape, dt))

        def sem(name):
            return cb.enter_context(nc.semaphore(name))

        NBK = 2 * NBLK
        MG = EH // P
        CUT = float(2 ** 13)
        PARTS = 5
        idb = sa("idb", [P, P])
        w13_in = sa("w13_in", [P, 2, 2 * EH])
        w_up, w_sum = sa("w_up", [P, 2, 2 * EH]), sa("w_sum", [P, 2, 2 * EH])
        w_hi = sa("w_hi", [P, 2, 2, 2 * EH], F32R)
        w_lo = sa("w_lo", [P, 2, 2, 2 * EH], F32R)
        w2_s = sa("w2e_s", [P, 2, EH // P, D])
        nw_s = sa("nw_s", [P, 2, 2])
        z = sa("z", [P, 2, BT, 2 * P])
        zT = sa("zT", [P, 2, 2, BLK])
        z_up = sa("z_up", [P, 2, BLK])
        z_hi = sa("z_hi", [P, 2, 2, BLK], F32R)
        z_lo = sa("z_lo", [P, 2, BLK], F32R)
        z_hl = sa("z_hl", [P, 2, BLK], F32R)
        sg = sa("sg", [P, 2, BLK])
        hm = sa("hm", [P, 2, EH // P, BLK])
        y = sa("y", [P, 2, BT, D])
        tr = [cb.enter_context(nc.psum_tensor(f"btr{i}", [P, 512], F32)) for i in range(2)]
        gu = [cb.enter_context(nc.psum_tensor(f"bgu{i}", [P, 512], F32)) for i in range(4)]
        yp = [cb.enter_context(nc.psum_tensor(f"byp{i}", [P, 512], F32)) for i in range(2)]
        id_in, raw_in, passed = sem("id_in"), sem("raw_in"), sem("passed_b")
        w_in = [sem(f"w_in{x}") for x in range(2)]
        z_in = [sem(f"z_in{b}") for b in range(2)]
        y_out = [sem(f"y_out{b}") for b in range(2)]
        t_full, zT_ready, z_up_ready, z_hi_ready, z_hl_ready, z_lo_ready = (
            sem("t_full"), sem("zT_ready"), sem("z_up_ready"), sem("z_hi_ready"), sem("z_hl_ready"), sem("z_lo_ready"))
        w_up_ready, w_ready, first_cut = sem("w_up_ready"), sem("w_ready"), sem("first_cut")
        g_full, silu_ready, hm_ready, y_full, y_ready = (
            sem("g_full"), sem("silu_ready"), sem("hm_ready"), sem("y_full"), sem("y_ready"))
        T0, Y0 = 4, 1
        block = cb.enter_context(nc.Block())
        zv = zbuf[0:SLOTS + BLK, :].rearrange("(b s p) c -> b p s c", s=BT, p=P)
        yv = ybuf.rearrange("(b s p) c -> b p s c", s=BT, p=P)

        @block.sync
        def _(sp):
            sp.dma_start(idb[:], consts[:, C_ID:C_ID + P]).then_inc(id_in, 16)
            sp.sem_inc(y_full, Y0)
            sp.sem_inc(w_ready, 1)
            it = 0

            def load_weights(j):
                x = j % 2
                sp.wait_ge(w_ready, it * 2 + (j + 1))
                sp.dma_start(w13_in[:], w13[bass.ds(it * 2 + j, 1)].rearrange("o p c f -> p (o c) f"),
                             ).then_inc(raw_in, 16)
                if j:
                    sp.wait_ge(y_full, it * (NBK * BT) + ((j - 1) * NBLK * BT + Y0))
                sp.dma_start(w2_s[:, x], w2e[bass.ds(it * 2 + j, 1)].rearrange("o p c f -> p (o c) f"),
                             ).then_inc(w_in[x], 16)
                sp.dma_start(nw_s[:, x], nw[bass.ds(it * 2 + j, 1)].rearrange("o p c -> p (o c)"),
                             ).then_inc(w_in[x], 16)

            def load_rows(b):
                sp.wait_ge(t_full, it * (2 * NBK) + (2 * (b - 1) + T0))
                rows = zv[bass.ds(it * NBK + b, 1)].rearrange("o p s c -> p (o s) c")
                sp.dma_start(z[:, b % 2, :, 0:D], rows).then_inc(z_in[b % 2], 16)
                sp.dma_start(z[:, b % 2, :, D:2 * P], rows[:, :, P:D]).then_inc(z_in[b % 2], 16)

            load_weights(0)
            load_rows(0)
            sp.wait_ge(first_cut, 3)
            with sp.Fori(0, NPAIR) as it:
                for b in range(NBK):
                    load_rows(b + 1)
                    if b % NBLK == 0:
                        load_weights(b // NBLK + 1)
            sp.wait_ge(z_in[0], 32 * (NPAIR * NBLK + 1))
            sp.wait_ge(w_in[0], 32 * (NPAIR + 1))
            sp.wait_ge(raw_in, 16 * (2 * NPAIR + 1))

        @block.gpsimd
        def _(pool):
            it, tt = 0, nc.gpsimd.tensor_tensor

            def cut_weights(j, n, b):
                x, c = j % 2, slice(0, 2 if j else 1)
                pool.wait_ge(z_lo_ready, it * (2 * NBK) + (2 * b + 3))
                if n == 0:
                    pool.wait_ge(raw_in, it * 32 + 16 * (j + 1))
                    if j:
                        pool.wait_ge(y_full, it * (NBK * BT) + ((j - 1) * NBLK * BT + Y0))
                    pool.sem_inc(passed, 1)
                    nc.gpsimd.tensor_scalar(w_up[:, c], w13_in[:, c], CUT, None, ALU.mult).then_inc(w_up_ready, 1)
                    return
                pool.wait_ge(w_up_ready, it * 6 + (3 * j + n))
                if n == 1:
                    tt(out=w_sum[:, c], in0=w13_in[:, c], in1=w_up[:, c], op=ALU.add).then_inc(w_up_ready, 1)
                elif n == 2:
                    tt(out=w_hi[:, x, c], in0=w_sum[:, c], in1=w_up[:, c], op=ALU.subtract).then_inc(w_up_ready, 1)
                else:
                    tt(out=w_lo[:, x, c], in0=w13_in[:, c], in1=w_hi[:, x, c], op=ALU.subtract).then_inc(w_ready, 1)

            def lo_rows(b):
                for c, r, dst in ((0, 0, z_lo), (1, P // 2, z_hl)):
                    pool.wait_ge(z_lo_ready, it * (2 * NBK) + (2 * b + c + 1))
                    pool.wait_ge(z_hi_ready, it * (2 * NBK) + (2 * b + c + 1))
                    tt(out=dst[r:P, b % 2, :], in0=zT[r:P, b % 2, c, :],
                       in1=z_hi[r:P, b % 2, c, :], op=ALU.subtract).then_inc(z_lo_ready, 1)

            for n in range(4):
                cut_weights(0, n, -1)
            pool.wait_ge(first_cut, 3)
            lo_rows(0)
            with pool.Fori(0, NPAIR) as it:
                for b in range(NBK):
                    lo_rows(b + 1)
                    if b % NBLK < 4:
                        cut_weights(b // NBLK + 1, b % NBLK, b + 1)

        @block.scalar
        def _(act):
            it = 0

            def store(b):
                act.wait_ge(y_ready, it * (NBK * BT) + (BT * (b + 1) + 1))
                act.dma_start(yv[bass.ds(it * NBK + b, 1)].rearrange("o p s c -> p (o s) c"), y[:, b % 2],
                              ).then_inc(y_out[b % 2], 16)

            def rows_out(b, n):
                x = b // NBLK % 2
                if n:
                    act.wait_ge(z_hi_ready, it * (2 * NBK) + (2 * b + 2))
                    nc.scalar.copy(z_hl[0:P // 2, b % 2, :], z_hi[0:P // 2, b % 2, 1, :]).then_inc(z_hl_ready, 1)
                    return
                if b % NBLK == 0:
                    act.wait_ge(w_in[x], it * 32 + 32 * (b // NBK + 1))
                for c in range(2):
                    act.wait_ge(t_full, it * (2 * NBK) + (2 * b + c + 1 + T0))
                    nc.scalar.mul(zT[:, b % 2, c, :], tr[c][:, :], nw_s[:, x, c:c + 1]).then_inc(zT_ready, 1)

            rows_out(0, 0)
            rows_out(0, 1)
            with act.Fori(0, NPAIR) as it:
                for b in range(NBK):
                    for m in range(MG):
                        k = b * MG + m
                        act.wait_ge(g_full, it * (NBK * MG) + (k + 1))
                        if k >= 2:
                            act.wait_ge(hm_ready, it * (NBK * MG) + k)
                        nc.scalar.activation(sg[:, k % 2, :], gu[2 * (k % 2)][:, :], ACT.Silu).then_inc(silu_ready, 1)
                        if m == 0:
                            rows_out(b + 1, 0)
                        if m == 2:
                            rows_out(b + 1, 1)
                    if b:
                        store(b - 1)
                store(NBK - 1)
            for b in range(2):
                act.wait_ge(y_out[b], 16 * NPAIR * NBLK + 16)

        @block.vector
        def _(dve):
            for b in range(2):
                dve.sem_inc(y_out[b], 16)
            it = 0

            def drain_rows(b):
                for s in range(BT):
                    k = b * BT + s
                    dve.wait_ge(y_full, it * (NBK * BT) + (k + 1 + Y0))
                    if s == 0:
                        dve.wait_ge(y_out[b % 2], it * (16 * NBLK) + 16 * (b // 2 + 1))
                    nc.vector.tensor_copy(y[:, b % 2, s, :], yp[k % 2][:, 0:D]).then_inc(y_ready, 1)

            def sum_rows(b):
                for c in range(2):
                    dve.wait_ge(zT_ready, it * (2 * NBK) + (2 * b + c + 2))
                    nc.vector.scalar_tensor_tensor(z_up[:, c, :], zT[:, b % 2, c, :], CUT, zT[:, b % 2, c, :],
                                                   ALU.mult, ALU.add).then_inc(z_up_ready, 1)

            def cut_rows(b):
                for c in range(2):
                    dve.wait_ge(z_up_ready, it * (2 * NBK) + (2 * b + c + 1))
                    nc.vector.scalar_tensor_tensor(z_hi[:, b % 2, c, :], zT[:, b % 2, c, :], -CUT, z_up[:, c, :],
                                                   ALU.mult, ALU.add).then_inc(z_hi_ready, 1)

            dve.wait_ge(raw_in, 16)
            nc.vector.scalar_tensor_tensor(w_sum[:, 1], w13_in[:, 1], CUT, w13_in[:, 1],
                                           ALU.mult, ALU.add).then_inc(first_cut, 1)
            dve.wait_ge(first_cut, 1)
            nc.vector.scalar_tensor_tensor(w_hi[:, 0, 1], w13_in[:, 1], -CUT, w_sum[:, 1],
                                           ALU.mult, ALU.add).then_inc(first_cut, 1)
            dve.wait_ge(first_cut, 2)
            nc.vector.tensor_tensor(out=w_lo[:, 0, 1], in0=w13_in[:, 1], in1=w_hi[:, 0, 1],
                                    op=ALU.subtract).then_inc(first_cut, 1)
            sum_rows(0)
            cut_rows(0)
            with dve.Fori(0, NPAIR) as it:
                for b in range(NBK):
                    for m in range(MG):
                        k = b * MG + m
                        dve.wait_ge(silu_ready, it * (NBK * MG) + (k + 1))
                        nc.vector.tensor_tensor(out=hm[:, b % 2, m, :], in0=gu[2 * (k % 2) + 1][:, :],
                                                in1=sg[:, k % 2, :], op=ALU.mult).then_inc(hm_ready, 1)
                        if m == 0:
                            sum_rows(b + 1)
                            if b:
                                drain_rows(b - 1)
                            cut_rows(b + 1)
                drain_rows(NBK - 1)

        @block.tensor
        def _(pe):
            pe.wait_ge(id_in, 16)
            for s in (zT_ready, y_ready, hm_ready, z_lo_ready):
                pe.sem_inc(s, 1)
            pe.sem_inc(t_full, T0)
            it = 0

            def transposes(b):
                pe.wait_ge(z_in[b % 2], it * (32 * NBLK) + 32 * (b // 2 + 1))
                for c in range(2):
                    pe.wait_ge(zT_ready, it * (2 * NBK) + max(2 * b + c, 1))
                    for s in range(BT):
                        ins = nc.tensor.transpose(tr[c][:, s * P:(s + 1) * P],
                                                  z[:, b % 2, s, c * P:(c + 1) * P], idb[:])
                    ins.then_inc(t_full, 1)

            def down(b):
                pe.wait_ge(hm_ready, it * (NBK * MG) + ((b + 1) * MG + 1))
                for s in range(BT):
                    k = b * BT + s
                    pe.wait_ge(y_ready, it * (NBK * BT) + max(k, 1))
                    for m in range(MG):
                        ins = nc.tensor.matmul(yp[k % 2][:, 0:D], hm[:, b % 2, m, s * P:(s + 1) * P],
                                               w2_s[:, b // NBLK, m, :], start=(m == 0), stop=(m == MG - 1))
                    ins.then_inc(y_full, 1)

            transposes(0)
            pe.wait_ge(first_cut, 3)
            with pe.Fori(0, NPAIR) as it:
                for b in range(NBK):
                    x = b // NBLK
                    if b % NBLK == 0:
                        pe.wait_ge(w_in[x], it * 32 + 32)
                        pe.wait_ge(w_ready, it * 2 + (x + 2))
                    pe.wait_ge(z_hl_ready, it * NBK + (b + 1))
                    pe.wait_ge(z_lo_ready, it * (2 * NBK) + (2 * b + 3))
                    for m in range(MG):
                        k = b * MG + m
                        pe.wait_ge(hm_ready, it * (NBK * MG) + max(k, 1))
                        for u in range(2):
                            f = slice(u * EH + m * P, u * EH + (m + 1) * P)
                            parts = ((w_lo[:, x, 0, f], z_hi[:, b % 2, 0, :]), (w_hi[:, x, 0, f], z_hi[:, b % 2, 0, :]),
                                     (w_hi[:, x, 0, f], z_lo[:, b % 2, :]), (w_hi[:, x, 1, f], z_hl[:, b % 2, :]),
                                     (w_lo[:, x, 1, f], z_hl[:, b % 2, :]))
                            for n, (w, rows) in enumerate(parts):
                                ins = nc.tensor.matmul(gu[2 * (k % 2) + u][:, :], w, rows,
                                                       start=(n == 0), stop=(n == PARTS - 1))
                        ins.then_inc(g_full, 1)
                        if m == 0:
                            transposes(b + 1)
                            if b:
                                down(b - 1)
                down(NBK - 1)


def phase_c(nc, hbase, ybuf, out, gidx, cw, NT):
    with ExitStack() as cc:
        def sa(name, shape, dt=F32):
            return cc.enter_context(nc.sbuf_tensor(name, shape, dt))

        def sem(name):
            return cc.enter_context(nc.semaphore(name))

        G, U = 2, 4
        R = G * U
        LEAD = R - U + 1
        passed = sem("passed_c")
        ix = sa("ix", [P, G, U, 2], I32)
        wt = sa("wt", [P, R, 3])
        hb = sa("hb", [P, R, 2, D])
        yg = sa("yg", [P, R, 2, D])
        o = sa("o", [P, R, 3, D])
        h_in = [sem(f"h_in{u}") for u in range(R)]
        y_in = [sem(f"y_in{u}") for u in range(R)]
        o_out = [sem(f"o_out{u}") for u in range(R)]
        ix_ready, w_ready, base_ready, one_ready, o_ready = (
            sem("ix_ready"), sem("w_ready"), sem("base_ready"), sem("one_ready"), sem("o_ready"))
        block = cc.enter_context(nc.Block())
        hv = hbase.rearrange("(t p) k c -> t p k c", p=P)
        ov = out.rearrange("(t p) c -> t p c", p=P)

        @block.sync
        def _(sp):
            with sp.Fori(0, NT // R) as it:
                for u in range(R):
                    if u % U == 0:
                        sp.wait_ge(o_ready, it * R + (u + U + LEAD - R))
                    sp.dma_start(hb[:, u], hv[bass.ds(it * R + u, 1)].rearrange("o p k c -> p (o k) c"),
                                 ).then_inc(h_in[u], 16)

        @block.gpsimd
        def _(pool):
            with pool.Fori(0, NT // R) as it:
                for g in range(G):
                    pool.wait_ge(o_ready, it * R + (g * U + U + LEAD - R))
                    nc.gpsimd.tensor_copy(ix[:, g], gidx[:, bass.ds(it * R + g * U, U), :]).then_inc(ix_ready, 1)
                    pool.wait_ge(ix_ready, it * G + (g + 1))
                    pool.sem_inc(passed, 1)
                    for u in range(U):
                        for k in range(2):
                            nc.gpsimd.indirect_dma_start(
                                out=yg[:, g * U + u, k, :], out_offset=None, in_=ybuf,
                                in_offset=bass.IndirectOffsetOnAxis(ap=ix[:, g, u, k:k + 1], axis=0),
                            ).then_inc(y_in[g * U + u], 16)

        @block.vector
        def _(dve):
            dve.sem_inc(o_ready, LEAD)
            for u in range(R):
                dve.sem_inc(o_out[u], 16)
            stt = nc.vector.scalar_tensor_tensor
            with dve.Fori(0, NT // R) as it:
                nc.vector.tensor_copy(wt[:, :, 0:2], cw[:, bass.ds(it * R, R), :]).then_inc(w_ready, 1)
                dve.wait_ge(w_ready, it * 2 + 1)
                nc.vector.tensor_tensor(out=wt[:, :, 2], in0=wt[:, :, 0], in1=wt[:, :, 1], op=ALU.add).then_inc(w_ready, 1)
                dve.wait_ge(w_ready, it * 2 + 2)
                for g in range(G):
                    group = range(g * U, g * U + U)
                    for u in group:
                        dve.wait_ge(h_in[u], it * 16 + 16)
                        stt(o[:, u, 0, :], hb[:, u, 1, :], wt[:, u, 2:3], hb[:, u, 0, :],
                            ALU.mult, ALU.add).then_inc(base_ready, 1)
                    dve.wait_ge(base_ready, it * R + (g * U + U))
                    for u in group:
                        dve.wait_ge(y_in[u], it * 32 + 32)
                        stt(o[:, u, 1, :], yg[:, u, 0, :], wt[:, u, 0:1], o[:, u, 0, :],
                            ALU.mult, ALU.add).then_inc(one_ready, 1)
                    dve.wait_ge(one_ready, it * R + (g * U + U))
                    for u in group:
                        dve.wait_ge(o_out[u], it * 16 + 16)
                        stt(o[:, u, 2, :], yg[:, u, 1, :], wt[:, u, 1:2], o[:, u, 1, :],
                            ALU.mult, ALU.add).then_inc(o_ready, 1)
                dve.wait_ge(o_ready, it * R + (R + LEAD))

        @block.scalar
        def _(act):
            with act.Fori(0, NT // R) as it:
                for u in range(R):
                    act.wait_ge(o_ready, it * R + (u + 1 + LEAD))
                    act.dma_start(ov[bass.ds(it * R + u, 1)].rearrange("o p c -> p (o c)"), o[:, u, 2, :],
                                  ).then_inc(o_out[u], 16)
            for u in range(R):
                act.wait_ge(o_out[u], 16 * (NT // R) + 16)


def lay_out(a):
    f = lambda n: np.asarray(a[n])
    g = lambda n: f("L0_attn_" + n)

    def with_bias(w, b):
        return np.ascontiguousarray(np.concatenate([w, b[None, :]], 0))

    qkv, qkv2 = (with_bias(g(n + "_w"), g(n + "_b")) for n in ("attn_qkv", "ssm_qkv"))
    two = lambda v: v.reshape(2, C).T

    def one_more(w):
        return np.concatenate([w, w[0:1]])

    def a_and_b(w):
        return np.stack([w[:, 0:P], np.concatenate([w[:, P:D], w[:, P:D]], 1)], 2)
    ins = {
        "ids": np.ascontiguousarray(f("x").reshape(NB * T, P).T),
        "table": f("L0_tok_embedding_lookup"),
        "consts": constants(),
        "cols": np.concatenate([two(g(n)) for n in ("ln1_g", "ln1_b", "lnm_g", "lnm_b")], 1),
        "rows3": np.broadcast_to(np.stack([g("ssm_ln_g"), g("ssm_ln_b"), g("mlp_b2")])[None], (P, 3, D)),
        "wqk": np.concatenate([qkv[:, 0:2 * D], qkv2[:, 0:2 * D]], 1),
        "wv": np.concatenate([qkv[:, 2 * D:], qkv2[:, 2 * D:]], 1),
        "wp": with_bias(g("attn_proj_w"), g("attn_proj_b")),
        "ws": with_bias(g("ssm_out_w"), g("ssm_out_b")),
        "wo": with_bias(g("out_w"), g("out_b")),
        "w1": with_bias(g("mlp_w1"), g("mlp_b1")),
        "w2": g("mlp_w2").reshape(FF // P, P, D).transpose(1, 0, 2),
        "gate": f("L0_ffn_gate_w").T.reshape(2, C, NE).transpose(1, 0, 2),
        "w13": one_more(a_and_b(f("L0_ffn_w13").transpose(0, 2, 1))),
        "w2e": one_more(f("L0_ffn_w2").transpose(0, 2, 1).reshape(NE, EH // P, P, D).transpose(0, 2, 1, 3)),
        "nw": one_more(a_and_b(f("L0_ffn_norm_w")[:, :, None])[..., 0]),
    }
    return {k: np.ascontiguousarray(v) for k, v in ins.items()}


def build(nc, ins, out, NBATCH=NB, NPAIR=NE // 2, NT=NB * T, phases="abc"):
    hbase = nc.dram_tensor("hbase", [NTOK, 2, D], F32).ap()
    zbuf = nc.dram_tensor("zbuf", [SLOTS + SPILL, D], F32).ap()
    ybuf = nc.dram_tensor("ybuf", [SLOTS, D], F32).ap()
    with nc.sbuf_tensor("gidx", [P, NB * T, 2], I32) as gidx, nc.sbuf_tensor("cw", [P, NB * T, 2], F32) as cw:
        phase_a(nc, ins["ids"], ins["table"], ins["consts"], ins["cols"], ins["rows3"], ins["wqk"], ins["wv"],
                ins["wp"], ins["ws"], ins["wo"], ins["w1"], ins["w2"], ins["gate"], hbase, zbuf, gidx, cw, NBATCH)
        if "b" in phases:
            phase_b(nc, ins["w13"], ins["w2e"], ins["nw"], ins["consts"], zbuf, ybuf, NPAIR)
        if "c" in phases:
            phase_c(nc, hbase, ybuf, out, gidx, cw, NT)


def kernel(**inputs):
    import concourse.bacc as bacc
    from concourse.bass_utils import run_bass_kernel_spmd

    arrays = lay_out(inputs)
    nc = bacc.Bacc("TRN2", target_bir_lowering=False, num_devices=1)
    ins = {k: nc.dram_tensor(k, v.shape, mybir.dt.from_np(v.dtype), kind="ExternalInput").ap()
           for k, v in arrays.items()}
    out = nc.dram_tensor("out", (NTOK, D), F32, kind="ExternalOutput").ap()
    build(nc, ins, out)
    r = run_bass_kernel_spmd(nc, [arrays], core_ids=[0])
    return r.results[0]["out"].reshape(NB, SEQ, D)
```
